# Optimizing a Trainium2 kernel written in Bass

```python
import numpy as np
import jax
import jax.numpy as jnp

def _softmax(x, axis=-1):
    return jax.nn.softmax(x, axis=axis)

def _gelu(x):
    return jax.nn.gelu(x, approximate=True)

def _silu(x):
    return jax.nn.silu(x)

def _sigmoid(x):
    return jax.nn.sigmoid(x)

def _layernorm(x, axis=-1, eps=1e-05):
    m = jnp.mean(x, axis=axis, keepdims=True)
    v = jnp.var(x, axis=axis, keepdims=True)
    return (x - m) / jnp.sqrt(v + eps)

def _scatter_add(tgt, idx, src, axis=0):
    return tgt.at[idx].add(src)

def _segment_sum(src, seg, n):
    return jax.ops.segment_sum(src, seg, n)
kernel_name = 'mk_decoder_preln_d4_seqx_r8_aa96a4'

def setup_inputs(seed: int=0):
    np.random.seed(seed)
    _w = jnp.asarray

    def _rec_inputs():
        import jax
        import jax.numpy as jnp
        _rk = jax.random.key(seed)
        x = -0.000125 + 0.9999 * jax.random.normal(jax.random.fold_in(_rk, 1), (32, 64, 128), jnp.float32)
        _lenS = 64 - jax.random.randint(jax.random.fold_in(_rk, 7), (32,), 0, max(1, 64 // 4) + 1, jnp.int32)
        _lenS2 = 64 - jax.random.randint(jax.random.fold_in(_rk, 8), (32,), 0, max(1, 64 // 4) + 1, jnp.int32)
        _ctx_1024P = jax.random.normal(jax.random.fold_in(_rk, 11), (32, 16, 128), jnp.float32)
        _ctx_1024c = jax.random.dirichlet(jax.random.fold_in(_rk, 511), 0.3 * jnp.ones((16,), jnp.float32), (32, 64))
        _ctx_1024t = jnp.einsum('bsk,bkd->bsd', _ctx_1024c, _ctx_1024P)
        _ctx_1024t = _ctx_1024t * jax.lax.rsqrt(jnp.mean(jnp.square(_ctx_1024t)) + 1e-12) * 0.953939
        ctx_1024 = -1.52775e-05 + 0.999936 * (_ctx_1024t + 0.3 * jax.random.normal(jax.random.fold_in(_rk, 611), (32, 64, 128), jnp.float32))
        return (x, ctx_1024)
    x, ctx_1024 = _rec_inputs()

    def _L0_attn_setup():
        import jax, jax.numpy as jnp
        import numpy as np
        import math
        B, T, D = (4, 256, 128)
        NHEAD = 16
        HEAD_DIM = D // NHEAD
        MAX_REL = 16

        def _relative_bias(rel_bias, seq_len):
            r = jnp.arange(seq_len)
            dist = jnp.clip(r[None, :] - r[:, None], -MAX_REL + 1, MAX_REL - 1) + MAX_REL - 1
            return jnp.transpose(rel_bias[dist], (2, 0, 1))
        key = jax.random.key(seed)
        ks = jax.random.split(key, 10)
        s = 1.0 / math.sqrt(D)
        inp = {'x': jax.random.normal(ks[0], (B, T, D), dtype=jnp.float32), 'Wq': jax.random.normal(ks[1], (D, D), dtype=jnp.float32) * s, 'bq': jnp.zeros((D,), dtype=jnp.float32), 'Wk': jax.random.normal(ks[2], (D, D), dtype=jnp.float32) * s, 'bk': jnp.zeros((D,), dtype=jnp.float32), 'Wv': jax.random.normal(ks[3], (D, D), dtype=jnp.float32) * s, 'bv': jnp.zeros((D,), dtype=jnp.float32), 'rel_bias': jax.random.normal(ks[4], (2 * MAX_REL - 1, NHEAD), dtype=jnp.float32) * 0.02, 'Wo': jax.random.normal(ks[5], (D, D), dtype=jnp.float32) * s, 'bo': jnp.zeros((D,), dtype=jnp.float32)}
        return inp
    _L0_attn_all = _L0_attn_setup()
    _L0_attn_in = {k: v for k, v in _L0_attn_all.items() if k in ('Wq', 'bq', 'Wk', 'bk', 'Wv', 'bv', 'rel_bias', 'Wo', 'bo')}
    del _L0_attn_all

    def _L0_xattn_setup():
        import jax, jax.numpy as jnp
        import numpy as np
        N_HEADS = 4
        IN_FEATURES = 128

        def _channel_attention(qm, km, vm, scale):
            b, n, c = qm.shape
            d = c // N_HEADS
            qh = qm.reshape(b, n, N_HEADS, d).transpose(0, 2, 3, 1)
            kh = km.reshape(b, n, N_HEADS, d).transpose(0, 2, 3, 1)
            vh = vm.reshape(b, n, N_HEADS, d).transpose(0, 2, 3, 1)
            scores = jnp.einsum('bhdn,bhen->bhde', qh, kh) * scale
            attn = jax.nn.softmax(scores, axis=-1)
            out = jnp.einsum('bhde,bhen->bhdn', attn, vh)
            return out.transpose(0, 3, 1, 2).reshape(b, n, c)
        key = jax.random.key(seed)
        ks = jax.random.split(key, 20)
        B, HW, C = (2, 2048, 128)
        inp = {'q': jax.random.normal(ks[0], (B, HW, C), dtype=jnp.float32), 'k': jax.random.normal(ks[1], (B, HW, C), dtype=jnp.float32), 'v': jax.random.normal(ks[2], (B, HW, C), dtype=jnp.float32)}
        names = ['wqg', 'bqg', 'wkg', 'bkg', 'wvg', 'bvg', 'wql', 'bql', 'wkl', 'bkl', 'wvl', 'bvl', 'wp', 'bp']
        for i, n in enumerate(names):
            inp[n] = jax.random.normal(ks[3 + i], (C,), dtype=jnp.float32)
        return inp
    _L0_xattn_all = _L0_xattn_setup()
    _L0_xattn_in = {k: v for k, v in _L0_xattn_all.items() if k in ('wqg', 'bqg', 'wkg', 'bkg', 'wvg', 'bvg', 'wql', 'bql', 'wkl', 'bkl', 'wvl', 'bvl', 'wp', 'bp')}
    del _L0_xattn_all

    def _L0_ffn_setup():
        import jax, jax.numpy as jnp
        import numpy as np
        DIM, E, K, H = (128, 8, 2, 512)
        key = jax.random.key(seed)
        ks = jax.random.split(key, 5)
        s_in = 1.0 / np.sqrt(DIM)
        s_h = 1.0 / np.sqrt(H)
        return {'x': jax.random.normal(ks[0], (4, 256, DIM), dtype=jnp.float32), 'Wr': jax.random.normal(ks[1], (DIM, E), dtype=jnp.float32) * s_in, 'W1': jax.random.normal(ks[2], (E, DIM, H), dtype=jnp.float32) * s_in, 'b1': jnp.zeros((E, H), dtype=jnp.float32), 'W2': jax.random.normal(ks[3], (E, H, DIM), dtype=jnp.float32) * s_h, 'b2': jnp.zeros((E, DIM), dtype=jnp.float32)}
    _L0_ffn_all = _L0_ffn_setup()
    _L0_ffn_in = {k: v for k, v in _L0_ffn_all.items() if k in ('Wr', 'W1', 'b1', 'W2', 'b2')}
    del _L0_ffn_all

    def _L1_attn_setup():
        import jax, jax.numpy as jnp
        import numpy as np
        HEADS = 16
        HEAD_DIM = 64
        DIM = 128
        INNER = HEADS * HEAD_DIM

        def rotate_half(t):
            x1, x2 = jnp.split(t, 2, axis=-1)
            return jnp.concatenate((-x2, x1), axis=-1)

        def rope_table(n, head_dim, dtype):
            inv_freq = 1.0 / 10000.0 ** (jnp.arange(0, head_dim, 2, dtype=jnp.float32) / head_dim)
            freqs = jnp.arange(n, dtype=jnp.float32)[:, None] * inv_freq[None, :]
            return jnp.concatenate((freqs, freqs), axis=-1).astype(dtype)
        key = jax.random.key(seed)
        k1, k2, k3, k4 = jax.random.split(key, 4)
        x = jax.random.normal(k1, (1, 512, DIM), dtype=jnp.float32)
        s = 0.02
        W_qkv = jax.random.normal(k2, (DIM, 3 * INNER), dtype=jnp.float32) * s
        W_o1 = jax.random.normal(k3, (INNER, DIM), dtype=jnp.float32) * s
        W_o2 = jax.random.normal(k4, (DIM, DIM), dtype=jnp.float32) * s
        gamma = jnp.ones((DIM,), dtype=jnp.float32)
        return {'x': x, 'W_qkv': W_qkv, 'W_o1': W_o1, 'W_o2': W_o2, 'gamma': gamma}
    _L1_attn_all = _L1_attn_setup()
    _L1_attn_in = {k: v for k, v in _L1_attn_all.items() if k in ('W_qkv', 'W_o1', 'W_o2', 'gamma')}
    del _L1_attn_all

    def _L1_xattn_setup():
        import jax, jax.numpy as jnp
        import numpy as np
        D_MODEL = 128
        N_HEADS = 16
        D_HEAD = D_MODEL // N_HEADS
        key = jax.random.key(seed)
        ks = jax.random.split(key, 6)
        B, S = (4, 256)
        scale = 1.0 / np.sqrt(D_MODEL)
        return {'query_input': jax.random.normal(ks[0], (B, S, D_MODEL), dtype=jnp.float32), 'kv_input': jax.random.normal(ks[1], (B, S, D_MODEL), dtype=jnp.float32), 'W_q': jax.random.normal(ks[2], (D_MODEL, D_MODEL), dtype=jnp.float32) * scale, 'W_k': jax.random.normal(ks[3], (D_MODEL, D_MODEL), dtype=jnp.float32) * scale, 'W_v': jax.random.normal(ks[4], (D_MODEL, D_MODEL), dtype=jnp.float32) * scale, 'W_o': jax.random.normal(ks[5], (D_MODEL, D_MODEL), dtype=jnp.float32) * scale}
    _L1_xattn_all = _L1_xattn_setup()
    _L1_xattn_in = {k: v for k, v in _L1_xattn_all.items() if k in ('W_q', 'W_k', 'W_v', 'W_o')}
    del _L1_xattn_all

    def _L1_ffn_setup():
        import jax, jax.numpy as jnp
        import numpy as np
        B, L, H, E, I = (4, 256, 128, 8, 512)
        S = B * L
        CAP_FACTOR_EVAL = 2.0
        MIN_CAP = 4
        _cap = int(np.floor(CAP_FACTOR_EVAL * S / E))
        _cap += _cap % 2
        CAPACITY = max(_cap, MIN_CAP)

        def _layer_norm(x, g, b, eps=1e-05):
            mu = x.mean(-1, keepdims=True)
            var = ((x - mu) ** 2).mean(-1, keepdims=True)
            return (x - mu) * jax.lax.rsqrt(var + eps) * g + b
        key = jax.random.key(seed)
        ks = jax.random.split(key, 8)
        gate_std = float(np.sqrt(0.1 / H))
        return {'inputs': jax.random.normal(ks[0], (B, L, H), jnp.float32), 'gate_weight': jax.random.normal(ks[1], (E, H), jnp.float32) * gate_std, 'ln_gamma': jnp.ones((H,), jnp.float32), 'ln_beta': jnp.zeros((H,), jnp.float32), 'wi': jax.random.normal(ks[2], (E, H, I), jnp.float32) * float(1.0 / np.sqrt(H)), 'wo': jax.random.normal(ks[3], (E, I, H), jnp.float32) * float(1.0 / np.sqrt(I)), 'conf_w1': jax.random.normal(ks[4], (H // 2, H), jnp.float32) * float(np.sqrt(2.0 / (H + H // 2))), 'conf_b1': -jnp.ones((H // 2,), jnp.float32), 'conf_w2': jax.random.normal(ks[5], (1, H // 2), jnp.float32) * float(np.sqrt(2.0 / (1 + H // 2))), 'conf_b2': -jnp.ones((1,), jnp.float32), 'comp_w': jax.random.normal(ks[6], (1, H), jnp.float32) * float(1.0 / np.sqrt(H)), 'comp_b': jnp.zeros((1,), jnp.float32)}
    _L1_ffn_all = _L1_ffn_setup()
    _L1_ffn_in = {k: v for k, v in _L1_ffn_all.items() if k in ('gate_weight', 'ln_gamma', 'ln_beta', 'wi', 'wo', 'conf_w1', 'conf_b1', 'conf_w2', 'conf_b2', 'comp_w', 'comp_b')}
    del _L1_ffn_all

    def _L2_attn_setup():
        import jax, jax.numpy as jnp
        import numpy as np
        B, T, D = (2, 256, 128)
        H = 16
        HD = D // H
        DL = 64
        NR = 64
        EPS = 1.1920929e-07

        def _rms_norm(x, w):
            ms = jnp.mean(jnp.square(x), axis=-1, keepdims=True)
            return x * jax.lax.rsqrt(ms + EPS) * w
        key = jax.random.key(seed)
        ks = jax.random.split(key, 10)
        s = 0.02
        return {'x': jax.random.normal(ks[0], (B, T, D), dtype=jnp.float32), 'W_DQ': jax.random.normal(ks[1], (DL, HD), dtype=jnp.float32) * s, 'W_UQ': jax.random.normal(ks[2], (HD, DL), dtype=jnp.float32) * s, 'W_DKV': jax.random.normal(ks[3], (2 * DL, HD), dtype=jnp.float32) * s, 'W_UKV': jax.random.normal(ks[4], (2 * HD, 2 * DL), dtype=jnp.float32) * s, 'W_QR': jax.random.normal(ks[5], (NR, HD), dtype=jnp.float32) * s, 'W_KR': jax.random.normal(ks[6], (NR, HD), dtype=jnp.float32) * s, 'W_O': jax.random.normal(ks[7], (HD, HD), dtype=jnp.float32) * s, 'q_norm_w': jnp.ones((HD,), dtype=jnp.float32), 'k_norm_w': jnp.ones((HD,), dtype=jnp.float32)}
    _L2_attn_all = _L2_attn_setup()
    _L2_attn_in = {k: v for k, v in _L2_attn_all.items() if k in ('W_DQ', 'W_UQ', 'W_DKV', 'W_UKV', 'W_QR', 'W_KR', 'W_O', 'q_norm_w', 'k_norm_w')}
    del _L2_attn_all

    def _L2_xattn_setup():
        import jax, jax.numpy as jnp
        import numpy as np
        B, S, H, NH = (2, 256, 128, 4)
        DH = H // NH
        EPS_BACKEND = 1e-06
        EPS_LN = 1e-06

        def _mlstm_parallel_stabilized(q, k, v, igate_preact, fgate_preact):
            b, nh, s, dh = q.shape
            log_fg = jax.nn.log_sigmoid(fgate_preact)
            cs = jnp.concatenate([jnp.zeros((b, nh, 1), q.dtype), jnp.cumsum(log_fg[..., 0], axis=2)], axis=2)
            fg_matrix = cs[:, :, :, None] - cs[:, :, None, :]
            fg_matrix = fg_matrix[:, :, 1:, 1:]
            causal = jnp.tril(jnp.ones((s, s), dtype=bool))
            log_fg_matrix = jnp.where(causal, fg_matrix, -jnp.inf)
            log_D = log_fg_matrix + jnp.swapaxes(igate_preact, -2, -1)
            max_log_D = jnp.max(log_D, axis=-1, keepdims=True)
            D = jnp.exp(log_D - max_log_D)
            qk = jnp.einsum('bhsd,bhtd->bhst', q, k) / jnp.sqrt(jnp.asarray(dh, q.dtype))
            C = qk * D
            normalizer = jnp.maximum(jnp.abs(jnp.sum(C, axis=-1, keepdims=True)), jnp.exp(-max_log_D))
            C_norm = C / (normalizer + EPS_BACKEND)
            return jnp.einsum('bhst,bhtd->bhsd', C_norm, v)

        def _multihead_layernorm(x, scale):
            mean = jnp.mean(x, axis=-1, keepdims=True)
            var = jnp.var(x, axis=-1, keepdims=True)
            xn = (x - mean) * jax.lax.rsqrt(var + EPS_LN)
            return xn * scale.reshape(NH, 1, DH)
        key = jax.random.key(seed)
        kq, kk, kv, kib = jax.random.split(key, 4)
        q = jax.random.normal(kq, (B, S, H), dtype=jnp.float32)
        k = jax.random.normal(kk, (B, S, H), dtype=jnp.float32)
        v = jax.random.normal(kv, (B, S, H), dtype=jnp.float32)
        igate_kernel = jnp.zeros((3 * H, NH), dtype=jnp.float32)
        igate_bias = 0.1 * jax.random.normal(kib, (NH,), dtype=jnp.float32)
        fgate_kernel = jnp.zeros((3 * H, NH), dtype=jnp.float32)
        fgate_bias = jnp.linspace(3.0, 6.0, NH, dtype=jnp.float32)
        outnorm_scale = jnp.ones((H,), dtype=jnp.float32)
        return {'q': q, 'k': k, 'v': v, 'igate_kernel': igate_kernel, 'igate_bias': igate_bias, 'fgate_kernel': fgate_kernel, 'fgate_bias': fgate_bias, 'outnorm_scale': outnorm_scale}
    _L2_xattn_all = _L2_xattn_setup()
    _L2_xattn_in = {k: v for k, v in _L2_xattn_all.items() if k in ('igate_kernel', 'igate_bias', 'fgate_kernel', 'fgate_bias', 'outnorm_scale')}
    del _L2_xattn_all

    def _L2_ffn_setup():
        import jax, jax.numpy as jnp
        import numpy as np
        EPS = 1e-06
        TOP_K = 2
        key = jax.random.key(seed)
        k0, k1, k2, k3, k4 = jax.random.split(key, 5)
        B, S, H, I, E = (1, 256, 128, 448, 8)
        return {'hidden_states': jax.random.normal(k0, (B, S, H), jnp.float32), 'rms_weight': jnp.ones((H,), jnp.float32), 'gate_w': jax.random.normal(k1, (E, H), jnp.float32) * H ** (-0.5), 'w1': jax.random.normal(k2, (E, I, H), jnp.float32) * H ** (-0.5), 'w2': jax.random.normal(k3, (E, H, I), jnp.float32) * I ** (-0.5), 'w3': jax.random.normal(k4, (E, I, H), jnp.float32) * H ** (-0.5)}
    _L2_ffn_all = _L2_ffn_setup()
    _L2_ffn_in = {k: v for k, v in _L2_ffn_all.items() if k in ('rms_weight', 'gate_w', 'w1', 'w2', 'w3')}
    del _L2_ffn_all

    def _L3_attn_setup():
        import jax, jax.numpy as jnp
        import numpy as np
        NUM_HEADS = 16
        CLIP = 16
        key = jax.random.key(seed)
        ks = jax.random.split(key, 7)
        d = 128
        return {'x': jax.random.normal(ks[0], (2, 256, d), dtype=jnp.float32), 'Wq': jax.random.normal(ks[1], (d, d), dtype=jnp.float32) / np.sqrt(d), 'Wk': jax.random.normal(ks[2], (d, d), dtype=jnp.float32) / np.sqrt(d), 'Wv': jax.random.normal(ks[3], (d, d), dtype=jnp.float32) / np.sqrt(d), 'Wo': jax.random.normal(ks[4], (d, d), dtype=jnp.float32) / np.sqrt(d), 'bo': jax.random.normal(ks[5], (d,), dtype=jnp.float32) * 0.01, 'rel_emb': jax.random.normal(ks[6], (CLIP + 1,), dtype=jnp.float32)}
    _L3_attn_all = _L3_attn_setup()
    _L3_attn_in = {k: v for k, v in _L3_attn_all.items() if k in ('Wq', 'Wk', 'Wv', 'Wo', 'bo', 'rel_emb')}
    del _L3_attn_all

    def _L3_xattn_setup():
        import jax, jax.numpy as jnp
        import numpy as np
        D_MODEL = 128
        N_HEADS = 16
        HEAD_DIM = D_MODEL // N_HEADS

        def sparsemax(x):
            x = x - jnp.max(x, axis=-1, keepdims=True)
            zs = -jnp.sort(-x, axis=-1)
            L = x.shape[-1]
            rho = jnp.arange(1, L + 1, dtype=x.dtype)
            cssv = jnp.cumsum(zs, axis=-1) - 1.0
            support = zs > cssv / rho
            k = jnp.maximum(jnp.sum(support, axis=-1, keepdims=True), 1)
            tau = jnp.take_along_axis(cssv, k - 1, axis=-1) / k.astype(x.dtype)
            return jnp.clip(x - tau, 0.0)

        def _split_heads(x):
            B, L, _ = x.shape
            return x.reshape(B, L, N_HEADS, HEAD_DIM).transpose(0, 2, 1, 3)
        key = jax.random.key(seed)
        ks = jax.random.split(key, 11)
        B, L = (2, 256)
        s = 0.02
        inp = {'q': jax.random.normal(ks[0], (B, L, D_MODEL), jnp.float32), 'k': jax.random.normal(ks[1], (B, L, D_MODEL), jnp.float32), 'v': jax.random.normal(ks[2], (B, L, D_MODEL), jnp.float32), 'Wq': jax.random.normal(ks[3], (D_MODEL, D_MODEL), jnp.float32) * s, 'bq': jnp.zeros((D_MODEL,), jnp.float32), 'Wk': jax.random.normal(ks[4], (D_MODEL, D_MODEL), jnp.float32) * s, 'bk': jnp.zeros((D_MODEL,), jnp.float32), 'Wv': jax.random.normal(ks[5], (D_MODEL, D_MODEL), jnp.float32) * s, 'bv': jnp.zeros((D_MODEL,), jnp.float32), 'Wo': jax.random.normal(ks[6], (D_MODEL, D_MODEL), jnp.float32) * s, 'bo': jnp.zeros((D_MODEL,), jnp.float32)}
        return inp
    _L3_xattn_all = _L3_xattn_setup()
    _L3_xattn_in = {k: v for k, v in _L3_xattn_all.items() if k in ('Wq', 'bq', 'Wk', 'bk', 'Wv', 'bv', 'Wo', 'bo')}
    del _L3_xattn_all

    def _L3_ffn_setup():
        import jax, jax.numpy as jnp
        import numpy as np
        D, H, NE, K, ED = (128, 16, 8, 2, 512)
        B, S = (4, 128)
        EPS = 1e-06

        def rmsnorm(x, w):
            ms = jnp.mean(jnp.square(x.astype(jnp.float32)), axis=-1, keepdims=True)
            return x * jax.lax.rsqrt(ms + EPS).astype(x.dtype) * w

        def attn(x, qkv_w, o_w):
            b, s, d = x.shape
            hd = d // H
            qkv = (x @ qkv_w.T).reshape(b, s, 3, H, hd).transpose(2, 0, 3, 1, 4)
            q, k, v = (qkv[0], qkv[1], qkv[2])
            a = jnp.einsum('bhqd,bhkd->bhqk', q, k) * hd ** (-0.5)
            mask = jnp.triu(jnp.ones((s, s), dtype=bool), 1)
            a = jax.nn.softmax(jnp.where(mask, -1000000000.0, a), axis=-1)
            out = jnp.einsum('bhqk,bhkd->bhqd', a, v).transpose(0, 2, 1, 3).reshape(b, s, d)
            return out @ o_w.T

        def moe(x, gate_w, up_w, down_w):
            b, s, d = x.shape
            xf = x.reshape(b * s, d)
            gp = jax.nn.softmax(xf @ gate_w.T, axis=-1)
            ew, _ = jax.lax.top_k(gp, K)
            ew = ew / (jnp.sum(ew, axis=-1, keepdims=True) + 1e-09)
            ef = jax.nn.silu(xf @ up_w.T) @ down_w.T
            out = ef * jnp.sum(ew, axis=-1, keepdims=True)
            return out.reshape(b, s, d)
        key = jax.random.key(seed)
        ks = jax.random.split(key, 8)
        sd = 1.0 / np.sqrt(D)
        se = 1.0 / np.sqrt(ED)
        return {'x': jax.random.normal(ks[0], (B, S, D), dtype=jnp.float32), 'n1_w': jnp.ones((D,), jnp.float32), 'qkv_w': jax.random.normal(ks[1], (3 * D, D), jnp.float32) * sd, 'o_w': jax.random.normal(ks[2], (D, D), jnp.float32) * sd, 'n2_w': jnp.ones((D,), jnp.float32), 'gate_w': jax.random.normal(ks[3], (NE, D), jnp.float32) * sd, 'up_w': jax.random.normal(ks[4], (ED, D), jnp.float32) * sd, 'down_w': jax.random.normal(ks[5], (D, ED), jnp.float32) * se}
    _L3_ffn_all = _L3_ffn_setup()
    _L3_ffn_in = {k: v for k, v in _L3_ffn_all.items() if k in ('n1_w', 'qkv_w', 'o_w', 'n2_w', 'gate_w', 'up_w', 'down_w')}
    del _L3_ffn_all
    return {'x': x, 'ctx_1024': ctx_1024, 'L0_attn_Wq': _L0_attn_in['Wq'], 'L0_attn_bq': _L0_attn_in['bq'], 'L0_attn_Wk': _L0_attn_in['Wk'], 'L0_attn_bk': _L0_attn_in['bk'], 'L0_attn_Wv': _L0_attn_in['Wv'], 'L0_attn_bv': _L0_attn_in['bv'], 'L0_attn_rel_bias': _L0_attn_in['rel_bias'], 'L0_attn_Wo': _L0_attn_in['Wo'], 'L0_attn_bo': _L0_attn_in['bo'], 'L0_xattn_wqg': _L0_xattn_in['wqg'], 'L0_xattn_bqg': _L0_xattn_in['bqg'], 'L0_xattn_wkg': _L0_xattn_in['wkg'], 'L0_xattn_bkg': _L0_xattn_in['bkg'], 'L0_xattn_wvg': _L0_xattn_in['wvg'], 'L0_xattn_bvg': _L0_xattn_in['bvg'], 'L0_xattn_wql': _L0_xattn_in['wql'], 'L0_xattn_bql': _L0_xattn_in['bql'], 'L0_xattn_wkl': _L0_xattn_in['wkl'], 'L0_xattn_bkl': _L0_xattn_in['bkl'], 'L0_xattn_wvl': _L0_xattn_in['wvl'], 'L0_xattn_bvl': _L0_xattn_in['bvl'], 'L0_xattn_wp': _L0_xattn_in['wp'], 'L0_xattn_bp': _L0_xattn_in['bp'], 'L0_ffn_Wr': _L0_ffn_in['Wr'], 'L0_ffn_W1': _L0_ffn_in['W1'], 'L0_ffn_b1': _L0_ffn_in['b1'], 'L0_ffn_W2': _L0_ffn_in['W2'], 'L0_ffn_b2': _L0_ffn_in['b2'], 'L1_attn_W_qkv': _L1_attn_in['W_qkv'], 'L1_attn_W_o1': _L1_attn_in['W_o1'], 'L1_attn_W_o2': _L1_attn_in['W_o2'], 'L1_attn_gamma': _L1_attn_in['gamma'], 'L1_xattn_W_q': _L1_xattn_in['W_q'], 'L1_xattn_W_k': _L1_xattn_in['W_k'], 'L1_xattn_W_v': _L1_xattn_in['W_v'], 'L1_xattn_W_o': _L1_xattn_in['W_o'], 'L1_ffn_gate_weight': _L1_ffn_in['gate_weight'], 'L1_ffn_ln_gamma': _L1_ffn_in['ln_gamma'], 'L1_ffn_ln_beta': _L1_ffn_in['ln_beta'], 'L1_ffn_wi': _L1_ffn_in['wi'], 'L1_ffn_wo': _L1_ffn_in['wo'], 'L1_ffn_conf_w1': _L1_ffn_in['conf_w1'], 'L1_ffn_conf_b1': _L1_ffn_in['conf_b1'], 'L1_ffn_conf_w2': _L1_ffn_in['conf_w2'], 'L1_ffn_conf_b2': _L1_ffn_in['conf_b2'], 'L1_ffn_comp_w': _L1_ffn_in['comp_w'], 'L1_ffn_comp_b': _L1_ffn_in['comp_b'], 'L2_attn_W_DQ': _L2_attn_in['W_DQ'], 'L2_attn_W_UQ': _L2_attn_in['W_UQ'], 'L2_attn_W_DKV': _L2_attn_in['W_DKV'], 'L2_attn_W_UKV': _L2_attn_in['W_UKV'], 'L2_attn_W_QR': _L2_attn_in['W_QR'], 'L2_attn_W_KR': _L2_attn_in['W_KR'], 'L2_attn_W_O': _L2_attn_in['W_O'], 'L2_attn_q_norm_w': _L2_attn_in['q_norm_w'], 'L2_attn_k_norm_w': _L2_attn_in['k_norm_w'], 'L2_xattn_igate_kernel': _L2_xattn_in['igate_kernel'], 'L2_xattn_igate_bias': _L2_xattn_in['igate_bias'], 'L2_xattn_fgate_kernel': _L2_xattn_in['fgate_kernel'], 'L2_xattn_fgate_bias': _L2_xattn_in['fgate_bias'], 'L2_xattn_outnorm_scale': _L2_xattn_in['outnorm_scale'], 'L2_ffn_rms_weight': _L2_ffn_in['rms_weight'], 'L2_ffn_gate_w': _L2_ffn_in['gate_w'], 'L2_ffn_w1': _L2_ffn_in['w1'], 'L2_ffn_w2': _L2_ffn_in['w2'], 'L2_ffn_w3': _L2_ffn_in['w3'], 'L3_attn_Wq': _L3_attn_in['Wq'], 'L3_attn_Wk': _L3_attn_in['Wk'], 'L3_attn_Wv': _L3_attn_in['Wv'], 'L3_attn_Wo': _L3_attn_in['Wo'], 'L3_attn_bo': _L3_attn_in['bo'], 'L3_attn_rel_emb': _L3_attn_in['rel_emb'], 'L3_xattn_Wq': _L3_xattn_in['Wq'], 'L3_xattn_bq': _L3_xattn_in['bq'], 'L3_xattn_Wk': _L3_xattn_in['Wk'], 'L3_xattn_bk': _L3_xattn_in['bk'], 'L3_xattn_Wv': _L3_xattn_in['Wv'], 'L3_xattn_bv': _L3_xattn_in['bv'], 'L3_xattn_Wo': _L3_xattn_in['Wo'], 'L3_xattn_bo': _L3_xattn_in['bo'], 'L3_ffn_n1_w': _L3_ffn_in['n1_w'], 'L3_ffn_qkv_w': _L3_ffn_in['qkv_w'], 'L3_ffn_o_w': _L3_ffn_in['o_w'], 'L3_ffn_n2_w': _L3_ffn_in['n2_w'], 'L3_ffn_gate_w': _L3_ffn_in['gate_w'], 'L3_ffn_up_w': _L3_ffn_in['up_w'], 'L3_ffn_down_w': _L3_ffn_in['down_w']}

def reference(x, ctx_1024, L0_attn_Wq, L0_attn_bq, L0_attn_Wk, L0_attn_bk, L0_attn_Wv, L0_attn_bv, L0_attn_rel_bias, L0_attn_Wo, L0_attn_bo, L0_xattn_wqg, L0_xattn_bqg, L0_xattn_wkg, L0_xattn_bkg, L0_xattn_wvg, L0_xattn_bvg, L0_xattn_wql, L0_xattn_bql, L0_xattn_wkl, L0_xattn_bkl, L0_xattn_wvl, L0_xattn_bvl, L0_xattn_wp, L0_xattn_bp, L0_ffn_Wr, L0_ffn_W1, L0_ffn_b1, L0_ffn_W2, L0_ffn_b2, L1_attn_W_qkv, L1_attn_W_o1, L1_attn_W_o2, L1_attn_gamma, L1_xattn_W_q, L1_xattn_W_k, L1_xattn_W_v, L1_xattn_W_o, L1_ffn_gate_weight, L1_ffn_ln_gamma, L1_ffn_ln_beta, L1_ffn_wi, L1_ffn_wo, L1_ffn_conf_w1, L1_ffn_conf_b1, L1_ffn_conf_w2, L1_ffn_conf_b2, L1_ffn_comp_w, L1_ffn_comp_b, L2_attn_W_DQ, L2_attn_W_UQ, L2_attn_W_DKV, L2_attn_W_UKV, L2_attn_W_QR, L2_attn_W_KR, L2_attn_W_O, L2_attn_q_norm_w, L2_attn_k_norm_w, L2_xattn_igate_kernel, L2_xattn_igate_bias, L2_xattn_fgate_kernel, L2_xattn_fgate_bias, L2_xattn_outnorm_scale, L2_ffn_rms_weight, L2_ffn_gate_w, L2_ffn_w1, L2_ffn_w2, L2_ffn_w3, L3_attn_Wq, L3_attn_Wk, L3_attn_Wv, L3_attn_Wo, L3_attn_bo, L3_attn_rel_emb, L3_xattn_Wq, L3_xattn_bq, L3_xattn_Wk, L3_xattn_bk, L3_xattn_Wv, L3_xattn_bv, L3_xattn_Wo, L3_xattn_bo, L3_ffn_n1_w, L3_ffn_qkv_w, L3_ffn_o_w, L3_ffn_n2_w, L3_ffn_gate_w, L3_ffn_up_w, L3_ffn_down_w):
    import jax
    import jax.numpy as jnp

    def _L0_attn_ref(x, Wq, bq, Wk, bk, Wv, bv, rel_bias, Wo, bo):
        import jax, jax.numpy as jnp
        import numpy as np
        import math
        B, T, D = (4, 256, 128)
        NHEAD = 16
        HEAD_DIM = D // NHEAD
        MAX_REL = 16

        def _relative_bias(rel_bias, seq_len):
            r = jnp.arange(seq_len)
            dist = jnp.clip(r[None, :] - r[:, None], -MAX_REL + 1, MAX_REL - 1) + MAX_REL - 1
            return jnp.transpose(rel_bias[dist], (2, 0, 1))
        Bdim, Tdim, Ddim = x.shape
        Q = x @ Wq.T + bq
        K = x @ Wk.T + bk
        V = x @ Wv.T + bv
        Q = Q.reshape(Bdim, Tdim, NHEAD, HEAD_DIM).transpose(0, 2, 1, 3)
        K = K.reshape(Bdim, Tdim, NHEAD, HEAD_DIM).transpose(0, 2, 1, 3)
        V = V.reshape(Bdim, Tdim, NHEAD, HEAD_DIM).transpose(0, 2, 1, 3)
        scores = jnp.einsum('bhqd,bhkd->bhqk', Q, K) / math.sqrt(HEAD_DIM)
        scores = scores + _relative_bias(rel_bias, Tdim)[None]
        attn = jax.nn.softmax(scores, axis=-1)
        out = jnp.einsum('bhqk,bhkd->bhqd', attn, V)
        out = out.transpose(0, 2, 1, 3).reshape(Bdim, Tdim, Ddim)
        return out @ Wo.T + bo

    def _L0_xattn_ref(q, k, v, wqg, bqg, wkg, bkg, wvg, bvg, wql, bql, wkl, bkl, wvl, bvl, wp, bp):
        import jax, jax.numpy as jnp
        import numpy as np
        N_HEADS = 4
        IN_FEATURES = 128

        def _channel_attention(qm, km, vm, scale):
            b, n, c = qm.shape
            d = c // N_HEADS
            qh = qm.reshape(b, n, N_HEADS, d).transpose(0, 2, 3, 1)
            kh = km.reshape(b, n, N_HEADS, d).transpose(0, 2, 3, 1)
            vh = vm.reshape(b, n, N_HEADS, d).transpose(0, 2, 3, 1)
            scores = jnp.einsum('bhdn,bhen->bhde', qh, kh) * scale
            attn = jax.nn.softmax(scores, axis=-1)
            out = jnp.einsum('bhde,bhen->bhdn', attn, vh)
            return out.transpose(0, 3, 1, 2).reshape(b, n, c)
        scale = IN_FEATURES ** (-0.5)
        att_global = _channel_attention(q * wqg + bqg, k * wkg + bkg, v * wvg + bvg, scale)
        att_local = _channel_attention(q * wql + bql, k * wkl + bkl, v * wvl + bvl, scale)
        att = att_global + att_local
        return 2.0 * att * wp + bp

    def _L0_ffn_ref(x, Wr, W1, b1, W2, b2):
        import jax, jax.numpy as jnp
        import numpy as np
        DIM, E, K, H = (128, 8, 2, 512)
        batch, seq, dim = x.shape
        x_flat = x.reshape(-1, dim)
        logits = x_flat @ Wr
        w, ind = jax.lax.top_k(logits, K)
        w = jax.nn.softmax(w, axis=-1)
        combine = jnp.einsum('tke,tk->te', jax.nn.one_hot(ind, E, dtype=x.dtype), w)

        def body(acc, params):
            W1e, b1e, W2e, b2e, ce = params
            h = jax.nn.gelu(x_flat @ W1e + b1e, approximate=False)
            y = h @ W2e + b2e
            return (acc + ce[:, None] * y, None)
        out0 = jnp.zeros_like(x_flat)
        out, _ = jax.lax.scan(body, out0, (W1, b1, W2, b2, combine.T))
        return out.reshape(batch, seq, dim)

    def _L1_attn_ref(x, W_qkv, W_o1, W_o2, gamma):
        import jax, jax.numpy as jnp
        import numpy as np
        HEADS = 16
        HEAD_DIM = 64
        DIM = 128
        INNER = HEADS * HEAD_DIM

        def rotate_half(t):
            x1, x2 = jnp.split(t, 2, axis=-1)
            return jnp.concatenate((-x2, x1), axis=-1)

        def rope_table(n, head_dim, dtype):
            inv_freq = 1.0 / 10000.0 ** (jnp.arange(0, head_dim, 2, dtype=jnp.float32) / head_dim)
            freqs = jnp.arange(n, dtype=jnp.float32)[:, None] * inv_freq[None, :]
            return jnp.concatenate((freqs, freqs), axis=-1).astype(dtype)
        b, n, _ = x.shape
        scale = HEAD_DIM ** (-0.5)
        qkv = x @ W_qkv
        q, k, v = jnp.split(qkv, 3, axis=-1)
        to_heads = lambda t: t.reshape(b, n, HEADS, HEAD_DIM).transpose(0, 2, 1, 3)
        q, k, v = (to_heads(q), to_heads(k), to_heads(v))
        pos = rope_table(n, HEAD_DIM, x.dtype)
        cos, sin = (jnp.cos(pos), jnp.sin(pos))
        apply_rope = lambda t: t * cos + rotate_half(t) * sin
        q, k = (apply_rope(q), apply_rope(k))
        dots = jnp.einsum('bhid,bhjd->bhij', q, k) * scale
        causal = jnp.triu(jnp.ones((n, n), dtype=bool), 1)
        neg = -jnp.finfo(dots.dtype).max
        dots = jnp.where(causal, neg, dots)
        attn = jax.nn.softmax(dots, axis=-1)
        out = jnp.einsum('bhij,bhjd->bhid', attn, v)
        out = out.transpose(0, 2, 1, 3).reshape(b, n, INNER)
        out = jax.nn.relu(out @ W_o1) @ W_o2
        mean = jnp.mean(out, axis=-1, keepdims=True)
        var = jnp.var(out, axis=-1, keepdims=True)
        out = (out - mean) * jax.lax.rsqrt(var + 1e-05) * gamma
        return out

    def _L1_xattn_ref(query_input, kv_input, W_q, W_k, W_v, W_o):
        import jax, jax.numpy as jnp
        import numpy as np
        D_MODEL = 128
        N_HEADS = 16
        D_HEAD = D_MODEL // N_HEADS
        B, Sq, _ = query_input.shape
        Skv = kv_input.shape[1]
        q = (query_input @ W_q.T).reshape(B, Sq, N_HEADS, D_HEAD).transpose(0, 2, 1, 3)
        k = (kv_input @ W_k.T).reshape(B, Skv, N_HEADS, D_HEAD).transpose(0, 2, 1, 3)
        v = (kv_input @ W_v.T).reshape(B, Skv, N_HEADS, D_HEAD).transpose(0, 2, 1, 3)
        scores = jnp.einsum('bhqd,bhkd->bhqk', q, k) / jnp.sqrt(jnp.float32(D_HEAD))
        attn = jax.nn.softmax(scores, axis=-1)
        ctx = jnp.einsum('bhqk,bhkd->bhqd', attn, v)
        ctx = ctx.transpose(0, 2, 1, 3).reshape(B, Sq, D_MODEL)
        return ctx @ W_o.T

    def _L1_ffn_ref(inputs, gate_weight, ln_gamma, ln_beta, wi, wo, conf_w1, conf_b1, conf_w2, conf_b2, comp_w, comp_b):
        import jax, jax.numpy as jnp
        import numpy as np
        B, L, H, E, I = (4, 256, 128, 8, 512)
        S = B * L
        CAP_FACTOR_EVAL = 2.0
        MIN_CAP = 4
        _cap = int(np.floor(CAP_FACTOR_EVAL * S / E))
        _cap += _cap % 2
        CAPACITY = max(_cap, MIN_CAP)

        def _layer_norm(x, g, b, eps=1e-05):
            mu = x.mean(-1, keepdims=True)
            var = ((x - mu) ** 2).mean(-1, keepdims=True)
            return (x - mu) * jax.lax.rsqrt(var + eps) * g + b
        tokens = inputs.reshape(-1, H)
        residual = tokens
        tokens = _layer_norm(tokens, ln_gamma, ln_beta)
        complexity_score = jax.nn.sigmoid(tokens @ comp_w.T + comp_b).mean()
        hdn = jax.nn.relu(tokens @ conf_w1.T + conf_b1)
        confidence_score = jax.nn.sigmoid(hdn @ conf_w2.T + conf_b2).mean()
        logits = tokens.astype(jnp.float32) @ gate_weight.astype(jnp.float32).T
        probs = jax.nn.softmax(logits, axis=-1)
        top1 = jnp.argmax(logits, axis=-1)
        onehot = jax.nn.one_hot(top1, E, dtype=jnp.int32)
        rank_e = jnp.cumsum(onehot, axis=0) - onehot
        rank = jnp.sum(rank_e * onehot, axis=-1)
        keep = rank < CAPACITY
        weight = jnp.take_along_axis(probs, top1[:, None], axis=-1)[:, 0]
        weight = (weight * keep).astype(tokens.dtype)
        slot = jnp.where(keep, rank, 0)
        dispatch = jnp.zeros((E, CAPACITY, H), tokens.dtype)
        dispatch = dispatch.at[top1, slot].add(tokens * keep[:, None])
        h = jax.nn.gelu(jnp.einsum('ech,ehi->eci', dispatch, wi), approximate=False)
        expert_out = jnp.einsum('eci,eih->ech', h, wo)
        combined = weight[:, None] * expert_out[top1, slot]
        out = (residual + combined).reshape(inputs.shape)
        return out

    def _L2_attn_ref(x, W_DQ, W_UQ, W_DKV, W_UKV, W_QR, W_KR, W_O, q_norm_w, k_norm_w):
        import jax, jax.numpy as jnp
        import numpy as np
        B, T, D = (2, 256, 128)
        H = 16
        HD = D // H
        DL = 64
        NR = 64
        EPS = 1.1920929e-07

        def _rms_norm(x, w):
            ms = jnp.mean(jnp.square(x), axis=-1, keepdims=True)
            return x * jax.lax.rsqrt(ms + EPS) * w
        b, t, d = x.shape
        scale = HD ** (-0.5)
        xh = x.reshape(b, t, H, HD).transpose(0, 2, 1, 3)
        c_q = jnp.einsum('bhtd,ld->bhtl', xh, W_DQ)
        q_c = jnp.einsum('bhtl,dl->bhtd', c_q, W_UQ)
        q_c_norm = _rms_norm(q_c, q_norm_w)
        q_r = jnp.einsum('bhtd,rd->bhtr', q_c_norm, W_QR)
        q = jnp.concatenate([q_c_norm, q_r], axis=-1)
        c_kv = jnp.einsum('bhtd,ld->bhtl', xh, W_DKV)
        kv = jnp.einsum('bhtl,dl->bhtd', c_kv, W_UKV)
        k_c, v_c = (kv[..., :HD], kv[..., HD:])
        k_c_norm = _rms_norm(k_c, k_norm_w)
        k_r = jnp.einsum('bhtd,rd->bhtr', xh, W_KR)
        k = jnp.concatenate([k_c_norm, k_r], axis=-1)
        scores = jnp.einsum('bhqd,bhkd->bhqk', q, k) * scale
        causal = jnp.triu(jnp.full((t, t), -jnp.inf, dtype=scores.dtype), k=1)
        attn = jax.nn.softmax(scores + causal, axis=-1)
        ctx = jnp.einsum('bhqk,bhkd->bhqd', attn, v_c)
        out = jnp.einsum('bhtd,od->bhto', ctx, W_O)
        return out.transpose(0, 2, 1, 3).reshape(b, t, d)

    def _L2_xattn_ref(q, k, v, igate_kernel, igate_bias, fgate_kernel, fgate_bias, outnorm_scale):
        import jax, jax.numpy as jnp
        import numpy as np
        B, S, H, NH = (2, 256, 128, 4)
        DH = H // NH
        EPS_BACKEND = 1e-06
        EPS_LN = 1e-06

        def _mlstm_parallel_stabilized(q, k, v, igate_preact, fgate_preact):
            b, nh, s, dh = q.shape
            log_fg = jax.nn.log_sigmoid(fgate_preact)
            cs = jnp.concatenate([jnp.zeros((b, nh, 1), q.dtype), jnp.cumsum(log_fg[..., 0], axis=2)], axis=2)
            fg_matrix = cs[:, :, :, None] - cs[:, :, None, :]
            fg_matrix = fg_matrix[:, :, 1:, 1:]
            causal = jnp.tril(jnp.ones((s, s), dtype=bool))
            log_fg_matrix = jnp.where(causal, fg_matrix, -jnp.inf)
            log_D = log_fg_matrix + jnp.swapaxes(igate_preact, -2, -1)
            max_log_D = jnp.max(log_D, axis=-1, keepdims=True)
            D = jnp.exp(log_D - max_log_D)
            qk = jnp.einsum('bhsd,bhtd->bhst', q, k) / jnp.sqrt(jnp.asarray(dh, q.dtype))
            C = qk * D
            normalizer = jnp.maximum(jnp.abs(jnp.sum(C, axis=-1, keepdims=True)), jnp.exp(-max_log_D))
            C_norm = C / (normalizer + EPS_BACKEND)
            return jnp.einsum('bhst,bhtd->bhsd', C_norm, v)

        def _multihead_layernorm(x, scale):
            mean = jnp.mean(x, axis=-1, keepdims=True)
            var = jnp.var(x, axis=-1, keepdims=True)
            xn = (x - mean) * jax.lax.rsqrt(var + EPS_LN)
            return xn * scale.reshape(NH, 1, DH)
        b, s, h = q.shape
        gate_in = jnp.concatenate([q, k, v], axis=-1)
        ig = gate_in @ igate_kernel + igate_bias
        fg = gate_in @ fgate_kernel + fgate_bias
        ig = jnp.transpose(ig, (0, 2, 1))[..., None]
        fg = jnp.transpose(fg, (0, 2, 1))[..., None]
        qh = jnp.transpose(q.reshape(b, s, NH, DH), (0, 2, 1, 3))
        kh = jnp.transpose(k.reshape(b, s, NH, DH), (0, 2, 1, 3))
        vh = jnp.transpose(v.reshape(b, s, NH, DH), (0, 2, 1, 3))
        hs = _mlstm_parallel_stabilized(qh, kh, vh, ig, fg)
        hn = _multihead_layernorm(hs, outnorm_scale)
        return jnp.transpose(hn, (0, 2, 1, 3)).reshape(b, s, h)

    def _L2_ffn_ref(hidden_states, rms_weight, gate_w, w1, w2, w3):
        import jax, jax.numpy as jnp
        import numpy as np
        EPS = 1e-06
        TOP_K = 2
        B, S, H = hidden_states.shape
        E = gate_w.shape[0]
        x = hidden_states.astype(jnp.float32)
        var = jnp.mean(x * x, axis=-1, keepdims=True)
        h = rms_weight * (x * jax.lax.rsqrt(var + EPS))
        logits = jnp.einsum('bsh,eh->bse', h, gate_w)
        scores = jax.nn.softmax(logits.astype(jnp.float32), axis=-1)
        top_w, top_i = jax.lax.top_k(scores, TOP_K)
        top_w = top_w / jnp.sum(top_w, axis=-1, keepdims=True)
        top_w = top_w.astype(h.dtype)
        hf = h.reshape(-1, H)
        oh = jax.nn.one_hot(top_i.reshape(-1, TOP_K), E, dtype=h.dtype)
        cw = jnp.einsum('tke,tk->te', oh, top_w.reshape(-1, TOP_K))
        a = jnp.einsum('th,eih->eti', hf, w1)
        g = jnp.einsum('th,eih->eti', hf, w3)
        eo = jnp.einsum('eti,ehi->eth', jax.nn.silu(a) * g, w2)
        out = jnp.einsum('eth,te->th', eo, cw)
        return hidden_states + out.reshape(B, S, H)

    def _L3_attn_ref(x, Wq, Wk, Wv, Wo, bo, rel_emb):
        import jax, jax.numpy as jnp
        import numpy as np
        NUM_HEADS = 16
        CLIP = 16
        b, s, d_in = x.shape
        h, hd = (NUM_HEADS, x.shape[-1] // NUM_HEADS)
        q = (x @ Wq).reshape(b, s, h, hd).transpose(0, 2, 1, 3)
        k = (x @ Wk).reshape(b, s, h, hd).transpose(0, 2, 1, 3)
        v = (x @ Wv).reshape(b, s, h, hd).transpose(0, 2, 1, 3)
        r = jnp.arange(s)
        dist = jnp.clip(jnp.abs(r[None, :] - r[:, None]), 0, CLIP)
        a_k = rel_emb[dist]
        scores = jnp.einsum('bhqd,bhkd->bhqk', q, k) * a_k
        causal = jnp.triu(jnp.ones((s, s), dtype=bool), k=1)
        scores = jnp.where(causal, -jnp.inf, scores)
        attn = jax.nn.softmax(scores / np.sqrt(hd), axis=-1)
        ctx = jnp.einsum('bhqk,bhkd->bhqd', attn, v)
        ctx = ctx.transpose(0, 2, 1, 3).reshape(b, s, h * hd)
        return ctx @ Wo + bo

    def _L3_xattn_ref(q, k, v, Wq, bq, Wk, bk, Wv, bv, Wo, bo):
        import jax, jax.numpy as jnp
        import numpy as np
        D_MODEL = 128
        N_HEADS = 16
        HEAD_DIM = D_MODEL // N_HEADS

        def sparsemax(x):
            x = x - jnp.max(x, axis=-1, keepdims=True)
            zs = -jnp.sort(-x, axis=-1)
            L = x.shape[-1]
            rho = jnp.arange(1, L + 1, dtype=x.dtype)
            cssv = jnp.cumsum(zs, axis=-1) - 1.0
            support = zs > cssv / rho
            k = jnp.maximum(jnp.sum(support, axis=-1, keepdims=True), 1)
            tau = jnp.take_along_axis(cssv, k - 1, axis=-1) / k.astype(x.dtype)
            return jnp.clip(x - tau, 0.0)

        def _split_heads(x):
            B, L, _ = x.shape
            return x.reshape(B, L, N_HEADS, HEAD_DIM).transpose(0, 2, 1, 3)
        qh = _split_heads(q @ Wq + bq)
        kh = _split_heads(k @ Wk + bk)
        vh = _split_heads(v @ Wv + bv)
        scale = HEAD_DIM ** (-0.5)
        scores = jnp.einsum('bhqd,bhkd->bhqk', qh, kh) * scale
        attn = sparsemax(scores)
        out = jnp.einsum('bhqk,bhkd->bhqd', attn, vh)
        B, L = (q.shape[0], q.shape[1])
        out = out.transpose(0, 2, 1, 3).reshape(B, L, D_MODEL)
        return out @ Wo + bo

    def _L3_ffn_ref(x, n1_w, qkv_w, o_w, n2_w, gate_w, up_w, down_w):
        import jax, jax.numpy as jnp
        import numpy as np
        D, H, NE, K, ED = (128, 16, 8, 2, 512)
        B, S = (4, 128)
        EPS = 1e-06

        def rmsnorm(x, w):
            ms = jnp.mean(jnp.square(x.astype(jnp.float32)), axis=-1, keepdims=True)
            return x * jax.lax.rsqrt(ms + EPS).astype(x.dtype) * w

        def attn(x, qkv_w, o_w):
            b, s, d = x.shape
            hd = d // H
            qkv = (x @ qkv_w.T).reshape(b, s, 3, H, hd).transpose(2, 0, 3, 1, 4)
            q, k, v = (qkv[0], qkv[1], qkv[2])
            a = jnp.einsum('bhqd,bhkd->bhqk', q, k) * hd ** (-0.5)
            mask = jnp.triu(jnp.ones((s, s), dtype=bool), 1)
            a = jax.nn.softmax(jnp.where(mask, -1000000000.0, a), axis=-1)
            out = jnp.einsum('bhqk,bhkd->bhqd', a, v).transpose(0, 2, 1, 3).reshape(b, s, d)
            return out @ o_w.T

        def moe(x, gate_w, up_w, down_w):
            b, s, d = x.shape
            xf = x.reshape(b * s, d)
            gp = jax.nn.softmax(xf @ gate_w.T, axis=-1)
            ew, _ = jax.lax.top_k(gp, K)
            ew = ew / (jnp.sum(ew, axis=-1, keepdims=True) + 1e-09)
            ef = jax.nn.silu(xf @ up_w.T) @ down_w.T
            out = ef * jnp.sum(ew, axis=-1, keepdims=True)
            return out.reshape(b, s, d)
        x = x + attn(rmsnorm(x, n1_w), qkv_w, o_w)
        x = x + moe(rmsnorm(x, n2_w), gate_w, up_w, down_w)
        return x
    x = x + _L0_attn_ref(_layernorm(x, axis=-1), L0_attn_Wq, L0_attn_bq, L0_attn_Wk, L0_attn_bk, L0_attn_Wv, L0_attn_bv, L0_attn_rel_bias, L0_attn_Wo, L0_attn_bo)
    x = x + _L0_xattn_ref(_layernorm(x, axis=-1), ctx_1024, ctx_1024, L0_xattn_wqg, L0_xattn_bqg, L0_xattn_wkg, L0_xattn_bkg, L0_xattn_wvg, L0_xattn_bvg, L0_xattn_wql, L0_xattn_bql, L0_xattn_wkl, L0_xattn_bkl, L0_xattn_wvl, L0_xattn_bvl, L0_xattn_wp, L0_xattn_bp)
    x = x + _L0_ffn_ref(_layernorm(x, axis=-1), L0_ffn_Wr, L0_ffn_W1, L0_ffn_b1, L0_ffn_W2, L0_ffn_b2)
    x = x + _L1_attn_ref(_layernorm(x, axis=-1), L1_attn_W_qkv, L1_attn_W_o1, L1_attn_W_o2, L1_attn_gamma)
    x = x + _L1_xattn_ref(_layernorm(x, axis=-1), ctx_1024, L1_xattn_W_q, L1_xattn_W_k, L1_xattn_W_v, L1_xattn_W_o)
    x = x + _L1_ffn_ref(_layernorm(x, axis=-1), L1_ffn_gate_weight, L1_ffn_ln_gamma, L1_ffn_ln_beta, L1_ffn_wi, L1_ffn_wo, L1_ffn_conf_w1, L1_ffn_conf_b1, L1_ffn_conf_w2, L1_ffn_conf_b2, L1_ffn_comp_w, L1_ffn_comp_b)
    x = x + _L2_attn_ref(_layernorm(x, axis=-1), L2_attn_W_DQ, L2_attn_W_UQ, L2_attn_W_DKV, L2_attn_W_UKV, L2_attn_W_QR, L2_attn_W_KR, L2_attn_W_O, L2_attn_q_norm_w, L2_attn_k_norm_w)
    x = x + _L2_xattn_ref(_layernorm(x, axis=-1), ctx_1024, ctx_1024, L2_xattn_igate_kernel, L2_xattn_igate_bias, L2_xattn_fgate_kernel, L2_xattn_fgate_bias, L2_xattn_outnorm_scale)
    x = x + _L2_ffn_ref(_layernorm(x, axis=-1), L2_ffn_rms_weight, L2_ffn_gate_w, L2_ffn_w1, L2_ffn_w2, L2_ffn_w3)
    x = x + _L3_attn_ref(_layernorm(x, axis=-1), L3_attn_Wq, L3_attn_Wk, L3_attn_Wv, L3_attn_Wo, L3_attn_bo, L3_attn_rel_emb)
    x = x + _L3_xattn_ref(_layernorm(x, axis=-1), ctx_1024, ctx_1024, L3_xattn_Wq, L3_xattn_bq, L3_xattn_Wk, L3_xattn_bk, L3_xattn_Wv, L3_xattn_bv, L3_xattn_Wo, L3_xattn_bo)
    x = x + _L3_ffn_ref(_layernorm(x, axis=-1), L3_ffn_n1_w, L3_ffn_qkv_w, L3_ffn_o_w, L3_ffn_n2_w, L3_ffn_gate_w, L3_ffn_up_w, L3_ffn_down_w)
    return x

_drawn_inputs = setup_inputs


def setup_inputs(seed=0):
    import zlib

    import numpy as np

    out = dict(_drawn_inputs(seed))
    spreads = {'L0_attn_bq': (0.0, 0.292),
     'L0_attn_bk': (0.0, 2.0),
     'L0_attn_bv': (0.0, 0.1),
     'L0_attn_bo': (0.0, 0.1),
     'L0_ffn_b1': (0.0, 0.439),
     'L0_ffn_b2': (0.0, 0.339),
     'L1_attn_gamma': (1.0, 0.2),
     'L1_ffn_ln_gamma': (1.0, 0.6),
     'L1_ffn_ln_beta': (0.0, 0.645),
     'L1_ffn_conf_b1': (-1.0, 0.2),
     'L2_attn_q_norm_w': (1.0, 0.6),
     'L2_attn_k_norm_w': (1.0, 0.6),
     'L2_xattn_igate_kernel': (0.0, 0.1),
     'L2_xattn_fgate_kernel': (0.0, 0.1),
     'L2_xattn_outnorm_scale': (1.0, 0.2),
     'L2_ffn_rms_weight': (1.0, 0.2),
     'L3_xattn_bq': (0.0, 0.8),
     'L3_xattn_bk': (0.0, 2.0),
     'L3_xattn_bv': (0.0, 0.8),
     'L3_xattn_bo': (0.0, 0.499),
     'L3_ffn_n1_w': (1.0, 0.576),
     'L3_ffn_n2_w': (1.0, 0.6)}
    factors = {'L0_attn_rel_bias': 8.0,
     'L2_attn_W_DQ': 8.0,
     'L2_attn_W_UQ': 8.0,
     'L2_attn_W_DKV': 8.0,
     'L2_attn_W_UKV': 8.0,
     'L2_attn_W_QR': 8.0,
     'L2_attn_W_KR': 8.0,
     'L2_attn_W_O': 8.0,
     'L2_xattn_igate_bias': 200.0,
     'L3_attn_bo': 21.588,
     'L3_xattn_Wq': 8.0,
     'L3_xattn_Wk': 8.0,
     'L3_xattn_Wv': 8.0,
     'L3_xattn_Wo': 8.0,
     'L3_ffn_gate_w': 200.0}
    for name, (base, spread) in spreads.items():
        noise = np.random.default_rng([zlib.crc32(name.encode()), seed]).standard_normal(out[name].shape)
        drawn = base * np.exp(spread * noise) if base else spread * noise
        out[name] = jnp.asarray(drawn.astype(out[name].dtype))
    for name, factor in factors.items():
        out[name] = (out[name] * factor).astype(out[name].dtype)
    return out
```

```python
from collections import namedtuple
from contextlib import ExitStack

import numpy as np

import concourse.bass as bass
from concourse import mybir

F32 = mybir.dt.float32
ALU = mybir.AluOpType
ACT = mybir.ActivationFunctionType
AX = mybir.AxisListType

P = 128
D = 128
B, S = 32, 64
NT = 4
GROUP = NT * P
NG = B * S // GROUP
HEADS, HD = 16, 8
E = 8
HID = 512
HC = HID // P
I2W, I2C = 448, 4
IC = I2W // I2C
INNER, WH = 1024, 64
XR = 33
CAPACITY = 2 * 1024 // E
SIGNALS = 64
TOP = 8
SORT_STEPS = 21
BIG = 1.0e30


def shape_constants():
    p = np.arange(P)
    q = p % S
    k = np.arange(S)
    out = {}
    out["ident"] = np.eye(P)
    out["head_of_row"] = (p[:, None] % 32 // HD == np.arange(4)[None]) * 1.0
    out["causal"] = np.where(k[None, :] <= q[:, None], 0.0, -BIG)
    out["head_block"] = (p[:, None] // HD == p[None, :] // HD) * 1.0
    pair, col = p // 64, p % 64
    out["head_block_pairs"] = (p[:, None] // HD == (2 * (col // HD) + pair)[None, :]) * 1.0
    m = np.arange(127)
    dist = np.clip(63 - m, -16, 16) + 16
    out["distance_onehot"] = np.pad((np.arange(XR)[:, None] == dist[None]) * 1.0, ((0, 0), (0, 1)))
    out["ones"] = np.ones((P, P))
    out["same_seq"] = (p[:, None] // S == p[None] // S) * 1.0
    out["prefix_seq"] = ((p[:, None] // S == p[None] // S) & (p[:, None] <= p[None])) * 1.0
    out["before"] = (p[:, None] < p[None]) * 1.0
    out["pos_onehot"] = (q[:, None] == k[None]) * 1.0
    out["block32"] = (p[:, None] // 32 == np.arange(4)[None]) * 1.0
    d = np.arange(P) % WH % 32
    inv = (1.0 / np.float32(10000.0) ** (2 * d.astype(np.float32) / np.float32(WH))).astype(np.float32)
    freq = (np.arange(S, dtype=np.float32)[None, :] * inv[:, None]).astype(np.float32)
    out["rope_cos"] = np.cos(freq)
    out["rope_sin"] = np.sin(freq) * np.where(np.arange(P) % WH < 32, -1.0, 1.0)[:, None]
    out["expert_index"] = np.tile(np.arange(E, dtype=np.float32)[None], (P, 1))
    out["inverse_rank"] = np.broadcast_to(1.0 / np.arange(1, S + 1), (P, S))
    return {n: np.asarray(a, np.float32) for n, a in out.items()}


def pair_columns(w):
    return w.reshape(w.shape[0], HEADS // 2, 2, HD).transpose(0, 2, 1, 3).reshape(w.shape[0], D)


def column(v):
    return v.reshape(-1, 1)


def row(v):
    return np.broadcast_to(v.reshape(1, -1), (P, v.size))


def blocks(w, per):
    return w.reshape(-1, per, w.shape[-1]).transpose(1, 0, 2).reshape(per, -1)


def lay_out(i):
    small, big = dict(shape_constants()), {}
    rel = np.clip(np.arange(XR) - 16, -15, 15) + 15
    small["distance_table"] = np.concatenate(
        [i["L0_attn_rel_bias"][rel], i["L3_attn_rel_emb"][np.abs(np.arange(XR) - 16)][:, None]], 1)

    def attention(name, wq, wk, wv, wo):
        small[name + "_wq"], small[name + "_wk"] = wq, wk
        small[name + "_wv"], small[name + "_wo"] = pair_columns(wv), wo

    a = "L0_attn_"
    attention("L0a", i[a + "Wq"].T, i[a + "Wk"].T, i[a + "Wv"].T, i[a + "Wo"].T)
    small["L0a_bq"], small["L0a_bk"], small["L0a_bv"] = (column(i[a + n]) for n in ("bq", "bk", "bv"))
    small["L0a_bo"] = row(i[a + "bo"])
    a = "L0_xattn_"
    for s in "gl":
        small["L0x_wq" + s], small["L0x_bq" + s] = row(i[a + "wq" + s]), row(i[a + "bq" + s])
        small["L0x_wk" + s], small["L0x_bk" + s] = row(i[a + "wk" + s]), row(i[a + "bk" + s])
        small["L0x_wv" + s], small["L0x_bv" + s] = column(i[a + "wv" + s]), column(i[a + "bv" + s])
    small["L0x_wp"], small["L0x_bp"] = row(i[a + "wp"]), row(i[a + "bp"])
    small["L0f_wr"] = i["L0_ffn_Wr"]
    small["L0f_b1"] = i["L0_ffn_b1"].reshape(E * HC, P).T
    small["L0f_b2"] = i["L0_ffn_b2"]
    small["L1_wo1"] = blocks(i["L1_attn_W_o1"], P)
    small["L1_wo2"] = i["L1_attn_W_o2"]
    small["L1_gamma"] = row(i["L1_attn_gamma"])
    a = "L1_xattn_W_"
    attention("L1x", i[a + "q"].T, i[a + "k"].T, i[a + "v"].T, i[a + "o"].T)
    small["L1f_gate"] = i["L1_ffn_gate_weight"].T
    small["L1f_gamma"], small["L1f_beta"] = row(i["L1_ffn_ln_gamma"]), row(i["L1_ffn_ln_beta"])
    a = "L2_attn_W_"
    tile16 = lambda w: np.tile(w, (1, HEADS))
    small["L2a_dq"], small["L2a_uq"] = tile16(i[a + "DQ"]), tile16(i[a + "UQ"].T)
    small["L2a_dkv"] = tile16(i[a + "DKV"])
    small["L2a_uk"], small["L2a_uv"] = tile16(i[a + "UKV"][:HD].T), tile16(i[a + "UKV"][HD:].T)
    small["L2a_kr"], small["L2a_qr"] = tile16(i[a + "KR"]), tile16(i[a + "QR"])
    wo = np.zeros((D, D), np.float32)
    for h in range(HEADS):
        wo[h * HD:(h + 1) * HD, h * HD:(h + 1) * HD] = i[a + "O"].T
    small["L2a_wo"] = wo
    small["L2a_qn"] = column(np.tile(i["L2_attn_q_norm_w"], HEADS))
    small["L2a_kn"] = row(np.tile(i["L2_attn_k_norm_w"], HEADS))
    a = "L2_xattn_"
    for n in range(3):
        small[f"L2x_g{n}"] = np.concatenate(
            [i[a + "igate_kernel"][n * D:(n + 1) * D], i[a + "fgate_kernel"][n * D:(n + 1) * D]], 1)
    small["L2x_gb"] = row(np.concatenate([i[a + "igate_bias"], i[a + "fgate_bias"]]))
    small["L2x_on"] = row(i[a + "outnorm_scale"])
    small["L2f_rms"], small["L2f_gate"] = row(i["L2_ffn_rms_weight"]), i["L2_ffn_gate_w"].T
    a = "L3_attn_"
    attention("L3a", i[a + "Wq"], i[a + "Wk"], i[a + "Wv"], i[a + "Wo"])
    small["L3a_bo"] = row(i[a + "bo"])
    a = "L3_xattn_"
    attention("L3x", i[a + "Wq"], i[a + "Wk"], i[a + "Wv"], i[a + "Wo"])
    small["L3x_bq"], small["L3x_bk"], small["L3x_bv"] = (column(i[a + n]) for n in ("bq", "bk", "bv"))
    small["L3x_bo"] = row(i[a + "bo"])
    a = "L3_ffn_"
    w = i[a + "qkv_w"].T
    attention("L3f", w[:, :D], w[:, D:2 * D], w[:, 2 * D:], i[a + "o_w"].T)
    small["L3f_n1"], small["L3f_n2"] = row(i[a + "n1_w"]), row(i[a + "n2_w"])
    small["L3f_gate"], small["L3f_up"] = i[a + "gate_w"].T, i[a + "up_w"].T
    small["L3f_down"] = blocks(i[a + "down_w"].T, P)

    big["L0f_w1"] = np.ascontiguousarray(i["L0_ffn_W1"].transpose(1, 0, 2)).reshape(P, -1)
    big["L0f_w2"] = blocks(i["L0_ffn_W2"].reshape(-1, D), P)
    w = i["L1_attn_W_qkv"]
    turned = w[:, :2 * INNER].reshape(D, 2 * HEADS, 2, 32)[:, :, ::-1].reshape(D, 2 * INNER)
    v = w[:, 2 * INNER:].reshape(D, HEADS // 4, 2, 2, WH).transpose(0, 2, 1, 3, 4).reshape(D, INNER)
    big["L1_qkv"] = np.concatenate([w[:, :2 * INNER], turned, v], 1)
    big["L1f_w1"] = np.ascontiguousarray(i["L1_ffn_wi"].transpose(1, 0, 2)).reshape(P, -1)
    big["L1f_w2"] = blocks(i["L1_ffn_wo"].reshape(-1, D), P)
    big["L2f_w1"] = np.ascontiguousarray(i["L2_ffn_w1"].transpose(2, 0, 1)).reshape(P, -1)
    big["L2f_w3"] = np.ascontiguousarray(i["L2_ffn_w3"].transpose(2, 0, 1)).reshape(P, -1)
    big["L2f_w2"] = blocks(np.ascontiguousarray(i["L2_ffn_w2"].transpose(0, 2, 1)).reshape(-1, D), IC)
    return small, big


def pack(arrays):
    at, where, parts = 0, {}, []
    for name, a in arrays.items():
        where[name] = (at, a.shape[1], a.shape[0])
        parts.append(np.pad(a, ((0, P - a.shape[0]), (0, 0))))
        at += a.shape[1]
    return np.ascontiguousarray(np.concatenate(parts, 1)), where


def signals(core, names):
    words = names.split()
    first = core.taken
    core.taken += len(words)
    return namedtuple("Signals", words)(*core.halves[core.half][first:core.taken])


class Core:

    def __init__(self, nc, ctx, where, big):
        self.nc, self.ctx, self.where = nc, ctx, where
        self.halves = [[ctx.enter_context(nc.semaphore(f"signal_{h}_{i}")) for i in range(SIGNALS)]
                       for h in range(2)]
        self.half, self.taken = 1, 0
        self.small = self.buf("small", [P, max(a + n for a, n, _ in where.values())])
        self.big = {n: self.buf(n, [rows, cols]) for n, (rows, cols) in big.items() if n[:3] != "L1f"}
        for w in ("w1", "w2"):
            self.big["L1f_" + w] = self.big["L0f_" + w]
        self.x = self.buf("x", [P, NT, D])
        self.h = self.buf("h", [P, NT, D])
        self.hn = self.buf("hn", [P, NT, D])
        self.hT = self.buf("hT", [P, GROUP])
        self.ctx_tok = self.buf("ctx_tok", [P, NT, D])
        self.ctxT = self.buf("ctxT", [P, GROUP])
        self.qT = self.buf("qT", [P, GROUP])
        self.oT = self.buf("oT", [P, GROUP])
        self.att = self.buf("att", [P, NT, D])
        self.stats = self.buf("stats_buf", [P, NT, 6])
        self.moments = self.buf("moments_buf", [P, NT, 2])
        self.var_eps = self.buf("var_eps_buf", [P, NT])
        self.rstd = self.buf("rstd_buf", [P, NT])
        self.row_max = self.buf("row_max", [P, NT, HEADS])
        self.row_inv = self.buf("row_inv", [P, NT, HEADS])
        self.bias0 = self.buf("bias0", [P, HEADS * S])
        self.decay3 = self.buf("decay3", [P, S])
        self.vx = self.buf("vx", [P, NT, 2, HEADS // 2, 2 * (HD + 1)])
        self.minus_half = self.buf("minus_half", [P, 2 * HEADS])
        self.q_of_h = self.buf("q_of_h", [P, 3 * D])
        self.v_of_h = self.buf("v_of_h", [P, D])
        self.counts = self.buf("counts", [P, E])
        self.tiny = self.buf("tiny", [P, NT, 16, E])
        self.row_open = self.buf("row_open", [P, 1])
        self.count_open = self.ctx.enter_context(nc.sbuf_tensor("count_open", [1, 1], mybir.dt.int32))
        self.index = self.ctx.enter_context(nc.sbuf_tensor("index", [P, NT, E], mybir.dt.uint32))
        self.arena = self.buf("arena", [P, 9 * HEADS * S])
        self.ps = ctx.enter_context(nc.psum_tensor("ps", [P, 8, 512], F32))

    def turn_over(self):
        self.half, self.taken = 1 - self.half, 0

    def begin(self, g):
        last = self.halves[1 - self.half]
        g.sem_clear(range(last[0].num, last[-1].num + 1))

    def buf(self, name, shape):
        return self.ctx.enter_context(self.nc.sbuf_tensor(name, shape, F32))

    def w(self, name):
        at, n, rows = self.where[name]
        return self.small[0:rows, at:at + n]

    def room(self, k, n=1):
        return self.arena[:, k * 1024:(k + n) * 1024]


def bcast(ap, dim, n):
    ap = ap.unsqueeze(dim)
    shape = list(ap.shape)
    shape[dim] = n
    return ap.to_broadcast(shape)


def tok(t):
    return slice(t * P, (t + 1) * P)


def seq(t, b):
    return slice(t * P + b * S, t * P + (b + 1) * S)


def part(b):
    return slice(b * 64, (b + 1) * 64)


NORM = "stats moments square var_eps rstd scaled weighted ready "


def norm_vector(c, v, s, src, dst, kind="mean", weight=None, shift=None):
    for t in range(NT):
        v.bn_stats(c.stats[:, t], src[:, t]).then_inc(s.stats, 1)
    for t in range(NT):
        v.wait_ge(s.stats, t + 1)
        v.bn_aggr(c.moments[:, t], c.stats[:, t]).then_inc(s.moments, 1)
    v.wait_ge(s.moments, NT)
    v.wait_ge(s.rstd, 1)
    for t in range(NT):
        if kind == "rms":
            v.scalar_tensor_tensor(out=dst[:, t], in0=src[:, t], scalar=c.rstd[:, t:t + 1], in1=weight,
                                   op0=ALU.mult, op1=ALU.mult).then_inc(s.ready, 1)
            continue
        v.tensor_scalar(dst[:, t], src[:, t], c.moments[:, t, 0:1], c.rstd[:, t:t + 1],
                        ALU.subtract, ALU.mult).then_inc(s.ready if weight is None else s.scaled, 1)
        if weight is not None:
            v.wait_ge(s.scaled, t + 1)
            v.tensor_tensor(dst[:, t], dst[:, t], weight, ALU.mult)\
                .then_inc(s.ready if shift is None else s.weighted, 1)
        if shift is not None:
            v.wait_ge(s.weighted, t + 1)
            v.tensor_tensor(dst[:, t], dst[:, t], shift, ALU.add).then_inc(s.ready, 1)


def norm_gpsimd(c, g, s, eps, kind="mean"):
    mean, var = c.moments[:, :, 0], c.moments[:, :, 1]
    g.wait_ge(s.moments, NT)
    if kind == "rms":
        g.tensor_tensor(c.rstd[:], mean, mean, ALU.mult).then_inc(s.square, 1)
        g.wait_ge(s.square, 1)
        g.tensor_tensor(c.rstd[:], c.rstd[:], var, ALU.add).then_inc(s.square, 1)
        g.wait_ge(s.square, 2)
        var = c.rstd[:]
    g.tensor_scalar(c.var_eps[:], var, eps, None, ALU.add).then_inc(s.var_eps, 1)
    g.wait_ge(s.var_eps, 1)
    g.tensor_tensor(c.rstd[:], c.var_eps[:], c.minus_half[:, 0:NT], ALU.pow).then_inc(s.rstd, 1)


TURN = "turned_ps turned "


def turn_tensor(c, pe, ready, s, src):
    for t in range(NT):
        pe.wait_ge(ready, t + 1)
        pe.transpose(c.ps[:, t, 0:P], src[:, t], c.w("ident")).then_inc(s.turned_ps, 1)


def turn_scalar(c, act, s, dst):
    for t in range(NT):
        act.wait_ge(s.turned_ps, t + 1)
        act.copy(dst[:, tok(t)], c.ps[:, t, 0:P]).then_inc(s.turned, 1)


def attention(c, n, keys_from="h", mode="plain", q_scale=1.0, exp_scale=1.0, bias=False,
              out_bias=False, rms=False):
    nc = c.nc
    c.turn_over()
    s = signals(c, NORM + TURN + "k_ps v_ps q_ready kx_ready vx_ready scores_ps factored scored "
                "max_ready shifted probs_ready probsT_ps probsT_ready o_ps inv_ready att_ready oT_ps "
                "oT_ready y_ps y_added biased")
    if rms:
        r = signals(c, NORM)
    if mode == "latent":
        l = signals(c, "maps_ps copied squared sums means rms q_normed k_normed k_weighted keys_ready")
    if mode == "sparse":
        sp = signals(c, "row_starts top less_max summed candidates tau compared row_open open_ps count_open step "
                     "shifted_tau less_tau")
    kvT = c.hT if keys_from == "h" else c.ctxT
    kx = c.room(0, 2).rearrange("p (t b g k) -> p t b g k", t=NT, b=2, g=4)
    buf = lambda t: c.room((2, 3, 4, 7)[t] if mode == "sparse" else 2 + t % 3)
    probsT = lambda t: c.room(5 + t % 2)
    sums = lambda t: c.tiny[:, t, 0:4].rearrange("p a b -> p (a b)")
    rms_of = lambda t: c.tiny[:, t, 4:8].rearrange("p a b -> p (a b)")
    squares = lambda t: c.room(2)[:, t * 256:(t + 1) * 256]
    scores_ps = lambda g: c.ps[:, g, 0:256]
    q_ps = lambda t: c.ps[:, 4 + t, 0:P]
    k_ps = lambda t: c.ps[:, 4 + t, P:2 * P]
    maps = lambda t: c.room(3 + t // 2)[:, (t % 2) * 512:(t % 2) * 512 + 3 * D]
    o_ps = lambda t: c.ps[:, 6 + t % 2, 0:144]
    oT_ps = lambda t: c.ps[:, 6 + t % 2, 256:256 + P]
    y_ps = lambda t: c.ps[:, 6 + t % 2, 384:384 + P]
    heads = lambda a: a.rearrange("p (h d) -> p h d", d=HD)
    scores_read = s.shifted if mode == "plain" else s.factored if mode == "decay" else s.scored
    probs_ready = s.probs_ready

    with nc.Block() as block:
        @block.tensor
        def _(pe):
            turn_tensor(c, pe, r.ready if rms else s.ready, s, c.hn if rms else c.h)
            for t in range(NT):
                pe.wait_ge(s.turned, t + 1)
                if mode == "latent":
                    pe.matmul(c.ps[:, 4 + t, 0:3 * D], c.hT[:, tok(t)], c.q_of_h[:], start=True,
                              stop=True).then_inc(l.maps_ps, 1)
                else:
                    pe.matmul(q_ps(t), c.w(n + "_wq"), c.hT[:, tok(t)], start=True,
                              stop=True)
                    pe.matmul(k_ps(t), c.w(n + "_wk"), kvT[:, tok(t)], start=True,
                              stop=True).then_inc(s.k_ps, 1)
                wv = c.v_of_h[:] if mode == "latent" else c.w(n + "_wv")
                for b in range(2):
                    for u in range(2):
                        last = pe.matmul(c.ps[part(u), t, part(b)], kvT[:, seq(t, b)],
                                         wv[:, part(u)], start=True, stop=True)
                last.then_inc(s.v_ps, 1)
            if mode == "latent":
                for t in range(NT):
                    pe.wait_ge(l.q_normed, t + 1)
                    pe.transpose(q_ps(t), c.att[:, t], c.w("ident"))
                    pe.wait_ge(l.keys_ready, t + 1)
                    pe.transpose(k_ps(t), c.hn[:, t], c.w("ident")).then_inc(s.k_ps, 1)

            def scores(t):
                pe.wait_ge(s.q_ready, t + 1)
                pe.wait_ge(s.kx_ready, t + 1)
                for g in range(4):
                    if t == 0:
                        pe.wait_ge(s.vx_ready, 2 * (g + 1))
                    else:
                        pe.wait_ge(scores_read, 4 * (t - 1) + g + 1)
                    for b in range(2):
                        rows = slice(g * 32, (g + 1) * 32)
                        last = pe.matmul(scores_ps(g)[part(b)], c.qT[rows, seq(t, b)],
                                         kx[rows, t, b].rearrange("p g k -> p (g k)"), start=True, stop=True)
                    last.then_inc(s.scores_ps, 1)

            def turn_probs(t):
                pe.wait_ge(probs_ready, t + 1)
                if t == 0:
                    pe.wait_ge(s.kx_ready, 2)
                for k in range(2):
                    if t >= 1:
                        pe.wait_ge(s.probsT_ready, 2 * (t - 1) + k + 1)
                    for j in range(4):
                        last = pe.transpose(c.ps[:, 4 + k, j * P:(j + 1) * P],
                                            buf(t)[:, (4 * k + j) * P:(4 * k + j + 1) * P], c.w("ident"))
                    last.then_inc(s.probsT_ps, 1)

            def weigh_values(t):
                if t == 0:
                    pe.wait_ge(s.kx_ready, NT)
                if t >= 2:
                    pe.wait_ge(s.y_added, t - 1)
                pe.wait_ge(s.probsT_ready, 2 * t + 2)
                for j in range(HEADS // 2):
                    for b in range(2):
                        last = pe.matmul(o_ps(t)[part(b), j * 18:(j + 1) * 18],
                                         probsT(t)[:, seq(j, b)], c.vx[:, t, b, j], start=True, stop=True)
                last.then_inc(s.o_ps, 1)

            def project(t):
                pe.wait_ge(s.att_ready, t + 1)
                pe.transpose(oT_ps(t), c.att[:, t], c.w("ident")).then_inc(s.oT_ps, 1)
                pe.wait_ge(s.oT_ready, t + 1)
                pe.matmul(y_ps(t), c.oT[:, tok(t)], c.w(n + "_wo"), start=True, stop=True)\
                    .then_inc(s.y_ps, 1)

            if mode == "sparse":
                for t in range(NT):
                    scores(t)
                pe.wait_ge(s.kx_ready, NT)
                pe.wait_ge(sp.row_open, 1)
                pe.matmul(c.ps[0:1, 7, 0:1], c.row_open[:], c.w("ones")[:, 0:1], start=True, stop=True)\
                    .then_inc(sp.open_ps, 1)
            for k in range(NT + 3):
                if k < NT and mode != "sparse":
                    scores(k)
                if 0 <= k - 1 < NT:
                    turn_probs(k - 1)
                if 0 <= k - 2 < NT:
                    weigh_values(k - 2)
                if 0 <= k - 3 < NT:
                    project(k - 3)

        @block.scalar
        def _(act):
            turn_scalar(c, act, s, c.hT)
            for t in range(NT):
                act.wait_ge(s.v_ps, t + 1)
                for u in range(2):
                    act.copy(c.vx[part(u), t, :, :, u * 9:u * 9 + HD],
                             c.ps[part(u), t, 0:P].rearrange("p (b j d) -> p b j d", b=2, d=HD))\
                        .then_inc(s.vx_ready, 1)
                if mode == "latent":
                    act.wait_ge(l.maps_ps, t + 1)
                    act.copy(maps(t), c.ps[:, 4 + t, 0:3 * D]).then_inc(l.copied, 1)
                    act.wait_ge(l.copied, t + 1)
                    act.activation(squares(t), maps(t)[:, 0:2 * D], ACT.Square).then_inc(l.squared, 1)
            if mode == "sparse":
                for t in range(NT):
                    for g in range(4):
                        act.wait_ge(s.scores_ps, 4 * t + g + 1)
                        act.copy(buf(t)[:, g * 256:(g + 1) * 256], scores_ps(g)).then_inc(s.scored, 1)
            for k in range(NT + 3):
                if k < NT:
                    if mode == "sparse":
                        act.wait_ge(sp.less_tau, k + 1)
                    else:
                        act.wait_ge(s.shifted, 4 * k + 4 if mode == "plain" else k + 1)
                    act.activation(buf(k), buf(k), ACT.Relu if mode == "sparse" else ACT.Exp,
                                   scale=exp_scale).then_inc(s.probs_ready, 1)
                t = k - 1
                if 0 <= t < NT:
                    for j in range(2):
                        act.wait_ge(s.probsT_ps, 2 * t + j + 1)
                        if t >= 2:
                            act.wait_ge(s.o_ps, t - 1)
                        act.copy(probsT(t)[:, j * 512:(j + 1) * 512], c.ps[:, 4 + j])\
                            .then_inc(s.probsT_ready, 1)
                t = k - 3
                if 0 <= t < NT:
                    act.wait_ge(s.oT_ps, t + 1)
                    if bias:
                        act.activation(c.oT[:, tok(t)], oT_ps(t), ACT.Identity, bias=c.w(n + "_bv"))\
                            .then_inc(s.oT_ready, 1)
                    else:
                        act.copy(c.oT[:, tok(t)], oT_ps(t)).then_inc(s.oT_ready, 1)

        @block.gpsimd
        def _(g):
            c.begin(g)
            norm_gpsimd(c, g, s, 1e-5)
            if rms:
                norm_gpsimd(c, g, r, 1e-6, "rms")
            if mode == "sparse":
                row_starts = c.room(5)[:, 0:NT * HEADS * TOP]
                g.memset(row_starts, 1.0).then_inc(sp.row_starts, 1)
                g.wait_ge(sp.row_starts, 1)
                g.memset(row_starts.rearrange("p (r k) -> p r k", k=TOP)[:, :, 0], 0.0)\
                    .then_inc(sp.row_starts, 1)
            if mode == "latent":
                for t in range(NT):
                    g.wait_ge(l.sums, t + 1)
                    g.tensor_scalar(sums(t), sums(t), 1.0 / HD, 1.1920929e-07, ALU.mult, ALU.add)\
                        .then_inc(l.means, 1)
                    g.wait_ge(l.means, t + 1)
                    g.tensor_tensor(rms_of(t), sums(t), c.minus_half[:], ALU.pow).then_inc(l.rms, 1)

        @block.vector
        def _(v):
            norm_vector(c, v, s, c.x, c.h)
            if rms:
                v.wait_ge(s.ready, NT)
                norm_vector(c, v, r, c.h, c.hn, "rms", c.w(n + "_n1"))
            if mode == "latent":
                for t in range(NT):
                    v.wait_ge(l.squared, t + 1)
                    v.tensor_reduce(sums(t), heads(squares(t)), AX.X, ALU.add).then_inc(l.sums, 1)
                for t in range(NT):
                    keys = c.hn[:, t]
                    v.wait_ge(l.rms, t + 1)
                    v.tensor_tensor(heads(c.att[:, t]), heads(maps(t)[:, 0:D]),
                                    bcast(rms_of(t)[:, 0:HEADS], 2, HD), ALU.mult).then_inc(l.q_normed, 1)
                    v.tensor_tensor(heads(keys), heads(maps(t)[:, D:2 * D]),
                                    bcast(rms_of(t)[:, HEADS:2 * HEADS], 2, HD), ALU.mult)\
                        .then_inc(l.k_normed, 1)
                    v.wait_ge(l.k_normed, t + 1)
                    v.tensor_tensor(keys, keys, c.w("L2a_kn"), ALU.mult).then_inc(l.k_weighted, 1)
                    v.wait_ge(l.k_weighted, t + 1)
                    v.tensor_tensor(keys, keys, maps(t)[:, 2 * D:3 * D], ALU.add).then_inc(l.keys_ready, 1)
            for t in range(NT):
                v.wait_ge(s.k_ps, t + 1)
                if bias:
                    v.tensor_scalar(c.qT[:, tok(t)], q_ps(t), c.w(n + "_bq"), q_scale, ALU.add, ALU.mult)\
                        .then_inc(s.q_ready, 1)
                else:
                    v.tensor_scalar(c.qT[:, tok(t)], q_ps(t), c.w("L2a_qn") if mode == "latent" else q_scale,
                                    None, ALU.mult).then_inc(s.q_ready, 1)
                own = bcast(c.w("head_of_row"), 2, S)
                for b in range(2):
                    keys = bcast(k_ps(t)[:, part(b)], 1, 4)
                    if bias:
                        last = v.scalar_tensor_tensor(out=kx[:, t, b], in0=keys, scalar=c.w(n + "_bk"),
                                                      in1=own, op0=ALU.add, op1=ALU.mult)
                    else:
                        last = v.tensor_tensor(kx[:, t, b], keys, own, ALU.mult)
                last.then_inc(s.kx_ready, 1)

            def shift(t):
                shaped = buf(t).rearrange("p (h k) -> p h k", k=S)
                if t >= 3:
                    v.wait_ge(s.probsT_ps, 2 * (t - 2))
                if mode == "plain":
                    for g in range(4):
                        own = slice(4 * g, 4 * g + 4)
                        ps = scores_ps(g).rearrange("p (h k) -> p h k", k=S)
                        v.wait_ge(s.scores_ps, 4 * t + g + 1)
                        v.tensor_reduce(c.row_max[:, t, own], ps, AX.X, ALU.max).then_inc(s.max_ready, 1)
                        v.wait_ge(s.max_ready, 4 * t + g + 1)
                        v.tensor_tensor(shaped[:, own], ps, bcast(c.row_max[:, t, own], 2, S), ALU.subtract)\
                            .then_inc(s.shifted, 1)
                    return
                for g in range(4):
                    out = shaped[:, 4 * g:4 * g + 4]
                    ps = scores_ps(g).rearrange("p (h k) -> p h k", k=S)
                    v.wait_ge(s.scores_ps, 4 * t + g + 1)
                    if mode == "bias":
                        v.tensor_tensor(out, ps, c.bias0[:].rearrange("p (h k) -> p h k", k=S)
                                        [:, 4 * g:4 * g + 4], ALU.add).then_inc(s.scored, 1)
                    elif mode == "decay":
                        v.tensor_tensor(out, ps, bcast(c.decay3[:], 1, 4), ALU.mult).then_inc(s.factored, 1)
                    else:
                        v.tensor_tensor(out, ps, bcast(c.w("causal"), 1, 4), ALU.add).then_inc(s.scored, 1)
                if mode == "decay":
                    v.wait_ge(s.factored, 4 * t + 4)
                    v.tensor_tensor(shaped, shaped, bcast(c.w("causal"), 1, HEADS), ALU.add)\
                        .then_inc(s.scored, 1)
                v.wait_ge(s.scored, t + 1 if mode == "decay" else 4 * t + 4)
                v.tensor_reduce(c.row_max[:, t], shaped, AX.X, ALU.max).then_inc(s.max_ready, 1)
                v.wait_ge(s.max_ready, t + 1)
                v.tensor_tensor(shaped, shaped, bcast(c.row_max[:, t], 2, S), ALU.subtract)\
                    .then_inc(s.shifted, 1)

            def normalise(t):
                o = o_ps(t).rearrange("p (h d) -> p h d", d=HD + 1)
                v.wait_ge(s.o_ps, t + 1)
                v.reciprocal(c.row_inv[:, t], o[:, :, HD]).then_inc(s.inv_ready, 1)
                v.wait_ge(s.inv_ready, t + 1)
                v.tensor_tensor(heads(c.att[:, t]), o[:, :, 0:HD], bcast(c.row_inv[:, t], 2, HD),
                                ALU.mult).then_inc(s.att_ready, 1)

            def add(t):
                x = c.h if rms else c.x
                v.wait_ge(s.y_ps, t + 1)
                v.tensor_tensor(x[:, t], x[:, t], y_ps(t), ALU.add).then_inc(s.y_added, 1)
                if out_bias:
                    v.wait_ge(s.y_added, t + 1)
                    v.tensor_tensor(x[:, t], x[:, t], c.w(n + "_bo"), ALU.add).then_inc(s.biased, 1)

            def less_threshold(t):
                shaped = buf(t).rearrange("p (h k) -> p h k", k=S)
                v.tensor_tensor(shaped, shaped, bcast(c.row_inv[:, t], 2, S), ALU.subtract)\
                    .then_inc(sp.less_tau, 1)

            if mode == "sparse":
                thresholds(c, v, s, sp, buf)
            for k in range(NT + 3):
                if k < NT:
                    if mode == "sparse":
                        less_threshold(k)
                    else:
                        shift(k)
                if 0 <= k - 2 < NT:
                    normalise(k - 2)
                if 0 <= k - 3 < NT:
                    add(k - 3)


def thresholds(c, v, s, sp, z):
    parts = c.room(8).rearrange("p (s r k) -> p s r k", s=2, k=TOP)
    top, sums = parts[:, 0], parts[:, 1]
    of_head = c.row_max[:].rearrange("p t h -> p (t h)")
    tau = c.row_inv[:].rearrange("p t h -> p (t h)")
    open_rows = c.tiny[:, 0, 0:8].rearrange("p a b -> p (a b)")
    for t in range(NT):
        v.wait_ge(s.scored, 4 * t + 4)
        for h in range(HEADS):
            last = v.max(out=top[:, HEADS * t + h], in_=z(t)[:, h * S:(h + 1) * S])
        last.then_inc(sp.top, 1)
    v.wait_ge(sp.top, NT)
    v.tensor_copy(of_head, top[:, :, 0]).then_inc(s.max_ready, 1)
    v.wait_ge(s.max_ready, 1)
    v.tensor_tensor(top, top, bcast(of_head, 2, TOP), ALU.subtract).then_inc(sp.less_max, 1)
    v.wait_ge(sp.less_max, 1)
    flat = lambda a: a.rearrange("p r k -> p (r k)")
    v.wait_ge(sp.row_starts, 2)
    v.tensor_tensor_scan(flat(sums), c.room(5)[:, 0:NT * HEADS * TOP], flat(top), 0.0, ALU.mult, ALU.add)\
        .then_inc(sp.summed, 1)
    v.wait_ge(sp.summed, 1)
    v.scalar_tensor_tensor(out=sums, in0=sums, scalar=-1.0,
                           in1=bcast(c.w("inverse_rank")[:, 0:TOP], 1, NT * HEADS), op0=ALU.add,
                           op1=ALU.mult).then_inc(sp.candidates, 1)
    v.wait_ge(sp.candidates, 1)
    v.tensor_reduce(tau, sums, AX.X, ALU.max).then_inc(sp.tau, 1)
    v.wait_ge(sp.tau, 1)
    v.tensor_tensor(open_rows, top[:, :, TOP - 1], tau, ALU.is_gt).then_inc(sp.compared, 1)
    v.wait_ge(sp.compared, 1)
    v.tensor_reduce(c.row_open[:], open_rows, AX.X, ALU.max).then_inc(sp.row_open, 1)
    v.wait_ge(sp.open_ps, 1)
    v.tensor_copy(c.count_open[:], c.ps[0:1, 7, 0:1]).then_inc(sp.count_open, 1)
    v.wait_ge(sp.count_open, 1)
    open_count = v.value_load(c.count_open[0:1, 0:1], min_val=0, max_val=P)
    with v.If(open_count > 0):
        v.memset(c.room(8), 1.0).then_inc(sp.step, 1)
        v.wait_ge(sp.step, 1)
        v.memset(c.room(8).rearrange("p (h k) -> p h k", k=S)[:, :, 0], 0.0).then_inc(sp.step, 1)
        for t in range(NT):
            sort_rows(c, v, sp.step, t, z(t))
    v.tensor_tensor(tau, tau, of_head, ALU.add).then_inc(sp.shifted_tau, 1)
    v.wait_ge(sp.shifted_tau, 1)


def sort_rows(c, v, step, t, z):
    spare = [c.room(5), c.room(6)]
    shaped = lambda a: a.rearrange("p (h k) -> p h k", k=S)
    done = (SORT_STEPS + 4) * t + 3
    src, at = spare[1], 0
    v.tensor_tensor(shaped(src), shaped(z), bcast(c.row_max[:, t], 2, S), ALU.subtract).then_inc(step, 1)
    v.wait_ge(step, done)
    k = 2
    while k <= S:
        j = k // 2
        while j >= 1:
            dst = spare[at % 2]
            ways = 2 if k < S else 1
            cut = lambda a: a.rearrange("p (b way g s r) -> p b way g s r", way=ways, g=k // (2 * j), s=2, r=j)
            for way in range(ways):
                for side in range(2):
                    op = ALU.max if side == way else ALU.min
                    last = v.tensor_tensor(cut(dst)[:, :, way, :, side], cut(src)[:, :, way, :, 0],
                                           cut(src)[:, :, way, :, 1], op)
            at += 1
            last.then_inc(step, 1)
            v.wait_ge(step, done + at)
            src = dst
            j //= 2
        k *= 2
    sums = spare[at % 2]
    v.tensor_tensor_scan(sums, c.room(8), src, 0.0, ALU.mult, ALU.add).then_inc(step, 1)
    v.wait_ge(step, done + at + 1)
    v.scalar_tensor_tensor(out=shaped(src), in0=shaped(sums), scalar=-1.0,
                           in1=bcast(c.w("inverse_rank"), 1, HEADS), op0=ALU.add, op1=ALU.mult)\
        .then_inc(step, 1)
    v.wait_ge(step, done + at + 2)
    v.tensor_reduce(c.row_inv[:, t], shaped(src), AX.X, ALU.max).then_inc(step, 1)
    v.wait_ge(step, done + at + 3)


def channel_attention(c):
    nc = c.nc
    c.turn_over()
    s = signals(c, NORM + "q_scaled q_ready k_scaled k_ready v_ready scores_ps max_ready shifted "
                "exp_ready sum_ready inv_ready weights_ready spread turned_ps turned y_ps doubled summed "
                "biased")
    SETS = "gl"
    q = [c.room(0)[:, i * 512:(i + 1) * 512].rearrange("p (t d) -> p t d", t=NT) for i in range(2)]
    k = [c.room(1)[:, i * 512:(i + 1) * 512].rearrange("p (t d) -> p t d", t=NT) for i in range(2)]
    vT = [c.room(2)[:, i * 512:(i + 1) * 512] for i in range(2)]
    score = c.room(3)[:, 0:512].rearrange("p (b m e) -> p b m e", b=2, e=32)
    score_ps = c.ps[:, 0:2, 0:256].rearrange("p b (m e) -> p b m e", e=32)
    row = c.tiny[:, 0].rearrange("p a b -> p (a b)")
    stat = lambda i: row[:, i * 16:(i + 1) * 16].rearrange("p (b m) -> p b m", b=2)
    spread = c.room(3, 2)
    blocks_of = c.room(5, 2)
    diag = c.room(7, 2)
    with nc.Block() as block:
        @block.tensor
        def _(pe):
            pe.wait_ge(s.q_ready, 2)
            pe.wait_ge(s.k_ready, 2)
            for t in range(NT):
                for b in range(2):
                    for i in range(2):
                        for h in range(4):
                            ch = slice(32 * h, 32 * h + 32)
                            last = pe.matmul(c.ps[ch, b, (2 * t + i) * 32:(2 * t + i + 1) * 32],
                                             q[i][part(b), t, ch], k[i][part(b), t, ch],
                                             start=True, stop=True,
                                             tile_position=(64 * b, 32 * h))
            last.then_inc(s.scores_ps, 1)
            for m in range(4):
                pe.wait_ge(s.spread, m + 1)
                for j in range(4):
                    last = pe.transpose(c.ps[:, 2 + m, j * P:(j + 1) * P],
                                        diag[:, (4 * m + j) * P:(4 * m + j + 1) * P], c.w("ident"))
                last.then_inc(s.turned_ps, 1)
            pe.wait_ge(s.v_ready, 2)
            pe.wait_ge(s.turned, 4)
            for t in range(NT):
                for b in range(2):
                    for i in range(2):
                        last = pe.matmul(c.ps[part(b), 6, tok(t)], vT[i][:, seq(t, b)],
                                         blocks_of[:, (8 * b + 2 * t + i) * P:(8 * b + 2 * t + i + 1) * P],
                                         start=(i == 0), stop=(i == 1))
            last.then_inc(s.y_ps, 1)

        @block.scalar
        def _(act):
            for i, n in enumerate(SETS):
                act.activation(vT[i], c.ctxT[:], ACT.Identity, bias=c.w("L0x_bv" + n),
                               scale=c.w("L0x_wv" + n)).then_inc(s.v_ready, 1)
            act.wait_ge(s.shifted, 1)
            act.activation(score, score, ACT.Exp, scale=D ** -0.5).then_inc(s.exp_ready, 1)
            for m in range(4):
                act.wait_ge(s.turned_ps, m + 1)
                act.copy(blocks_of[:, m * 512:(m + 1) * 512], c.ps[:, 2 + m]).then_inc(s.turned, 1)

        @block.gpsimd
        def _(g):
            c.begin(g)
            norm_gpsimd(c, g, s, 1e-5)
            for i, n in enumerate(SETS):
                g.tensor_tensor(k[i], c.ctx_tok[:], bcast(c.w("L0x_wk" + n), 1, NT), ALU.mult)\
                    .then_inc(s.k_scaled, 1)
                g.wait_ge(s.k_scaled, i + 1)
                g.tensor_tensor(k[i], k[i], bcast(c.w("L0x_bk" + n), 1, NT), ALU.add).then_inc(s.k_ready, 1)

        @block.vector
        def _(v):
            norm_vector(c, v, s, c.x, c.h)
            v.wait_ge(s.ready, NT)
            for i, n in enumerate(SETS):
                v.tensor_tensor(q[i], c.h[:], bcast(c.w("L0x_wq" + n), 1, NT), ALU.mult)\
                    .then_inc(s.q_scaled, 1)
                v.wait_ge(s.q_scaled, i + 1)
                v.tensor_tensor(q[i], q[i], bcast(c.w("L0x_bq" + n), 1, NT), ALU.add).then_inc(s.q_ready, 1)
            v.wait_ge(s.scores_ps, 1)
            v.tensor_reduce(stat(0), score_ps, AX.X, ALU.max).then_inc(s.max_ready, 1)
            v.wait_ge(s.max_ready, 1)
            v.tensor_tensor(score, score_ps, bcast(stat(0), 3, 32), ALU.subtract).then_inc(s.shifted, 1)
            v.wait_ge(s.exp_ready, 1)
            v.tensor_reduce(stat(1), score, AX.X, ALU.add).then_inc(s.sum_ready, 1)
            v.wait_ge(s.sum_ready, 1)
            v.reciprocal(stat(2), stat(1)).then_inc(s.inv_ready, 1)
            v.wait_ge(s.inv_ready, 1)
            v.tensor_tensor(score, score, bcast(stat(2), 3, 32), ALU.mult).then_inc(s.weights_ready, 1)
            v.wait_ge(s.weights_ready, 1)
            flat = c.room(3)[:, 0:512].rearrange("p (m e) -> p m e", e=32)
            for m in range(4):
                v.tensor_tensor(diag[:, m * 512:(m + 1) * 512].rearrange("p (m h e) -> p m h e", h=4, e=32),
                                bcast(flat[:, 4 * m:4 * m + 4], 2, 4),
                                bcast(bcast(c.w("block32"), 2, 32), 1, 4), ALU.mult).then_inc(s.spread, 1)
            v.wait_ge(s.y_ps, 1)
            y = c.att[:]
            v.scalar_tensor_tensor(out=y, in0=c.ps[:, 6].rearrange("p (t d) -> p t d", t=NT), scalar=2.0,
                                   in1=bcast(c.w("L0x_wp"), 1, NT), op0=ALU.mult, op1=ALU.mult)\
                .then_inc(s.doubled, 1)
            v.wait_ge(s.doubled, 1)
            v.tensor_tensor(c.x[:], c.x[:], y, ALU.add).then_inc(s.summed, 1)
            v.wait_ge(s.summed, 1)
            v.tensor_tensor(c.x[:], c.x[:], bcast(c.w("L0x_bp"), 1, NT), ALU.add).then_inc(s.biased, 1)


ROUTE = "logits_ps logits_ready top_ready index_ready index_f gap gap_exp denominator first second "


def route_vector(c, v, s, top, bank):
    T = c.tiny
    v.wait_ge(s.logits_ps, NT)
    for t in range(NT):
        v.tensor_copy(T[:, t, 0], c.ps[:, bank, t * E:(t + 1) * E]).then_inc(s.logits_ready, 1)
        v.wait_ge(s.logits_ready, t + 1)
        v.max(T[:, t, 1], T[:, t, 0]).then_inc(s.top_ready, 1)
        v.wait_ge(s.top_ready, t + 1)
        v.max_index(c.index[:, t], T[:, t, 1], T[:, t, 0]).then_inc(s.index_ready, 1)
    v.wait_ge(s.index_ready, NT)
    v.tensor_copy(T[:, :, 2], c.index[:]).then_inc(s.index_f, 1)


def experts(c, n, top, gated):
    nc = c.nc
    twice = n != "L0f"
    c.turn_over()
    s = signals(c, NORM + TURN + ROUTE + "up_ps gate_ps hidden_ready activated down_ps added base "
                "total prob onehot rank_ps ranked kept counted picked weights_ready wT_ps wT_ready counts_ps")
    if twice:
        r = signals(c, NORM)
    src = c.hn if twice else c.h
    chunks, width = (I2C, IC) if gated else (HC, P)
    hidden = lambda e: c.room(2 * (e % 2), 2)[0:width].rearrange("p (c n) -> p c n", c=chunks)
    act_buf = lambda k: c.room(4)[0:width, (k % 2) * 512:(k % 2 + 1) * 512]
    T = c.tiny
    wT = c.room(5)[0:E, 0:GROUP]
    ps_small = 7
    with nc.Block() as block:
        @block.tensor
        def _(pe):
            turn_tensor(c, pe, (r if twice else s).ready, s, src)
            for t in range(NT):
                pe.wait_ge(s.turned, t + 1)
                pe.matmul(c.ps[:, ps_small, t * E:(t + 1) * E], c.hT[:, tok(t)],
                          c.w(n + ("_wr" if n == "L0f" else "_gate")), start=True, stop=True)\
                    .then_inc(s.logits_ps, 1)

            def up(e):
                for j in range(chunks):
                    k = e * chunks + j
                    cols = slice(k * width, (k + 1) * width)
                    if gated:
                        for w, bank, sig in (("w1", 0, s.up_ps), ("w3", 2, s.gate_ps)):
                            if k >= 2:
                                pe.wait_ge(s.hidden_ready, k - 1)
                            pe.matmul(c.ps[0:width, bank + k % 2], c.big[n + "_" + w][:, cols], c.hT[:],
                                      start=True, stop=True).then_inc(sig, 1)
                    else:
                        if k >= 4:
                            pe.wait_ge(s.hidden_ready, k - 3)
                        pe.matmul(c.ps[:, k % 4], c.big[n + "_w1"][:, cols], c.hT[:], start=True,
                                  stop=True).then_inc(s.up_ps, 1)

            def down(e):
                pe.wait_ge(s.hidden_ready, (e + 1) * chunks)
                if e >= 2:
                    pe.wait_ge(s.added, NT * (e - 1))
                for t in range(NT):
                    for j in range(chunks):
                        k = e * chunks + j
                        last = pe.matmul(c.ps[:, 4 + e % 2, tok(t)], hidden(e)[:, j, tok(t)],
                                         c.big[n + "_w2"][0:width, k * D:(k + 1) * D],
                                         start=(j == 0), stop=(j == chunks - 1))
                last.then_inc(s.down_ps, 1)

            for m in ("w1", "w3", "w2") if gated else ("w1", "w2"):
                pe.wait_ge(c.loaded[f"{n}_{m}"], 16)
            up(0)
            if n == "L1f":
                for t in range(NT):
                    pe.wait_ge(s.onehot, NT)
                    for q in range(t + 1):
                        m = "before" if q == t else "ones"
                        last = pe.matmul(c.ps[:, 6, 256 + t * E:256 + (t + 1) * E], c.w(m), T[:, q, 4],
                                         start=(q == 0), stop=(q == t))
                    last.then_inc(s.rank_ps, 1)
                for q in range(NT):
                    last = pe.matmul(c.ps[:, 6, 384:384 + E], c.w("ones"), T[:, q, 4], start=(q == 0),
                                     stop=(q == NT - 1))
                last.then_inc(s.counts_ps, 1)
            if n == "L0f":
                for t in range(NT):
                    pe.wait_ge(s.weights_ready, t + 1)
                    pe.transpose(c.ps[0:E, 6, tok(t)], T[:, t, 3], c.w("ident")).then_inc(s.wT_ps, 1)
                pe.wait_ge(s.wT_ready, 1)
                for t in range(NT):
                    pe.matmul(c.ps[:, 7, tok(t)], wT[:, tok(t)], c.w("L0f_b2"), start=True, stop=True)\
                        .then_inc(s.rank_ps, 1)
            for e in range(E):
                if e + 1 < E:
                    up(e + 1)
                down(e)

        @block.scalar
        def _(act):
            turn_scalar(c, act, s, c.hT)

            def activate(e):
                for j in range(chunks):
                    k = e * chunks + j
                    act.wait_ge(s.up_ps, k + 1)
                    if gated:
                        if k >= 2:
                            act.wait_ge(s.hidden_ready, k - 1)
                        act.activation(act_buf(k), c.ps[0:width, k % 2], ACT.Silu).then_inc(s.activated, 1)
                    else:
                        if e >= 2:
                            act.wait_ge(s.down_ps, e - 1)
                        out = hidden(e)[:, j]
                        if n == "L0f":
                            act.activation(out, c.ps[:, k % 4], ACT.Gelu, bias=c.w("L0f_b1")[:, k:k + 1])\
                                .then_inc(s.hidden_ready, 1)
                        else:
                            act.activation(out, c.ps[:, k % 4], ACT.Gelu).then_inc(s.hidden_ready, 1)

            act.wait_ge(s.gap, 1)
            exp_in = T[:, :, 5] if n == "L1f" else T[:, :, 5, 0:1]
            act.activation(exp_in, exp_in, ACT.Exp).then_inc(s.gap_exp, 1)
            if n == "L0f":
                act.wait_ge(s.wT_ps, NT)
                act.copy(wT, c.ps[0:E, 6]).then_inc(s.wT_ready, 1)
            for e in range(E):
                activate(e)

        @block.gpsimd
        def _(g):
            c.begin(g)
            norm_gpsimd(c, g, s, 1e-5)
            if twice:
                norm_gpsimd(c, g, r, 1e-6 if gated else 1e-5, "rms" if gated else "mean")

        @block.vector
        def _(v):
            norm_vector(c, v, s, c.x, c.h)
            if twice:
                v.wait_ge(s.ready, NT)
                if gated:
                    norm_vector(c, v, r, c.h, c.hn, "rms", c.w(n + "_rms"))
                else:
                    norm_vector(c, v, r, c.h, c.hn, "mean", c.w(n + "_gamma"), c.w(n + "_beta"))
                v.tensor_tensor(c.x[:], c.x[:], c.h[:], ALU.add).then_inc(s.base, 1)
            route_vector(c, v, s, top, ps_small)
            v.wait_ge(s.index_f, 1)
            where = lambda t, k: T[:, t, 2, k:k + 1]
            if n == "L1f":
                for t in range(NT):
                    last = v.tensor_scalar(T[:, t, 5], T[:, t, 0], T[:, t, 1, 0:1], None, ALU.subtract)
                last.then_inc(s.gap, 1)
                for t in range(NT):
                    v.tensor_scalar(T[:, t, 4], c.w("expert_index"), where(t, 0), None, ALU.is_equal)\
                        .then_inc(s.onehot, 1)
                v.wait_ge(s.gap_exp, 1)
                v.tensor_reduce(T[:, :, 6, 0:1], T[:, :, 5], AX.X, ALU.add).then_inc(s.total, 1)
                v.wait_ge(s.total, 1)
                v.reciprocal(T[:, :, 6, 1:2], T[:, :, 6, 0:1]).then_inc(s.prob, 1)
                v.wait_ge(s.rank_ps, NT)
                v.wait_ge(s.counts_ps, 1)
                for t in range(NT):
                    v.tensor_tensor(T[:, t, 7], c.ps[:, 6, 256 + t * E:256 + (t + 1) * E], c.counts[:],
                                    ALU.add).then_inc(s.ranked, 1)
                    v.wait_ge(s.ranked, t + 1)
                    v.scalar_tensor_tensor(out=T[:, t, 8], in0=T[:, t, 7], scalar=float(CAPACITY),
                                           in1=T[:, t, 4], op0=ALU.is_lt, op1=ALU.mult).then_inc(s.kept, 1)
                    v.wait_ge(s.kept, t + 1)
                    if t == 0:
                        v.wait_ge(s.prob, 1)
                    v.tensor_scalar(T[:, t, 3], T[:, t, 8], T[:, t, 6, 1:2], None, ALU.mult)\
                        .then_inc(s.weights_ready, 1)
                v.wait_ge(s.ranked, NT)
                v.tensor_tensor(c.counts[:], c.counts[:], c.ps[:, 6, 384:384 + E], ALU.add)\
                    .then_inc(s.counted, 1)
            else:
                v.tensor_tensor(T[:, :, 5, 0:1], T[:, :, 1, 1:2], T[:, :, 1, 0:1], ALU.subtract)\
                    .then_inc(s.gap, 1)
                v.wait_ge(s.gap_exp, 1)
                v.tensor_scalar(T[:, :, 5, 1:2], T[:, :, 5, 0:1], 1.0, None, ALU.add)\
                    .then_inc(s.denominator, 1)
                v.wait_ge(s.denominator, 1)
                v.reciprocal(T[:, :, 5, 2:3], T[:, :, 5, 1:2]).then_inc(s.first, 1)
                v.wait_ge(s.first, 1)
                v.tensor_tensor(T[:, :, 5, 3:4], T[:, :, 5, 0:1], T[:, :, 5, 2:3], ALU.mult)\
                    .then_inc(s.second, 1)
                v.wait_ge(s.second, 1)
                for t in range(NT):
                    v.tensor_scalar(T[:, t, 4], c.w("expert_index"), where(t, 0), T[:, t, 5, 2:3],
                                    ALU.is_equal, ALU.mult)
                    v.tensor_scalar(T[:, t, 6], c.w("expert_index"), where(t, 1), T[:, t, 5, 3:4],
                                    ALU.is_equal, ALU.mult).then_inc(s.picked, 1)
                    v.wait_ge(s.picked, t + 1)
                    v.tensor_tensor(T[:, t, 3], T[:, t, 4], T[:, t, 6], ALU.add).then_inc(s.weights_ready, 1)
            v.wait_ge(s.weights_ready, NT)

            def hide(e):
                for j in range(chunks):
                    k = e * chunks + j
                    v.wait_ge(s.gate_ps, k + 1)
                    v.wait_ge(s.activated, k + 1)
                    if e >= 2:
                        v.wait_ge(s.down_ps, e - 1)
                    v.tensor_tensor(hidden(e)[:, j], act_buf(k), c.ps[0:width, 2 + k % 2], ALU.mult)\
                        .then_inc(s.hidden_ready, 1)

            if n == "L0f":
                v.wait_ge(s.rank_ps, NT)
                for t in range(NT):
                    v.tensor_tensor(c.x[:, t], c.x[:, t], c.ps[:, 7, tok(t)], ALU.add).then_inc(s.base, 1)
            if gated:
                hide(0)
            for e in range(E):
                if gated and e + 1 < E:
                    hide(e + 1)
                v.wait_ge(s.down_ps, e + 1)
                for t in range(NT):
                    if e == 0:
                        v.wait_ge(s.base, t + 1 if n == "L0f" else 1)
                    else:
                        v.wait_ge(s.added, NT * (e - 1) + t + 1)
                    v.scalar_tensor_tensor(out=c.x[:, t], in0=c.ps[:, 4 + e % 2, tok(t)],
                                           scalar=T[:, t, 3, e:e + 1], in1=c.x[:, t], op0=ALU.mult,
                                           op1=ALU.add).then_inc(s.added, 1)


def rotary_attention(c):
    nc = c.nc
    n = "L1a"
    c.turn_over()
    s = signals(c, NORM + TURN + "plain_ps turned_cols_ps by_cos by_sin rotated v_ps v_ready scores_ps "
                "scored max_ready shifted exp_ready sum_ready inv_ready probs_ready probsT_ps "
                "probsT_ready o_ps o_ready mid_ps mid_ready y_ps y_ready added")
    r = signals(c, NORM)
    w = c.big["L1_qkv"]
    CH = INNER // P
    roomq, roomk = c.room(0), c.room(1)
    sines = lambda k: c.room((2, 8)[k])
    values = lambda t: c.room((3, 7)[t % 2])
    probs, probsT, outT = c.room(4), c.room(5), c.room(6)
    cos = lambda a: a.rearrange("p (m k) -> p m k", k=S)
    banks = lambda k: c.ps[:, k:k + 2].rearrange("p b n -> p (b n)")
    with nc.Block() as block:
        @block.sync
        def _(sp):
            for m in ("L0f_w1", "L0f_w2"):
                sp.wait_ge(c.loaded[m], 16)
            for m in ("L1f_w1", "L1f_w2"):
                sp.dma_start(c.big[m][:], c.dram[m]).then_inc(c.loaded[m], 16)

        @block.tensor
        def _(pe):
            turn_tensor(c, pe, s.ready, s, c.h)
            pe.wait_ge(s.turned, NT)
            pe.wait_ge(c.loaded["L1_qkv"], 16)

            def project(t, k):
                if t > 0 or k > 0:
                    pe.wait_ge(s.by_sin, 2 * t + k)
                if t > 0:
                    pe.wait_ge(s.scored, t)
                for m in range(2):
                    for j in range(CH):
                        at = (2 * m + k) * INNER + j * P
                        last = pe.matmul(c.ps[:, 2 * m + j // 4, (j % 4) * P:(j % 4 + 1) * P],
                                         w[:, at:at + P], c.hT[:, tok(t)], start=True, stop=True)
                last.then_inc(s.plain_ps, 1)

            def project_values(t):
                if t == 1:
                    pe.wait_ge(s.v_ready, 1)
                elif t >= 2:
                    pe.wait_ge(s.probsT_ready, 2 * (t - 1))
                for b in range(2):
                    for u in range(2):
                        last = pe.matmul(c.ps[part(u), 4 + b], c.hT[:, seq(t, b)],
                                         w[:, 4 * INNER + u * 512:4 * INNER + (u + 1) * 512],
                                         start=True, stop=True)
                last.then_inc(s.v_ps, 1)

            def scores(t):
                pe.wait_ge(s.rotated, 2 * t + 2)
                for j in range(CH):
                    for a in range(2):
                        for b in range(2):
                            ch = slice(j * P + b * S, j * P + b * S + S)
                            last = pe.matmul(c.ps[part(b), a, j * S:(j + 1) * S], roomq[part(a), ch],
                                             roomk[part(a), ch], start=True, stop=True)
                last.then_inc(s.scores_ps, 1)

            def turn_probs(t):
                pe.wait_ge(s.v_ready, min(t + 2, NT))
                pe.wait_ge(s.probs_ready, t + 1)
                for k in range(2):
                    for j in range(4):
                        last = pe.transpose(c.ps[:, 4 + k, j * P:(j + 1) * P],
                                            probs[:, (4 * k + j) * P:(4 * k + j + 1) * P], c.w("ident"))
                    last.then_inc(s.probsT_ps, 1)

            def weigh_values(t):
                pe.wait_ge(s.probsT_ready, 2 * t + 2)
                if t > 0:
                    pe.wait_ge(s.y_ready, t)
                for q in range(CH):
                    u, m = q % 2, q // 2
                    for a in range(2):
                        for b in range(2):
                            last = pe.matmul(c.ps[part(a), 6 + u, m * P + b * S:m * P + b * S + S],
                                             values(t)[part(u), b * 512 + m * P + a * 64:b * 512 + m * P + a * 64 + 64],
                                             probsT[part(u), a * 512 + m * P + b * S:a * 512 + m * P + b * S + S],
                                             start=True, stop=True)
                last.then_inc(s.o_ps, 1)

            def project_out(t):
                pe.wait_ge(s.o_ready, 2 * t + 2)
                for q in range(CH):
                    last = pe.matmul(c.ps[:, 6, 0:P], c.w("L1_wo1")[:, q * P:(q + 1) * P],
                                     outT[:, (q % 2) * 512 + (q // 2) * P:(q % 2) * 512 + (q // 2 + 1) * P],
                                     start=(q == 0), stop=(q == CH - 1))
                last.then_inc(s.mid_ps, 1)
                pe.wait_ge(s.mid_ready, t + 1)
                pe.matmul(c.ps[:, 7, 0:P], c.oT[:, tok(t)], c.w("L1_wo2"), start=True, stop=True)\
                    .then_inc(s.y_ps, 1)

            for t in range(NT + 1):
                if t < NT:
                    project_values(t)
                    project(t, 0)
                if t > 0:
                    turn_probs(t - 1)
                if t < NT:
                    project(t, 1)
                if t > 0:
                    weigh_values(t - 1)
                if t < NT:
                    scores(t)
                if t > 0:
                    project_out(t - 1)

        @block.scalar
        def _(act):
            turn_scalar(c, act, s, c.hT)
            for k in range(NT + 1):
                t = k - 1
                if t >= 0:
                    act.wait_ge(s.shifted, t + 1)
                    act.activation(probs, probs, ACT.Exp, scale=WH ** -0.5).then_inc(s.exp_ready, 1)
                if k < NT:
                    act.wait_ge(s.v_ps, k + 1)
                    if k >= 2:
                        act.wait_ge(s.o_ps, k - 1)
                    act.copy(values(k), banks(4)).then_inc(s.v_ready, 1)
                if t < 0:
                    continue
                for j in range(2):
                    act.wait_ge(s.probsT_ps, 2 * t + j + 1)
                    if t > 0:
                        act.wait_ge(s.o_ps, t)
                    act.copy(probsT[:, j * 512:(j + 1) * 512], c.ps[:, 4 + j]).then_inc(s.probsT_ready, 1)
                act.wait_ge(s.o_ps, t + 1)
                if t > 0:
                    act.wait_ge(s.mid_ps, t)
                for u in range(2):
                    act.copy(outT[:, u * 512:(u + 1) * 512], c.ps[:, 6 + u]).then_inc(s.o_ready, 1)
                act.wait_ge(s.mid_ps, t + 1)
                act.activation(c.oT[:, tok(t)], c.ps[:, 6, 0:P], ACT.Relu).then_inc(s.mid_ready, 1)
                act.wait_ge(s.y_ps, t + 1)
                act.copy(c.att[:, t], c.ps[:, 7, 0:P]).then_inc(s.y_ready, 1)

        @block.gpsimd
        def _(g):
            c.begin(g)
            norm_gpsimd(c, g, s, 1e-5)
            for k in range(NT + 1):
                if k > 0:
                    g.wait_ge(s.inv_ready, k)
                    g.tensor_tensor(cos(probs), cos(probs), bcast(c.row_inv[:, k - 1], 2, S), ALU.mult)\
                        .then_inc(s.probs_ready, 1)
                if k < NT:
                    for j, room in enumerate((roomq, roomk)):
                        g.wait_ge(s.by_sin, 2 * k + j + 1)
                        g.tensor_tensor(room, room, sines(j), ALU.add).then_inc(s.rotated, 1)
            norm_gpsimd(c, g, r, 1e-5)

        @block.vector
        def _(v):
            norm_vector(c, v, s, c.x, c.h)

            def rotate(t, k):
                room = (roomq, roomk)[k]
                v.wait_ge(s.plain_ps, 2 * t + k + 1)
                if t > 0:
                    v.wait_ge(s.scores_ps, t)
                    v.wait_ge(s.rotated, 2 * (t - 1) + k + 1)
                v.tensor_tensor(cos(room), cos(banks(0)), bcast(c.w("rope_cos"), 1, 2 * CH), ALU.mult)\
                    .then_inc(s.by_cos, 1)
                v.tensor_tensor(cos(sines(k)), cos(banks(2)), bcast(c.w("rope_sin"), 1, 2 * CH), ALU.mult)\
                    .then_inc(s.by_sin, 1)

            def soften(t):
                v.wait_ge(s.scores_ps, t + 1)
                if t > 0:
                    v.wait_ge(s.probsT_ps, 2 * t)
                v.tensor_tensor(cos(probs), cos(banks(0)), bcast(c.w("causal"), 1, HEADS), ALU.add)\
                    .then_inc(s.scored, 1)
                v.wait_ge(s.scored, t + 1)
                v.tensor_reduce(c.row_max[:, t], cos(probs), AX.X, ALU.max).then_inc(s.max_ready, 1)
                v.wait_ge(s.max_ready, t + 1)
                v.tensor_tensor(cos(probs), cos(probs), bcast(c.row_max[:, t], 2, S), ALU.subtract)\
                    .then_inc(s.shifted, 1)
                v.wait_ge(s.exp_ready, t + 1)
                v.tensor_reduce(c.row_max[:, t], cos(probs), AX.X, ALU.add).then_inc(s.sum_ready, 1)
                v.wait_ge(s.sum_ready, t + 1)
                v.reciprocal(c.row_inv[:, t], c.row_max[:, t]).then_inc(s.inv_ready, 1)

            for t in range(NT + 1):
                if t > 0:
                    soften(t - 1)
                if t < NT:
                    rotate(t, 0)
                    rotate(t, 1)
            v.wait_ge(s.y_ready, NT)
            norm_vector(c, v, r, c.att, c.hn, "mean", c.w("L1_gamma"))
            v.wait_ge(r.ready, NT)
            v.tensor_tensor(c.x[:], c.x[:], c.hn[:], ALU.add).then_inc(s.added, 1)


def matrix_lstm(c):
    nc = c.nc
    c.turn_over()
    s = signals(c, NORM + TURN + "gates_ps gates_ready magnitude exp_ready log_ready floor log_f "
                "decay_ps input spread level_ps masked max_ready shifted weights_ready top floor_exp "
                "qk_ps qk_weighted sum_ready absolute least eps_added inv_ready CT_ps CT_ready o_ps normed "
                "values head_stats head_moments head_eps head_rstd centred scaled_heads gained added")
    H4, W = 4, 32
    T = lambda i: c.tiny[:, :, i, 0:H4]
    gates = c.tiny[:, :, 0]
    weights = c.room(0).rearrange("p (t h k) -> p t h k", t=NT, k=S)
    C = c.room(1).rearrange("p (t h k) -> p t h k", t=NT, k=S)
    CT = c.room(2)
    spread = c.room(3).rearrange("p (t h k) -> p t h k", t=NT, k=S)
    stats = c.room(4)[:, 0:NT * H4 * 6].rearrange("p (t h k) -> p t h k", t=NT, k=6)
    moments = c.room(4)[:, 512:512 + NT * H4 * 2].rearrange("p (t h k) -> p t h k", t=NT, k=2)
    eps = c.room(4)[:, 768:768 + NT * H4].rearrange("p (t h) -> p t h", t=NT)
    rstd = c.room(4)[:, 896:896 + NT * H4].rearrange("p (t h) -> p t h", t=NT)
    hs = c.att[:].rearrange("p t (h d) -> p t h d", d=W)
    values = c.room(5).rearrange("p (t b d) -> p t b d", t=NT, b=2)
    with nc.Block() as block:
        @block.sync
        def _(sp):
            for b in range(2):
                for u in range(2):
                    sp.dma_start(values[part(u), :, b], c.context[c.group, part(b)]).then_inc(s.values, 16)

        @block.tensor
        def _(pe):
            turn_tensor(c, pe, s.ready, s, c.h)
            for t in range(NT):
                pe.wait_ge(s.turned, t + 1)
                for m, src in enumerate((c.hT, c.ctxT, c.ctxT)):
                    last = pe.matmul(c.ps[:, 7, t * 8:t * 8 + 8], src[:, tok(t)], c.w(f"L2x_g{m}"),
                                     start=(m == 0), stop=(m == 2))
                last.then_inc(s.gates_ps, 1)
            pe.wait_ge(s.turned, NT)
            for t in range(NT):
                for h in range(H4):
                    rows = slice(W * h, W * h + W)
                    for b in range(2):
                        last = pe.matmul(c.ps[part(b), h, t * S:(t + 1) * S], c.hT[rows, seq(t, b)],
                                         c.ctxT[rows, seq(t, b)], start=True, stop=True)
            last.then_inc(s.qk_ps, 1)
            pe.wait_ge(s.log_f, 1)
            for t in range(NT):
                last = pe.matmul(c.ps[:, 7, 64 + t * 4:64 + t * 4 + 4], c.w("prefix_seq"), T(3)[:, t],
                                 start=True, stop=True)
            last.then_inc(s.decay_ps, 1)
            pe.wait_ge(s.spread, 1)
            for t in range(NT):
                last = pe.matmul(c.ps[:, 4 + t // 2, (t % 2) * 256:(t % 2 + 1) * 256], c.w("same_seq"),
                                 spread[:, t].rearrange("p h k -> p (h k)"), start=True, stop=True)
            last.then_inc(s.level_ps, 1)
            pe.wait_ge(s.qk_weighted, 1)
            pe.wait_ge(s.masked, 1)
            for t in range(NT):
                for j in range(2):
                    last = pe.transpose(c.ps[:, 4 + t // 2, (2 * (t % 2) + j) * P:(2 * (t % 2) + j + 1) * P],
                                        C[:, t, 2 * j:2 * j + 2].rearrange("p h k -> p (h k)"),
                                        c.w("ident"))
                if t % 2:
                    last.then_inc(s.CT_ps, 1)
            pe.wait_ge(s.CT_ready, 2)
            pe.wait_ge(s.values, 4 * 16)
            for t in range(NT):
                for b in range(2):
                    for h in range(H4):
                        at = (2 * t + h // 2) * P + b * S
                        last = pe.matmul(c.ps[part(b), h % 2, t * P + h * W:t * P + h * W + W],
                                         CT[part(h % 2), at:at + S],
                                         values[part(h % 2), t, b, h * W:h * W + W],
                                         start=True, stop=True)
            last.then_inc(s.o_ps, 1)

        @block.scalar
        def _(act):
            turn_scalar(c, act, s, c.hT)
            act.wait_ge(s.magnitude, 1)
            act.activation(T(1), T(1), ACT.Exp).then_inc(s.exp_ready, 1)
            act.wait_ge(s.exp_ready, 1)
            act.activation(T(1), T(1), ACT.Ln, bias=1.0).then_inc(s.log_ready, 1)
            act.wait_ge(s.shifted, 1)
            act.activation(weights, weights, ACT.Exp).then_inc(s.weights_ready, 1)
            act.wait_ge(s.top, 1)
            act.activation(T(7), T(6), ACT.Exp, scale=-1.0).then_inc(s.floor_exp, 1)
            for k in range(2):
                act.wait_ge(s.CT_ps, k + 1)
                act.copy(CT[:, k * 512:(k + 1) * 512], c.ps[:, 4 + k]).then_inc(s.CT_ready, 1)

        @block.gpsimd
        def _(g):
            c.begin(g)
            norm_gpsimd(c, g, s, 1e-5)
            g.wait_ge(s.head_moments, NT * H4)
            g.tensor_scalar(eps, moments[:, :, :, 1], 1e-6, None, ALU.add).then_inc(s.head_eps, 1)
            g.wait_ge(s.head_eps, 1)
            g.tensor_tensor(rstd, eps, c.minus_half[:, 0:NT * H4].rearrange("p (t h) -> p t h", t=NT),
                            ALU.pow).then_inc(s.head_rstd, 1)

        @block.vector
        def _(v):
            norm_vector(c, v, s, c.x, c.h)
            v.wait_ge(s.gates_ps, NT)
            v.tensor_tensor(gates, c.ps[:, 7, 0:32].rearrange("p (t n) -> p t n", t=NT),
                            bcast(c.w("L2x_gb"), 1, NT), ALU.add).then_inc(s.gates_ready, 1)
            v.wait_ge(s.gates_ready, 1)
            forget, enter = gates[:, :, 4:8], gates[:, :, 0:4]
            v.scalar_tensor_tensor(out=T(1), in0=forget, scalar=-1.0, in1=forget, op0=ALU.mult, op1=ALU.min)\
                .then_inc(s.magnitude, 1)
            v.tensor_scalar(T(2), forget, 0.0, None, ALU.min).then_inc(s.floor, 1)
            v.wait_ge(s.floor, 1)
            v.wait_ge(s.log_ready, 1)
            v.tensor_tensor(T(3), T(2), T(1), ALU.subtract).then_inc(s.log_f, 1)
            v.wait_ge(s.decay_ps, 1)
            decay_ps = c.ps[:, 7, 64:80].rearrange("p (t h) -> p t h", t=NT)
            v.tensor_tensor(T(4), enter, decay_ps, ALU.subtract).then_inc(s.input, 1)
            v.wait_ge(s.input, 1)
            for t in range(NT):
                last = v.tensor_tensor(spread[:, t], bcast(T(4)[:, t], 2, S), bcast(c.w("pos_onehot"), 1, H4),
                                       ALU.mult)
            last.then_inc(s.spread, 1)
            v.wait_ge(s.level_ps, 1)
            for t in range(NT):
                last = v.tensor_tensor(weights[:, t], c.ps[:, 4 + t // 2, (t % 2) * 256:(t % 2 + 1) * 256]
                                       .rearrange("p (h k) -> p h k", k=S), bcast(c.w("causal"), 1, H4), ALU.add)
            last.then_inc(s.masked, 1)
            v.wait_ge(s.masked, 1)
            v.tensor_reduce(T(5), weights, AX.X, ALU.max).then_inc(s.max_ready, 1)
            v.wait_ge(s.max_ready, 1)
            for t in range(NT):
                last = v.tensor_tensor(weights[:, t], weights[:, t], bcast(T(5)[:, t], 2, S), ALU.subtract)
            last.then_inc(s.shifted, 1)
            v.tensor_tensor(T(6), T(5), decay_ps, ALU.add).then_inc(s.top, 1)
            v.wait_ge(s.weights_ready, 1)
            v.wait_ge(s.qk_ps, 1)
            for t in range(NT):
                last = v.scalar_tensor_tensor(out=C[:, t], in0=c.ps[:, 0:4, t * S:(t + 1) * S],
                                              scalar=W ** -0.5, in1=weights[:, t], op0=ALU.mult, op1=ALU.mult)
            last.then_inc(s.qk_weighted, 1)
            v.wait_ge(s.qk_weighted, 1)
            v.tensor_reduce(T(8), C, AX.X, ALU.add).then_inc(s.sum_ready, 1)
            v.wait_ge(s.sum_ready, 1)
            v.scalar_tensor_tensor(out=T(9), in0=T(8), scalar=-1.0, in1=T(8), op0=ALU.mult, op1=ALU.max)\
                .then_inc(s.absolute, 1)
            v.wait_ge(s.absolute, 1)
            v.wait_ge(s.floor_exp, 1)
            v.tensor_tensor(T(12), T(9), T(7), ALU.max).then_inc(s.least, 1)
            v.wait_ge(s.least, 1)
            v.tensor_scalar(T(10), T(12), 1e-6, None, ALU.add).then_inc(s.eps_added, 1)
            v.wait_ge(s.eps_added, 1)
            v.reciprocal(T(11), T(10)).then_inc(s.inv_ready, 1)
            v.wait_ge(s.inv_ready, 1)
            v.wait_ge(s.o_ps, 1)
            for t in range(NT):
                for u in range(2):
                    last = v.tensor_tensor(hs[:, t, u::2], c.ps[:, u, tok(t)]
                                           .rearrange("p (h d) -> p h d", d=W)[:, u::2],
                                           bcast(T(11)[:, t, u::2], 2, W), ALU.mult)
            last.then_inc(s.normed, 1)
            v.wait_ge(s.normed, 1)
            for t in range(NT):
                for h in range(H4):
                    v.bn_stats(stats[:, t, h], hs[:, t, h]).then_inc(s.head_stats, 1)
            for t in range(NT):
                for h in range(H4):
                    v.wait_ge(s.head_stats, t * H4 + h + 1)
                    v.bn_aggr(moments[:, t, h], stats[:, t, h]).then_inc(s.head_moments, 1)
            v.wait_ge(s.head_moments, NT * H4)
            for t in range(NT):
                last = v.tensor_tensor(hs[:, t], hs[:, t], bcast(moments[:, t, :, 0], 2, W), ALU.subtract)
            last.then_inc(s.centred, 1)
            v.wait_ge(s.centred, 1)
            v.wait_ge(s.head_rstd, 1)
            for t in range(NT):
                last = v.tensor_tensor(hs[:, t], hs[:, t], bcast(rstd[:, t], 2, W), ALU.mult)
            last.then_inc(s.scaled_heads, 1)
            v.wait_ge(s.scaled_heads, 1)
            v.tensor_tensor(c.att[:], c.att[:], bcast(c.w("L2x_on"), 1, NT), ALU.mult).then_inc(s.gained, 1)
            v.wait_ge(s.gained, 1)
            v.tensor_tensor(c.x[:], c.x[:], c.att[:], ALU.add).then_inc(s.added, 1)


def gated_mlp(c):
    nc = c.nc
    c.turn_over()
    s = signals(c, NORM + TURN + "logits_ps logits_ready top_ready less_max exps total inv prob "
                "two eps_added eps_inv factor up_ps hidden_ready down_ps y_ready added")
    T = c.tiny
    hidden = c.room(0, 2).rearrange("p (c n) -> p c n", c=HC)
    with nc.Block() as block:
        @block.tensor
        def _(pe):
            turn_tensor(c, pe, s.ready, s, c.hn)
            for t in range(NT):
                pe.wait_ge(s.turned, t + 1)
                pe.matmul(c.ps[:, 7, t * E:(t + 1) * E], c.hT[:, tok(t)], c.w("L3f_gate"), start=True,
                          stop=True).then_inc(s.logits_ps, 1)
            for j in range(HC):
                pe.matmul(c.ps[:, j], c.w("L3f_up")[:, j * P:(j + 1) * P], c.hT[:], start=True,
                          stop=True).then_inc(s.up_ps, 1)
            pe.wait_ge(s.hidden_ready, HC)
            for t in range(NT):
                for j in range(HC):
                    last = pe.matmul(c.ps[:, 4, tok(t)], hidden[:, j, tok(t)],
                                     c.w("L3f_down")[:, j * D:(j + 1) * D], start=(j == 0), stop=(j == HC - 1))
                last.then_inc(s.down_ps, 1)

        @block.scalar
        def _(act):
            turn_scalar(c, act, s, c.hT)
            act.wait_ge(s.less_max, 1)
            act.activation(T[:, :, 2], T[:, :, 2], ACT.Exp).then_inc(s.exps, 1)
            for j in range(HC):
                act.wait_ge(s.up_ps, j + 1)
                act.activation(hidden[:, j], c.ps[:, j], ACT.Silu).then_inc(s.hidden_ready, 1)

        @block.gpsimd
        def _(g):
            c.begin(g)
            norm_gpsimd(c, g, s, 1e-6, "rms")

        @block.vector
        def _(v):
            norm_vector(c, v, s, c.h, c.hn, "rms", c.w("L3f_n2"))
            v.wait_ge(s.logits_ps, NT)
            for t in range(NT):
                v.tensor_copy(T[:, t, 0], c.ps[:, 7, t * E:(t + 1) * E]).then_inc(s.logits_ready, 1)
                v.wait_ge(s.logits_ready, t + 1)
                v.max(T[:, t, 1], T[:, t, 0]).then_inc(s.top_ready, 1)
                v.wait_ge(s.top_ready, t + 1)
                last = v.tensor_scalar(T[:, t, 2], T[:, t, 1], T[:, t, 1, 0:1], None, ALU.subtract)
            last.then_inc(s.less_max, 1)
            v.wait_ge(s.exps, 1)
            v.tensor_reduce(T[:, :, 3, 0:1], T[:, :, 2], AX.X, ALU.add).then_inc(s.total, 1)
            v.tensor_reduce(T[:, :, 3, 1:2], T[:, :, 2, 0:2], AX.X, ALU.add).then_inc(s.two, 1)
            v.wait_ge(s.total, 1)
            v.reciprocal(T[:, :, 3, 2:3], T[:, :, 3, 0:1]).then_inc(s.inv, 1)
            v.wait_ge(s.inv, 1)
            v.wait_ge(s.two, 1)
            v.tensor_tensor(T[:, :, 3, 3:4], T[:, :, 3, 1:2], T[:, :, 3, 2:3], ALU.mult).then_inc(s.prob, 1)
            v.wait_ge(s.prob, 1)
            v.tensor_scalar(T[:, :, 3, 4:5], T[:, :, 3, 3:4], 1e-9, None, ALU.add).then_inc(s.eps_added, 1)
            v.wait_ge(s.eps_added, 1)
            v.reciprocal(T[:, :, 3, 5:6], T[:, :, 3, 4:5]).then_inc(s.eps_inv, 1)
            v.wait_ge(s.eps_inv, 1)
            v.tensor_tensor(T[:, :, 3, 6:7], T[:, :, 3, 3:4], T[:, :, 3, 5:6], ALU.mult).then_inc(s.factor, 1)
            v.wait_ge(s.factor, 1)
            v.wait_ge(s.down_ps, NT)
            for t in range(NT):
                v.scalar_tensor_tensor(out=c.h[:, t], in0=c.ps[:, 4, tok(t)], scalar=T[:, t, 3, 6:7],
                                       in1=c.h[:, t], op0=ALU.mult, op1=ALU.add).then_inc(s.y_ready, 1)
            v.wait_ge(s.y_ready, NT)
            v.tensor_tensor(c.x[:], c.x[:], c.h[:], ALU.add).then_inc(s.added, 1)


def prepare(c, dram_small, dram_big):
    nc = c.nc
    c.half = 1
    s = signals(c, "small constants tables_ps maps_ps maps")
    with nc.Block() as block:
        @block.sync
        def _(sp):
            sp.dma_start(c.small[:], dram_small).then_inc(s.small, 16)
            for n in ("L1_qkv", "L2f_w1", "L2f_w3", "L2f_w2"):
                sp.dma_start(c.big[n][:], dram_big[n]).then_inc(c.loaded[n], 16)

        @block.gpsimd
        def _(g):
            g.memset(c.minus_half[:], -0.5).then_inc(s.constants, 1)
            g.memset(c.counts[:], 0.0).then_inc(s.constants, 1)
            g.memset(c.vx[:].rearrange("p t b j n -> p (t b j n)"), 0.0).then_inc(s.constants, 1)
            g.wait_ge(s.constants, 3)
            for u in range(2):
                g.memset(c.vx[part(u)].rearrange("p t b j n -> p (t b j) n")[:, :, u * 9 + HD], 1.0)\
                    .then_inc(s.constants, 1)

        @block.tensor
        def _(pe):
            pe.wait_ge(s.small, 16)
            for k in range(S):
                for b in range(2):
                    last = pe.matmul(c.ps[part(b), k // 16, (k % 16) * 32:(k % 16) * 32 + 17],
                                     c.w("distance_onehot")[:, 63 - k:127 - k], c.w("distance_table"),
                                     start=True, stop=True)
            last.then_inc(s.tables_ps, 1)
            for i, (a, b) in enumerate((("dq", "uq"), ("dkv", "uk"), ("kr", "qr"), ("dkv", "uv"))):
                last = pe.matmul(c.ps[:, 4, i * P:(i + 1) * P], c.w("L2a_" + a), c.w("L2a_" + b),
                                 start=True, stop=True)
            last.then_inc(s.maps_ps, 1)

        @block.vector
        def _(v):
            v.wait_ge(s.tables_ps, 1)
            table = c.ps[:, 0:4].rearrange("p b (k n) -> p b k n", n=32)
            by_head = c.bias0[:].rearrange("p (h k) -> p h k", k=S)
            for q in range(4):
                v.tensor_copy(by_head[:, :, q * 16:(q + 1) * 16].rearrange("p h k -> p k h"),
                              table[:, q, :, 0:HEADS])
                v.tensor_copy(c.decay3[:, q * 16:(q + 1) * 16], table[:, q, :, HEADS])
            v.wait_ge(s.maps_ps, 1)
            for i in range(3):
                v.tensor_tensor(c.q_of_h[:, i * D:(i + 1) * D], c.ps[:, 4, i * P:(i + 1) * P],
                                c.w("head_block"), ALU.mult)
            v.tensor_tensor(c.v_of_h[:], c.ps[:, 4, 3 * P:4 * P], c.w("head_block_pairs"), ALU.mult)\
                .then_inc(s.maps, 1)


def load_group(c, x_dram, ctx_dram, big_dram, i):
    nc = c.nc
    c.turn_over()
    s = signals(c, "x ctx ctxT_ps ctxT")
    with nc.Block() as block:
        @block.sync
        def _(sp):
            sp.dma_start(c.x[:], x_dram[i]).then_inc(s.x, 16)
            sp.dma_start(c.ctx_tok[:], ctx_dram[i]).then_inc(s.ctx, 16)
            sp.dma_start(c.big["L0f_w1"][:], big_dram["L0f_w1"]).then_inc(c.loaded["L0f_w1"], 16)
            sp.dma_start(c.big["L0f_w2"][:], big_dram["L0f_w2"]).then_inc(c.loaded["L0f_w2"], 16)
            sp.wait_ge(s.x, 16)
            sp.wait_ge(s.ctx, 16)

        @block.tensor
        def _(pe):
            pe.wait_ge(s.ctx, 16)
            for t in range(NT):
                pe.transpose(c.ps[:, 0, tok(t)], c.ctx_tok[:, t], c.w("ident")).then_inc(s.ctxT_ps, 1)

        @block.scalar
        def _(act):
            act.wait_ge(s.ctxT_ps, NT)
            act.copy(c.ctxT[:], c.ps[:, 0]).then_inc(s.ctxT, 1)

        @block.gpsimd
        def _(g):
            c.begin(g)


def store_group(c, out_dram, i):
    nc = c.nc
    c.turn_over()
    s = signals(c, "out")
    with nc.Block() as block:
        @block.sync
        def _(sp):
            sp.dma_start(out_dram[i], c.x[:]).then_inc(s.out, 16)
            sp.wait_ge(s.out, 16)

        @block.gpsimd
        def _(g):
            c.begin(g)


def end_group(c):
    c.turn_over()
    with c.nc.Block() as block:
        @block.gpsimd
        def _(g):
            c.begin(g)
            for s in c.per_group:
                g.sem_clear(s)


STAGES = {
    "L0a": lambda c: attention(c, "L0a", mode="bias", q_scale=HD ** -0.5, bias=True, out_bias=True),
    "L0x": channel_attention,
    "L0f": lambda c: experts(c, "L0f", 2, False),
    "L1a": rotary_attention,
    "L1x": lambda c: attention(c, "L1x", "ctx", exp_scale=HD ** -0.5),
    "L1f": lambda c: experts(c, "L1f", 1, False),
    "L2a": lambda c: attention(c, "L2a", mode="latent", exp_scale=HD ** -0.5),
    "L2x": matrix_lstm,
    "L2f": lambda c: experts(c, "L2f", 2, True),
    "L3a": lambda c: attention(c, "L3a", mode="decay", exp_scale=HD ** -0.5, out_bias=True),
    "L3x": lambda c: attention(c, "L3x", "ctx", mode="sparse", q_scale=HD ** -0.5, bias=True, out_bias=True),
    "L3f": lambda c: (attention(c, "L3f", mode="causal", exp_scale=HD ** -0.5, rms=True), gated_mlp(c)),
}


def decoder(nc, x, context, small, big, out, where, stages=tuple(STAGES), groups=NG):
    with ExitStack() as ctx:
        c = Core(nc, ctx, where, {n: a.shape for n, a in big.items()})
        c.dram = big
        c.loaded = {n: ctx.enter_context(nc.semaphore("loaded_" + n)) for n in big}
        c.per_group = [s for n, s in c.loaded.items() if n[:3] in ("L0f", "L1f")]
        prepare(c, small, big)
        with nc.Fori(0, groups) as i:
            c.group, c.context = i, context
            load_group(c, x, context, big, i)
            for n in stages:
                STAGES[n](c)
            store_group(c, out, i)
            end_group(c)
            if c.half == 0:
                end_group(c)


def kernel(**inputs):
    import concourse.bacc as bacc
    from concourse.bass_utils import run_bass_kernel_spmd

    i = {n: np.asarray(a) for n, a in inputs.items()}
    small, big = lay_out(i)
    packed, where = pack(small)
    grouped = lambda a: np.ascontiguousarray(a.reshape(NG, NT, P, D).transpose(0, 2, 1, 3))
    arrays = {"x_in": grouped(i["x"]), "ctx_in": grouped(i["ctx_1024"]), "small_in": packed}
    arrays.update({n + "_in": np.ascontiguousarray(a) for n, a in big.items()})
    nc = bacc.Bacc("TRN2", target_bir_lowering=False, num_devices=1)
    dram = {n: nc.dram_tensor(n, a.shape, F32, kind="ExternalInput").ap() for n, a in arrays.items()}
    out = nc.dram_tensor("out", (NG, P, NT, D), F32, kind="ExternalOutput").ap()
    decoder(nc, dram["x_in"], dram["ctx_in"], dram["small_in"], {n: dram[n + "_in"] for n in big}, out, where)
    got = run_bass_kernel_spmd(nc, [arrays], core_ids=[0]).results[0]["out"]
    return np.ascontiguousarray(np.asarray(got).transpose(0, 2, 1, 3)).reshape(B, S, D)
```

```python
from collections import namedtuple
from contextlib import ExitStack

import numpy as np

import concourse.bass as bass
from concourse import mybir

F32 = mybir.dt.float32
ALU = mybir.AluOpType
ACT = mybir.ActivationFunctionType
AX = mybir.AxisListType

P = 128
D = 128
B, S = 32, 64
NT = 8
HT = 4
GROUP = NT * P
NG = B * S // GROUP
HEADS, HD = 16, 8
E = 8
HID = 512
HC = HID // P
I2W, I2C = 448, 4
IC = I2W // I2C
INNER, WH = 1024, 64
XR = 33
CAPACITY = 2 * 1024 // E
SIGNALS = 64
TOP = 8
SORT_STEPS = 21
BIG = 1.0e30


def shape_constants():
    p = np.arange(P)
    q = p % S
    k = np.arange(S)
    out = {}
    out["ident"] = np.eye(P)
    out["head_of_row"] = (p[:, None] % 64 // HD == np.arange(HEADS // 2)[None]) * 1.0
    out["causal"] = np.where(k[None, :] <= q[:, None], 0.0, -BIG)
    out["head_block"] = (p[:, None] // HD == p[None, :] // HD) * 1.0
    pair, col = p // 64, p % 64
    out["head_block_pairs"] = (p[:, None] // HD == (2 * (col // HD) + pair)[None, :]) * 1.0
    m = np.arange(127)
    dist = np.clip(63 - m, -16, 16) + 16
    out["distance_onehot"] = np.pad((np.arange(XR)[:, None] == dist[None]) * 1.0, ((0, 0), (0, 1)))
    out["ones"] = np.ones((P, P))
    out["same_seq"] = (p[:, None] // S == p[None] // S) * 1.0
    out["prefix_seq"] = ((p[:, None] // S == p[None] // S) & (p[:, None] <= p[None])) * 1.0
    out["before"] = (p[:, None] < p[None]) * 1.0
    out["pos_onehot"] = (q[:, None] == k[None]) * 1.0
    out["block32"] = (p[:, None] // 32 == np.arange(4)[None]) * 1.0
    d = np.arange(P) % WH % 32
    inv = (1.0 / np.float32(10000.0) ** (2 * d.astype(np.float32) / np.float32(WH))).astype(np.float32)
    freq = (np.arange(S, dtype=np.float32)[None, :] * inv[:, None]).astype(np.float32)
    out["rope_cos"] = np.cos(freq)
    out["rope_sin"] = np.sin(freq) * np.where(np.arange(P) % WH < 32, -1.0, 1.0)[:, None]
    out["expert_index"] = np.tile(np.arange(E, dtype=np.float32)[None], (P, 1))
    out["inverse_rank"] = np.broadcast_to(1.0 / np.arange(1, S + 1), (P, S))
    return {n: np.asarray(a, np.float32) for n, a in out.items()}


def pair_columns(w):
    return w.reshape(w.shape[0], HEADS // 2, 2, HD).transpose(0, 2, 1, 3).reshape(w.shape[0], D)


def column(v):
    return v.reshape(-1, 1)


def halves(v):
    return np.tile(v.reshape(2, 64).T, (2, 1))


def row(v):
    return np.broadcast_to(v.reshape(1, -1), (P, v.size))


def blocks(w, per):
    return w.reshape(-1, per, w.shape[-1]).transpose(1, 0, 2).reshape(per, -1)


def lay_out(i):
    small, big = dict(shape_constants()), {}
    rel = np.clip(np.arange(XR) - 16, -15, 15) + 15
    small["distance_table"] = np.concatenate(
        [i["L0_attn_rel_bias"][rel], i["L3_attn_rel_emb"][np.abs(np.arange(XR) - 16)][:, None]], 1)

    def attention(name, wq, wk, wv, wo):
        small[name + "_wq"], small[name + "_wk"] = wq, wk
        small[name + "_wv"], small[name + "_wo"] = pair_columns(wv), wo

    a = "L0_attn_"
    attention("L0a", i[a + "Wq"].T, i[a + "Wk"].T, i[a + "Wv"].T, i[a + "Wo"].T)
    small["L0a_bq"], small["L0a_bk"] = halves(i[a + "bq"]), halves(i[a + "bk"])
    small["L0a_bv"] = column(i[a + "bv"])
    small["L0a_bo"] = row(i[a + "bo"])
    a = "L0_xattn_"
    for s in "gl":
        small["L0x_wq" + s], small["L0x_bq" + s] = row(i[a + "wq" + s]), row(i[a + "bq" + s])
        small["L0x_wk" + s], small["L0x_bk" + s] = row(i[a + "wk" + s]), row(i[a + "bk" + s])
        small["L0x_wv" + s], small["L0x_bv" + s] = column(i[a + "wv" + s]), column(i[a + "bv" + s])
    small["L0x_wp"], small["L0x_bp"] = row(i[a + "wp"]), row(i[a + "bp"])
    small["L0f_wr"] = i["L0_ffn_Wr"]
    small["L0f_b1"] = i["L0_ffn_b1"].reshape(E * HC, P).T
    small["L0f_b2"] = i["L0_ffn_b2"]
    small["L1_wo1"] = blocks(i["L1_attn_W_o1"], P)
    small["L1_wo2"] = i["L1_attn_W_o2"]
    small["L1_gamma"] = row(i["L1_attn_gamma"])
    a = "L1_xattn_W_"
    attention("L1x", i[a + "q"].T, i[a + "k"].T, i[a + "v"].T, i[a + "o"].T)
    small["L1f_gate"] = i["L1_ffn_gate_weight"].T
    small["L1f_gamma"], small["L1f_beta"] = row(i["L1_ffn_ln_gamma"]), row(i["L1_ffn_ln_beta"])
    a = "L2_attn_W_"
    tile16 = lambda w: np.tile(w, (1, HEADS))
    small["L2a_dq"], small["L2a_uq"] = tile16(i[a + "DQ"]), tile16(i[a + "UQ"].T)
    small["L2a_dkv"] = tile16(i[a + "DKV"])
    small["L2a_uk"], small["L2a_uv"] = tile16(i[a + "UKV"][:HD].T), tile16(i[a + "UKV"][HD:].T)
    small["L2a_kr"], small["L2a_qr"] = tile16(i[a + "KR"]), tile16(i[a + "QR"])
    wo = np.zeros((D, D), np.float32)
    for h in range(HEADS):
        wo[h * HD:(h + 1) * HD, h * HD:(h + 1) * HD] = i[a + "O"].T
    small["L2a_wo"] = wo
    small["L2a_qn"] = column(np.tile(i["L2_attn_q_norm_w"], HEADS))
    small["L2a_kn"] = row(np.tile(i["L2_attn_k_norm_w"], HEADS))
    a = "L2_xattn_"
    for n in range(3):
        small[f"L2x_g{n}"] = np.concatenate(
            [i[a + "igate_kernel"][n * D:(n + 1) * D], i[a + "fgate_kernel"][n * D:(n + 1) * D]], 1)
    small["L2x_gb"] = row(np.concatenate([i[a + "igate_bias"], i[a + "fgate_bias"]]))
    small["L2x_on"] = row(i[a + "outnorm_scale"])
    small["L2f_rms"], small["L2f_gate"] = row(i["L2_ffn_rms_weight"]), i["L2_ffn_gate_w"].T
    a = "L3_attn_"
    attention("L3a", i[a + "Wq"], i[a + "Wk"], i[a + "Wv"], i[a + "Wo"])
    small["L3a_bo"] = row(i[a + "bo"])
    a = "L3_xattn_"
    attention("L3x", i[a + "Wq"], i[a + "Wk"], i[a + "Wv"], i[a + "Wo"])
    small["L3x_bq"], small["L3x_bk"] = halves(i[a + "bq"]), halves(i[a + "bk"])
    small["L3x_bv"] = column(i[a + "bv"])
    small["L3x_bo"] = row(i[a + "bo"])
    a = "L3_ffn_"
    w = i[a + "qkv_w"].T
    attention("L3f", w[:, :D], w[:, D:2 * D], w[:, 2 * D:], i[a + "o_w"].T)
    small["L3f_n1"], small["L3f_n2"] = row(i[a + "n1_w"]), row(i[a + "n2_w"])
    small["L3f_gate"], small["L3f_up"] = i[a + "gate_w"].T, i[a + "up_w"].T
    small["L3f_down"] = blocks(i[a + "down_w"].T, P)

    big["L0f_w1"] = np.ascontiguousarray(i["L0_ffn_W1"].transpose(1, 0, 2)).reshape(P, -1)
    big["L0f_w2"] = blocks(i["L0_ffn_W2"].reshape(-1, D), P)
    w = i["L1_attn_W_qkv"]
    turned = w[:, :2 * INNER].reshape(D, 2 * HEADS, 2, 32)[:, :, ::-1].reshape(D, 2 * INNER)
    v = w[:, 2 * INNER:].reshape(D, HEADS // 4, 2, 2, WH).transpose(0, 2, 1, 3, 4).reshape(D, INNER)
    big["L1_qkv"] = np.concatenate([w[:, :2 * INNER], turned, v], 1)
    big["L1f_w1"] = np.ascontiguousarray(i["L1_ffn_wi"].transpose(1, 0, 2)).reshape(P, -1)
    big["L1f_w2"] = blocks(i["L1_ffn_wo"].reshape(-1, D), P)
    big["L2f_w1"] = np.ascontiguousarray(i["L2_ffn_w1"].transpose(2, 0, 1)).reshape(P, -1)
    big["L2f_w3"] = np.ascontiguousarray(i["L2_ffn_w3"].transpose(2, 0, 1)).reshape(P, -1)
    big["L2f_w2"] = blocks(np.ascontiguousarray(i["L2_ffn_w2"].transpose(0, 2, 1)).reshape(-1, D), IC)
    return small, big


def pack(arrays):
    at, where, parts = 0, {}, []
    for name, a in arrays.items():
        where[name] = (at, a.shape[1], a.shape[0])
        parts.append(np.pad(a, ((0, P - a.shape[0]), (0, 0))))
        at += a.shape[1]
    return np.ascontiguousarray(np.concatenate(parts, 1)), where


def signals(core, names):
    words = names.split()
    turns = core.turns
    first = turns.taken
    turns.taken += len(words)
    return namedtuple("Signals", words)(*core.halves[turns.half][first:turns.taken])


class Turns:
    half, taken = 1, 0


class Core:

    def __init__(self, nc, ctx, where, big):
        self.nc, self.ctx, self.where = nc, ctx, where
        self.halves = [[ctx.enter_context(nc.semaphore(f"signal_{h}_{i}")) for i in range(SIGNALS)]
                       for h in range(2)]
        self.turns = Turns()
        self.small = self.buf("small", [P, max(a + n for a, n, _ in where.values())])
        self.big = {"L1_qkv": self.buf("L1_qkv", big["L1_qkv"])}
        layers = [[n for n in big if n[:3] == layer] for layer in ("L0f", "L1f", "L2f")]
        place = self.buf("experts_weights", [P, max(sum(big[n][1] for n in layer) for layer in layers)])
        for layer in layers:
            at = 0
            for n in layer:
                rows, cols = big[n]
                self.big[n] = place[0:rows, at:at + cols]
                at += cols
        self.nt, self.own_tiles = NT, slice(0, NT)
        self.x = self.buf("x", [P, NT, D])
        self.h = self.buf("h", [P, NT, D])
        self.hn = self.buf("hn", [P, NT, D])
        self.hT = self.buf("hT", [P, GROUP])
        self.ctx_tok = self.buf("ctx_tok", [P, NT, D])
        self.ctxT = self.buf("ctxT", [P, GROUP])
        self.q_apart = self.buf("q_apart", [P, NT, 2, 2, S])
        self.scaled_bias = self.buf("scaled_bias", [P, 2])
        self.oT = self.buf("oT", [P, GROUP])
        self.att = self.buf("att", [P, NT, D])
        self.stats = self.buf("stats_buf", [P, NT, 6])
        self.moments = self.buf("moments_buf", [P, NT, 2])
        self.var_eps = self.buf("var_eps_buf", [P, NT])
        self.rstd = self.buf("rstd_buf", [P, NT])
        self.row_max = self.buf("row_max", [P, NT, HEADS])
        self.row_inv = self.buf("row_inv", [P, NT, HEADS])
        self.bias0 = self.buf("bias0", [P, HEADS * S])
        self.decay3 = self.buf("decay3", [P, S])
        self.vx = self.buf("vx", [P, NT, 2, HEADS // 2, 2 * (HD + 1)])
        self.minus_half = self.buf("minus_half", [P, 2 * HEADS])
        self.q_of_h = self.buf("q_of_h", [P, 3 * D])
        self.v_of_h = self.buf("v_of_h", [P, D])
        self.counts = self.buf("counts", [P, E])
        self.tiny = self.buf("tiny", [P, NT, 16, E])
        self.row_open = self.buf("row_open", [P, 1])
        self.count_open = self.ctx.enter_context(nc.sbuf_tensor("count_open", [1, 1], mybir.dt.int32))
        self.index = self.ctx.enter_context(nc.sbuf_tensor("index", [P, NT, E], mybir.dt.uint32))
        self.arena = self.buf("arena", [P, 9 * HEADS * S])
        self.ps = ctx.enter_context(nc.psum_tensor("ps", [P, 8, 512], F32))

    def turn_over(self):
        self.turns.half, self.turns.taken = 1 - self.turns.half, 0

    def begin(self, g):
        last = self.halves[1 - self.turns.half]
        g.sem_clear(range(last[0].num, last[-1].num + 1))

    def buf(self, name, shape):
        return self.ctx.enter_context(self.nc.sbuf_tensor(name, shape, F32))

    def w(self, name):
        at, n, rows = self.where[name]
        return self.small[0:rows, at:at + n]

    def room(self, k, n=1):
        return self.arena[:, k * 1024:(k + n) * 1024]


class SomeTiles(Core):

    def __init__(self, c, first, end):
        own, columns = slice(first, end), slice(first * P, end * P)
        self.nt, self.own_tiles = end - first, own
        self.nc, self.where, self.small, self.big, self.ps = c.nc, c.where, c.small, c.big, c.ps
        self.halves, self.turns, self.loaded = c.halves, c.turns, c.loaded
        self.group, self.context, self.arena = c.group, c.context, c.arena
        self.bias0, self.decay3, self.minus_half, self.counts = c.bias0, c.decay3, c.minus_half, c.counts
        self.scaled_bias, self.row_open, self.count_open = c.scaled_bias, c.row_open, c.count_open
        self.x, self.h, self.hn, self.att = c.x[:, own], c.h[:, own], c.hn[:, own], c.att[:, own]
        self.ctx_tok, self.vx, self.q_apart = c.ctx_tok[:, own], c.vx[:, own], c.q_apart[:, own]
        self.hT, self.ctxT, self.oT = c.hT[:, columns], c.ctxT[:, columns], c.oT[:, columns]
        self.stats, self.moments = c.stats[:, own], c.moments[:, own]
        self.var_eps, self.rstd = c.var_eps[:, own], c.rstd[:, own]
        self.row_max, self.row_inv = c.row_max[:, own], c.row_inv[:, own]
        self.tiny, self.index = c.tiny[:, own], c.index[:, own]


def bcast(ap, dim, n):
    ap = ap.unsqueeze(dim)
    shape = list(ap.shape)
    shape[dim] = n
    return ap.to_broadcast(shape)


def tok(t):
    return slice(t * P, (t + 1) * P)


def seq(t, b):
    return slice(t * P + b * S, t * P + (b + 1) * S)


def part(b):
    return slice(b * 64, (b + 1) * 64)


NORM = "stats moments square var_eps rstd scaled weighted ready "


def norm_vector(c, v, s, src, dst, kind="mean", weight=None, shift=None):
    for t in range(c.nt):
        v.bn_stats(c.stats[:, t], src[:, t]).then_inc(s.stats, 1)
    for t in range(c.nt):
        v.wait_ge(s.stats, t + 1)
        v.bn_aggr(c.moments[:, t], c.stats[:, t]).then_inc(s.moments, 1)
    v.wait_ge(s.moments, c.nt)
    v.wait_ge(s.rstd, 1)
    for t in range(c.nt):
        if kind == "rms":
            v.scalar_tensor_tensor(out=dst[:, t], in0=src[:, t], scalar=c.rstd[:, t:t + 1], in1=weight,
                                   op0=ALU.mult, op1=ALU.mult).then_inc(s.ready, 1)
            continue
        v.tensor_scalar(dst[:, t], src[:, t], c.moments[:, t, 0:1], c.rstd[:, t:t + 1],
                        ALU.subtract, ALU.mult).then_inc(s.ready if weight is None else s.scaled, 1)
        if weight is not None:
            v.wait_ge(s.scaled, t + 1)
            v.tensor_tensor(dst[:, t], dst[:, t], weight, ALU.mult)\
                .then_inc(s.ready if shift is None else s.weighted, 1)
        if shift is not None:
            v.wait_ge(s.weighted, t + 1)
            v.tensor_tensor(dst[:, t], dst[:, t], shift, ALU.add).then_inc(s.ready, 1)


def norm_gpsimd(c, g, s, eps, kind="mean"):
    mean, var = c.moments[:, :, 0], c.moments[:, :, 1]
    g.wait_ge(s.moments, c.nt)
    if kind == "rms":
        g.tensor_tensor(c.rstd[:], mean, mean, ALU.mult).then_inc(s.square, 1)
        g.wait_ge(s.square, 1)
        g.tensor_tensor(c.rstd[:], c.rstd[:], var, ALU.add).then_inc(s.square, 1)
        g.wait_ge(s.square, 2)
        var = c.rstd[:]
    g.tensor_scalar(c.var_eps[:], var, eps, None, ALU.add).then_inc(s.var_eps, 1)
    g.wait_ge(s.var_eps, 1)
    g.tensor_tensor(c.rstd[:], c.var_eps[:], c.minus_half[:, 0:c.nt], ALU.pow).then_inc(s.rstd, 1)


TURN = "turned_ps turned "


def turn_tensor(c, pe, ready, s, src, half=0, bank_free=None):
    for t in range(4 * half, 4 * half + 4):
        pe.wait_ge(ready, t + 1)
        if half > 0:
            pe.wait_ge(bank_free, t - 3)
        pe.transpose(c.ps[:, t % 4, 0:P], src[:, t], c.w("ident")).then_inc(s.turned_ps, 1)


def turn_scalar(c, act, s, dst, half=0):
    for t in range(4 * half, 4 * half + 4):
        act.wait_ge(s.turned_ps, t + 1)
        act.copy(dst[:, tok(t)], c.ps[:, t % 4, 0:P]).then_inc(s.turned, 1)


def attention(c, n, keys_from="h", mode="plain", q_scale=1.0, exp_scale=1.0, bias=False,
              out_bias=False, rms=False, loads=()):
    nc, nt = c.nc, c.nt
    c.turn_over()
    s = signals(c, NORM + TURN + "k_ps v_ps q_ready kx_ready vx_ready scores_ps factored scored "
                "max_ready shifted probs_ready probsT_ps probsT_ready o_ps inv_ready att_ready oT_ps "
                "oT_ready y_ps y_added biased values_read qk_read bias_scaled")
    if rms:
        r = signals(c, NORM)
    if mode == "latent":
        l = signals(c, "maps_ps copied squared sums means rms q_normed k_normed k_weighted keys_ready")
    if mode == "sparse":
        sp = signals(c, "row_starts top less_max summed candidates tau compared row_open open_ps count_open step "
                     "shifted_tau less_tau")
    kvT = c.hT if keys_from == "h" else c.ctxT
    kc = c.room(2)[:, 0:nt * P].rearrange("p (t m k) -> p t m k", t=nt, m=2)
    kx = lambda t: c.room(t % 2)
    if mode == "sparse":
        buf = lambda t: c.room((3, 4, 5, 8)[t])
    else:
        buf = lambda t: c.room(3 + t % 3)
    probsT = lambda t: c.room(6 + t % 2)
    sums = lambda t: c.tiny[:, t, 0:4].rearrange("p a b -> p (a b)")
    rms_of = lambda t: c.tiny[:, t, 4:8].rearrange("p a b -> p (a b)")
    squares = lambda t: c.room(5)[:, (t % 4) * 256:(t % 4 + 1) * 256]
    scores_ps = lambda t: c.ps[:, 2 * (t % 2):2 * (t % 2) + 2].rearrange("p m n -> p (m n)")
    q_ps = lambda t: c.ps[:, 4 + t % 4, 0:P]
    k_ps = lambda t: c.ps[:, 4 + t % 4, P:2 * P]
    maps_ps = lambda t: c.ps[:, 4 + t % 4, 0:3 * D]
    maps = lambda t: c.room(3 + t % 4 // 2)[:, (t % 2) * 512:(t % 2) * 512 + 3 * D]
    o_ps = lambda t: c.ps[:, 6 + t % 2, 0:144]
    oT_ps = lambda t: c.ps[:, 6 + t % 2, 256:256 + P]
    y_ps = lambda t: c.ps[:, 6 + t % 2, 384:384 + P]
    heads = lambda a: a.rearrange("p (h d) -> p h d", d=HD)
    scores_read = s.shifted if mode == "plain" else s.factored if mode == "decay" else s.scored
    probs_ready = s.probs_ready

    with nc.Block() as block:
        if loads:
            @block.sync
            def _(sp):
                for m in ("L1f_w1", "L1f_w2"):
                    sp.wait_ge(c.loaded[m], 16)
                for m in loads:
                    sp.dma_start(c.big[m][:], c.dram[m]).then_inc(c.loaded[m], 16)

        @block.tensor
        def _(pe):
            for half in range(nt // 4):
                tiles = range(4 * half, 4 * half + 4)
                turn_tensor(c, pe, r.ready if rms else s.ready, s, c.hn if rms else c.h, half,
                            s.values_read)
                for t in tiles:
                    pe.wait_ge(s.turned, t + 1)
                    if t >= 4:
                        pe.wait_ge(s.qk_read, t - 3)
                    if mode == "latent":
                        pe.matmul(maps_ps(t), c.hT[:, tok(t)], c.q_of_h[:], start=True, stop=True)\
                            .then_inc(l.maps_ps, 1)
                    else:
                        for at, w, src in ((0, "_wq", c.hT), (P, "_wk", kvT)):
                            for b in range(2):
                                for m in range(2):
                                    cols = slice(at + m * S, at + m * S + S)
                                    last = pe.matmul(c.ps[part(b), 4 + t % 4, cols], c.w(n + w)[:, part(m)],
                                                     src[:, seq(t, b)], start=True, stop=True)
                        last.then_inc(s.k_ps, 1)
                    wv = c.v_of_h[:] if mode == "latent" else c.w(n + "_wv")
                    for b in range(2):
                        for u in range(2):
                            last = pe.matmul(c.ps[part(u), t % 4, part(b)], kvT[:, seq(t, b)],
                                             wv[:, part(u)], start=True, stop=True)
                    last.then_inc(s.v_ps, 1)
                if mode == "latent":
                    for t in tiles:
                        pe.wait_ge(l.q_normed, t + 1)
                        pe.wait_ge(l.keys_ready, t + 1)
                        for at, src in ((0, c.att), (P, c.hn)):
                            for b in range(2):
                                for m in range(2):
                                    cols = slice(at + m * S, at + m * S + S)
                                    last = pe.matmul(c.ps[part(b), 4 + t % 4, cols], src[part(b), t, part(m)],
                                                     c.w("ident")[part(b), part(b)], start=True, stop=True)
                        last.then_inc(s.k_ps, 1)

            def scores(t):
                pe.wait_ge(s.q_ready, t + 1)
                pe.wait_ge(s.kx_ready, t + 1)
                if t < 2:
                    pe.wait_ge(s.values_read, nt - 2 + 2 * t)
                else:
                    pe.wait_ge(scores_read, t - 1)
                for m in range(2):
                    last = pe.matmul(c.ps[:, 2 * (t % 2) + m], c.q_apart[:, t, m].rearrange("p b q -> p (b q)"),
                                     kx(t)[:, m * 512:(m + 1) * 512], start=True, stop=True)
                last.then_inc(s.scores_ps, 1)

            def turn_probs(t):
                pe.wait_ge(probs_ready, t + 1)
                if t == 0:
                    pe.wait_ge(s.qk_read, nt - 2)
                for k in range(2):
                    if t >= 1:
                        pe.wait_ge(s.probsT_ready, 2 * (t - 1) + k + 1)
                    for j in range(4):
                        last = pe.transpose(c.ps[:, 4 + k, j * P:(j + 1) * P],
                                            buf(t)[:, (4 * k + j) * P:(4 * k + j + 1) * P], c.w("ident"))
                    last.then_inc(s.probsT_ps, 1)

            def weigh_values(t):
                if t == 0:
                    pe.wait_ge(s.qk_read, nt)
                if t >= 2:
                    pe.wait_ge(s.y_added, t - 1)
                pe.wait_ge(s.probsT_ready, 2 * t + 2)
                for j in range(HEADS // 2):
                    for b in range(2):
                        last = pe.matmul(o_ps(t)[part(b), j * 18:(j + 1) * 18],
                                         probsT(t)[:, seq(j, b)], c.vx[:, t, b, j], start=True, stop=True)
                last.then_inc(s.o_ps, 1)

            def turn_output(t):
                pe.wait_ge(s.att_ready, t + 1)
                pe.transpose(oT_ps(t), c.att[:, t], c.w("ident")).then_inc(s.oT_ps, 1)

            def project(t):
                pe.wait_ge(s.oT_ready, t + 1)
                pe.matmul(y_ps(t), c.oT[:, tok(t)], c.w(n + "_wo"), start=True, stop=True)\
                    .then_inc(s.y_ps, 1)

            if mode == "sparse":
                for t in range(nt):
                    scores(t)
                pe.wait_ge(s.qk_read, nt)
                pe.wait_ge(sp.row_open, 1)
                pe.matmul(c.ps[0:1, 7, 0:1], c.row_open[:], c.w("ones")[:, 0:1], start=True, stop=True)\
                    .then_inc(sp.open_ps, 1)
            for k in range(nt + 3):
                if k < nt and mode != "sparse":
                    scores(k)
                if 0 <= k - 1 < nt:
                    turn_probs(k - 1)
                if 0 <= k - 3 < nt:
                    turn_output(k - 3)
                if 0 <= k - 2 < nt:
                    weigh_values(k - 2)
                if 0 <= k - 3 < nt:
                    project(k - 3)

        @block.scalar
        def _(act):
            def take_values(t):
                act.wait_ge(s.v_ps, t + 1)
                for u in range(2):
                    act.copy(c.vx[part(u), t, :, :, u * 9:u * 9 + HD],
                             c.ps[part(u), t % 4, 0:P].rearrange("p (b j d) -> p b j d", b=2, d=HD))\
                        .then_inc(s.vx_ready if u == 0 else s.values_read, 1)

            def take_maps(t):
                act.wait_ge(l.maps_ps, t + 1)
                if t >= 4:
                    act.wait_ge(l.keys_ready, t - 3)
                act.copy(maps(t), maps_ps(t)).then_inc(l.copied, 1)
                act.wait_ge(l.copied, t + 1)
                act.activation(squares(t), maps(t)[:, 0:2 * D], ACT.Square).then_inc(l.squared, 1)

            def take_queries_and_keys(t):
                act.wait_ge(s.k_ps, t + 1)
                halves_of = lambda a: a.rearrange("p (m k) -> p m k", m=2)
                if bias:
                    if t == 0:
                        act.wait_ge(s.bias_scaled, 1)
                    for m in range(2):
                        for b in range(2):
                            last = act.activation(c.q_apart[part(b), t, m, b], q_ps(t)[part(b), part(m)],
                                                  ACT.Identity, bias=c.scaled_bias[part(b), m:m + 1],
                                                  scale=q_scale)
                    last.then_inc(s.q_ready, 1)
                    for m in range(2):
                        last = act.activation(kc[:, t, m], k_ps(t)[:, part(m)], ACT.Identity,
                                              bias=c.w(n + "_bk")[:, m:m + 1])
                    last.then_inc(s.qk_read, 1)
                    return
                for b in range(2):
                    own = c.q_apart[part(b), t, :, b]
                    if mode == "latent":
                        last = act.activation(own, halves_of(q_ps(t)[part(b)]), ACT.Identity,
                                              scale=c.w("L2a_qn")[part(b)])
                    else:
                        last = act.copy(own, halves_of(q_ps(t)[part(b)]))
                last.then_inc(s.q_ready, 1)
                act.copy(kc[:, t], halves_of(k_ps(t))).then_inc(s.qk_read, 1)

            for half in range(nt // 4):
                turn_scalar(c, act, s, c.hT, half)
                for t in range(4 * half, 4 * half + 4):
                    if mode == "latent":
                        take_values(t)
                        take_maps(t)
                    else:
                        take_queries_and_keys(t)
                        take_values(t)
                if mode == "latent":
                    for t in range(4 * half, 4 * half + 4):
                        take_queries_and_keys(t)
            if mode == "sparse":
                for t in range(nt):
                    act.wait_ge(s.scores_ps, t + 1)
                    act.copy(buf(t), scores_ps(t)).then_inc(s.scored, 1)
            def weights(k):
                if mode == "sparse":
                    act.wait_ge(sp.less_tau, k + 1)
                else:
                    act.wait_ge(s.shifted, k + 1)
                act.activation(buf(k), buf(k), ACT.Relu if mode == "sparse" else ACT.Exp,
                               scale=exp_scale).then_inc(s.probs_ready, 1)

            for k in range(nt + 3):
                if k < nt and mode == "sparse":
                    weights(k)
                t = k - 1
                if 0 <= t < nt:
                    for j in range(2):
                        act.wait_ge(s.probsT_ps, 2 * t + j + 1)
                        if t >= 2:
                            act.wait_ge(s.o_ps, t - 1)
                        act.copy(probsT(t)[:, j * 512:(j + 1) * 512], c.ps[:, 4 + j])\
                            .then_inc(s.probsT_ready, 1)
                t = k - 3
                if 0 <= t < nt:
                    act.wait_ge(s.oT_ps, t + 1)
                    if bias:
                        act.activation(c.oT[:, tok(t)], oT_ps(t), ACT.Identity, bias=c.w(n + "_bv"))\
                            .then_inc(s.oT_ready, 1)
                    else:
                        act.copy(c.oT[:, tok(t)], oT_ps(t)).then_inc(s.oT_ready, 1)
                if k < nt and mode != "sparse":
                    weights(k)

        @block.gpsimd
        def _(g):
            c.begin(g)
            if bias:
                g.tensor_scalar(c.scaled_bias[:], c.w(n + "_bq"), q_scale, None, ALU.mult)\
                    .then_inc(s.bias_scaled, 1)
            norm_gpsimd(c, g, s, 1e-5)
            if rms:
                norm_gpsimd(c, g, r, 1e-6, "rms")
            if mode == "sparse":
                row_starts = c.room(6)[:, 0:nt * HEADS * TOP]
                g.memset(row_starts, 1.0).then_inc(sp.row_starts, 1)
                g.wait_ge(sp.row_starts, 1)
                g.memset(row_starts.rearrange("p (r k) -> p r k", k=TOP)[:, :, 0], 0.0)\
                    .then_inc(sp.row_starts, 1)
            if mode == "latent":
                for t in range(nt):
                    g.wait_ge(l.sums, t + 1)
                    g.tensor_scalar(sums(t), sums(t), 1.0 / HD, 1.1920929e-07, ALU.mult, ALU.add)\
                        .then_inc(l.means, 1)
                    g.wait_ge(l.means, t + 1)
                    g.tensor_tensor(rms_of(t), sums(t), c.minus_half[:], ALU.pow).then_inc(l.rms, 1)
            for t in range(nt):
                g.wait_ge(s.qk_read, t + 1)
                if t >= 2:
                    g.wait_ge(s.scores_ps, t - 1)
                g.tensor_tensor(kx(t).rearrange("p (m h k) -> p m h k", m=2, k=S), bcast(kc[:, t], 2, HEADS // 2),
                                bcast(bcast(c.w("head_of_row"), 2, S), 1, 2), ALU.mult)\
                    .then_inc(s.kx_ready, 1)

        @block.vector
        def _(v):
            norm_vector(c, v, s, c.x, c.h)
            if rms:
                v.wait_ge(s.ready, nt)
                norm_vector(c, v, r, c.h, c.hn, "rms", c.w(n + "_n1"))
            for half in range(nt // 4):
                tiles = range(4 * half, 4 * half + 4)
                if mode == "latent":
                    for t in tiles:
                        v.wait_ge(l.squared, t + 1)
                        v.tensor_reduce(sums(t), heads(squares(t)), AX.X, ALU.add).then_inc(l.sums, 1)
                    for t in tiles:
                        keys = c.hn[:, t]
                        v.wait_ge(l.rms, t + 1)
                        v.tensor_tensor(heads(c.att[:, t]), heads(maps(t)[:, 0:D]),
                                        bcast(rms_of(t)[:, 0:HEADS], 2, HD), ALU.mult).then_inc(l.q_normed, 1)
                        v.tensor_tensor(heads(keys), heads(maps(t)[:, D:2 * D]),
                                        bcast(rms_of(t)[:, HEADS:2 * HEADS], 2, HD), ALU.mult)\
                            .then_inc(l.k_normed, 1)
                        v.wait_ge(l.k_normed, t + 1)
                        v.tensor_tensor(keys, keys, c.w("L2a_kn"), ALU.mult).then_inc(l.k_weighted, 1)
                        v.wait_ge(l.k_weighted, t + 1)
                        v.tensor_tensor(keys, keys, maps(t)[:, 2 * D:3 * D], ALU.add)\
                            .then_inc(l.keys_ready, 1)

            def shift(t):
                shaped = buf(t).rearrange("p (h k) -> p h k", k=S)
                if t >= 3:
                    v.wait_ge(s.probsT_ps, 2 * (t - 2))
                ps = scores_ps(t).rearrange("p (h k) -> p h k", k=S)
                v.wait_ge(s.scores_ps, t + 1)
                if mode == "bias":
                    v.tensor_tensor(buf(t), scores_ps(t), c.bias0[:], ALU.add).then_inc(s.scored, 1)
                elif mode == "decay":
                    v.tensor_tensor(shaped, ps, bcast(c.decay3[:], 1, HEADS), ALU.mult).then_inc(s.factored, 1)
                    v.wait_ge(s.factored, t + 1)
                    v.tensor_tensor(shaped, shaped, bcast(c.w("causal"), 1, HEADS), ALU.add)\
                        .then_inc(s.scored, 1)
                elif mode != "plain":
                    v.tensor_tensor(shaped, ps, bcast(c.w("causal"), 1, HEADS), ALU.add).then_inc(s.scored, 1)
                src = ps
                if mode != "plain":
                    src = shaped
                    v.wait_ge(s.scored, t + 1)
                v.tensor_reduce(c.row_max[:, t], src, AX.X, ALU.max).then_inc(s.max_ready, 1)
                v.wait_ge(s.max_ready, t + 1)
                v.tensor_tensor(shaped, src, bcast(c.row_max[:, t], 2, S), ALU.subtract).then_inc(s.shifted, 1)

            def normalise(t):
                o = o_ps(t).rearrange("p (h d) -> p h d", d=HD + 1)
                v.wait_ge(s.o_ps, t + 1)
                v.reciprocal(c.row_inv[:, t], o[:, :, HD]).then_inc(s.inv_ready, 1)
                v.wait_ge(s.inv_ready, t + 1)
                v.tensor_tensor(heads(c.att[:, t]), o[:, :, 0:HD], bcast(c.row_inv[:, t], 2, HD),
                                ALU.mult).then_inc(s.att_ready, 1)

            def add(t):
                x = c.h if rms else c.x
                v.wait_ge(s.y_ps, t + 1)
                v.tensor_tensor(x[:, t], x[:, t], y_ps(t), ALU.add).then_inc(s.y_added, 1)
                if out_bias:
                    v.wait_ge(s.y_added, t + 1)
                    v.tensor_tensor(x[:, t], x[:, t], c.w(n + "_bo"), ALU.add).then_inc(s.biased, 1)

            def less_threshold(t):
                shaped = buf(t).rearrange("p (h k) -> p h k", k=S)
                v.tensor_tensor(shaped, shaped, bcast(c.row_inv[:, t], 2, S), ALU.subtract)\
                    .then_inc(sp.less_tau, 1)

            if mode == "sparse":
                thresholds(c, v, s, sp, buf)
            for k in range(nt + 3):
                if k < nt:
                    if mode == "sparse":
                        less_threshold(k)
                    else:
                        shift(k)
                if 0 <= k - 2 < nt:
                    normalise(k - 2)
                if 0 <= k - 3 < nt:
                    add(k - 3)


def thresholds(c, v, s, sp, z):
    by_row = lambda a: a.rearrange("p (r k) -> p r k", k=TOP)
    count = c.nt * HEADS * TOP
    top, sums = by_row(c.room(2)[:, 512:512 + count]), by_row(c.room(0)[:, 0:count])
    of_head = c.row_max[:].rearrange("p t h -> p (t h)")
    tau = c.row_inv[:].rearrange("p t h -> p (t h)")
    open_rows = c.tiny[:, 0, 0:8].rearrange("p a b -> p (a b)")
    for t in range(c.nt):
        v.wait_ge(s.scored, t + 1)
        for h in range(HEADS):
            last = v.max(out=top[:, HEADS * t + h], in_=z(t)[:, h * S:(h + 1) * S])
        last.then_inc(sp.top, 1)
    v.wait_ge(sp.top, c.nt)
    v.tensor_copy(of_head, top[:, :, 0]).then_inc(s.max_ready, 1)
    v.wait_ge(s.max_ready, 1)
    v.tensor_tensor(top, top, bcast(of_head, 2, TOP), ALU.subtract).then_inc(sp.less_max, 1)
    v.wait_ge(sp.less_max, 1)
    flat = lambda a: a.rearrange("p r k -> p (r k)")
    v.wait_ge(sp.row_starts, 2)
    v.tensor_tensor_scan(flat(sums), c.room(6)[:, 0:c.nt * HEADS * TOP], flat(top), 0.0, ALU.mult, ALU.add)\
        .then_inc(sp.summed, 1)
    v.wait_ge(sp.summed, 1)
    v.scalar_tensor_tensor(out=sums, in0=sums, scalar=-1.0,
                           in1=bcast(c.w("inverse_rank")[:, 0:TOP], 1, c.nt * HEADS), op0=ALU.add,
                           op1=ALU.mult).then_inc(sp.candidates, 1)
    v.wait_ge(sp.candidates, 1)
    v.tensor_reduce(tau, sums, AX.X, ALU.max).then_inc(sp.tau, 1)
    v.wait_ge(sp.tau, 1)
    v.tensor_tensor(open_rows, top[:, :, TOP - 1], tau, ALU.is_gt).then_inc(sp.compared, 1)
    v.wait_ge(sp.compared, 1)
    v.tensor_reduce(c.row_open[:], open_rows, AX.X, ALU.max).then_inc(sp.row_open, 1)
    v.wait_ge(sp.open_ps, 1)
    v.tensor_copy(c.count_open[:], c.ps[0:1, 7, 0:1]).then_inc(sp.count_open, 1)
    v.wait_ge(sp.count_open, 1)
    open_count = v.value_load(c.count_open[0:1, 0:1], min_val=0, max_val=P)
    with v.If(open_count > 0):
        v.memset(c.room(1), 1.0).then_inc(sp.step, 1)
        v.wait_ge(sp.step, 1)
        v.memset(c.room(1).rearrange("p (h k) -> p h k", k=S)[:, :, 0], 0.0).then_inc(sp.step, 1)
        for t in range(c.nt):
            sort_rows(c, v, sp.step, t, z(t))
    v.tensor_tensor(tau, tau, of_head, ALU.add).then_inc(sp.shifted_tau, 1)
    v.wait_ge(sp.shifted_tau, 1)


def sort_rows(c, v, step, t, z):
    spare = [c.room(6), c.room(7)]
    shaped = lambda a: a.rearrange("p (h k) -> p h k", k=S)
    done = (SORT_STEPS + 4) * t + 3
    src, at = spare[1], 0
    v.tensor_tensor(shaped(src), shaped(z), bcast(c.row_max[:, t], 2, S), ALU.subtract).then_inc(step, 1)
    v.wait_ge(step, done)
    k = 2
    while k <= S:
        j = k // 2
        while j >= 1:
            dst = spare[at % 2]
            ways = 2 if k < S else 1
            cut = lambda a: a.rearrange("p (b way g s r) -> p b way g s r", way=ways, g=k // (2 * j), s=2, r=j)
            for way in range(ways):
                for side in range(2):
                    op = ALU.max if side == way else ALU.min
                    last = v.tensor_tensor(cut(dst)[:, :, way, :, side], cut(src)[:, :, way, :, 0],
                                           cut(src)[:, :, way, :, 1], op)
            at += 1
            last.then_inc(step, 1)
            v.wait_ge(step, done + at)
            src = dst
            j //= 2
        k *= 2
    sums = spare[at % 2]
    v.tensor_tensor_scan(sums, c.room(1), src, 0.0, ALU.mult, ALU.add).then_inc(step, 1)
    v.wait_ge(step, done + at + 1)
    v.scalar_tensor_tensor(out=shaped(src), in0=shaped(sums), scalar=-1.0,
                           in1=bcast(c.w("inverse_rank"), 1, HEADS), op0=ALU.add, op1=ALU.mult)\
        .then_inc(step, 1)
    v.wait_ge(step, done + at + 2)
    v.tensor_reduce(c.row_inv[:, t], shaped(src), AX.X, ALU.max).then_inc(step, 1)
    v.wait_ge(step, done + at + 3)


def channel_attention(c):
    nc = c.nc
    c.turn_over()
    s = signals(c, NORM + "q_scaled q_ready k_scaled k_ready v_ready scores_ps max_ready shifted "
                "exp_ready sum_ready inv_ready weights_ready spread turned_ps turned y_ps doubled summed "
                "biased")
    SETS = "gl"
    q = [c.room(0)[:, i * 512:(i + 1) * 512].rearrange("p (t d) -> p t d", t=HT) for i in range(2)]
    k = [c.room(1)[:, i * 512:(i + 1) * 512].rearrange("p (t d) -> p t d", t=HT) for i in range(2)]
    vT = [c.room(2)[:, i * 512:(i + 1) * 512] for i in range(2)]
    score = c.room(3)[:, 0:512].rearrange("p (b m e) -> p b m e", b=2, e=32)
    score_ps = c.ps[:, 0:2, 0:256].rearrange("p b (m e) -> p b m e", e=32)
    row = c.tiny[:, 0].rearrange("p a b -> p (a b)")
    stat = lambda i: row[:, i * 16:(i + 1) * 16].rearrange("p (b m) -> p b m", b=2)
    spread = c.room(3, 2)
    blocks_of = c.room(5, 2)
    diag = c.room(7, 2)
    with nc.Block() as block:
        @block.tensor
        def _(pe):
            pe.wait_ge(s.q_ready, 2)
            pe.wait_ge(s.k_ready, 2)
            for t in range(HT):
                for b in range(2):
                    for i in range(2):
                        for h in range(4):
                            ch = slice(32 * h, 32 * h + 32)
                            last = pe.matmul(c.ps[ch, b, (2 * t + i) * 32:(2 * t + i + 1) * 32],
                                             q[i][part(b), t, ch], k[i][part(b), t, ch],
                                             start=True, stop=True,
                                             tile_position=(64 * b, 32 * h))
            last.then_inc(s.scores_ps, 1)
            for m in range(4):
                pe.wait_ge(s.spread, m + 1)
                for j in range(4):
                    last = pe.transpose(c.ps[:, 2 + m, j * P:(j + 1) * P],
                                        diag[:, (4 * m + j) * P:(4 * m + j + 1) * P], c.w("ident"))
                last.then_inc(s.turned_ps, 1)
            pe.wait_ge(s.v_ready, 2)
            pe.wait_ge(s.turned, 4)
            for t in range(HT):
                for b in range(2):
                    for i in range(2):
                        last = pe.matmul(c.ps[part(b), 6, tok(t)], vT[i][:, seq(t, b)],
                                         blocks_of[:, (8 * b + 2 * t + i) * P:(8 * b + 2 * t + i + 1) * P],
                                         start=(i == 0), stop=(i == 1))
            last.then_inc(s.y_ps, 1)

        @block.scalar
        def _(act):
            for i, n in enumerate(SETS):
                act.activation(vT[i], c.ctxT[:], ACT.Identity, bias=c.w("L0x_bv" + n),
                               scale=c.w("L0x_wv" + n)).then_inc(s.v_ready, 1)
            act.wait_ge(s.shifted, 1)
            act.activation(score, score, ACT.Exp, scale=D ** -0.5).then_inc(s.exp_ready, 1)
            for m in range(4):
                act.wait_ge(s.turned_ps, m + 1)
                act.copy(blocks_of[:, m * 512:(m + 1) * 512], c.ps[:, 2 + m]).then_inc(s.turned, 1)

        @block.gpsimd
        def _(g):
            c.begin(g)
            norm_gpsimd(c, g, s, 1e-5)
            for i, n in enumerate(SETS):
                g.tensor_tensor(k[i], c.ctx_tok[:], bcast(c.w("L0x_wk" + n), 1, HT), ALU.mult)\
                    .then_inc(s.k_scaled, 1)
                g.wait_ge(s.k_scaled, i + 1)
                g.tensor_tensor(k[i], k[i], bcast(c.w("L0x_bk" + n), 1, HT), ALU.add).then_inc(s.k_ready, 1)

        @block.vector
        def _(v):
            norm_vector(c, v, s, c.x, c.h)
            v.wait_ge(s.ready, HT)
            for i, n in enumerate(SETS):
                v.tensor_tensor(q[i], c.h[:], bcast(c.w("L0x_wq" + n), 1, HT), ALU.mult)\
                    .then_inc(s.q_scaled, 1)
                v.wait_ge(s.q_scaled, i + 1)
                v.tensor_tensor(q[i], q[i], bcast(c.w("L0x_bq" + n), 1, HT), ALU.add).then_inc(s.q_ready, 1)
            v.wait_ge(s.scores_ps, 1)
            v.tensor_reduce(stat(0), score_ps, AX.X, ALU.max).then_inc(s.max_ready, 1)
            v.wait_ge(s.max_ready, 1)
            v.tensor_tensor(score, score_ps, bcast(stat(0), 3, 32), ALU.subtract).then_inc(s.shifted, 1)
            v.wait_ge(s.exp_ready, 1)
            v.tensor_reduce(stat(1), score, AX.X, ALU.add).then_inc(s.sum_ready, 1)
            v.wait_ge(s.sum_ready, 1)
            v.reciprocal(stat(2), stat(1)).then_inc(s.inv_ready, 1)
            v.wait_ge(s.inv_ready, 1)
            v.tensor_tensor(score, score, bcast(stat(2), 3, 32), ALU.mult).then_inc(s.weights_ready, 1)
            v.wait_ge(s.weights_ready, 1)
            flat = c.room(3)[:, 0:512].rearrange("p (m e) -> p m e", e=32)
            for m in range(4):
                v.tensor_tensor(diag[:, m * 512:(m + 1) * 512].rearrange("p (m h e) -> p m h e", h=4, e=32),
                                bcast(flat[:, 4 * m:4 * m + 4], 2, 4),
                                bcast(bcast(c.w("block32"), 2, 32), 1, 4), ALU.mult).then_inc(s.spread, 1)
            v.wait_ge(s.y_ps, 1)
            y = c.att[:]
            v.scalar_tensor_tensor(out=y, in0=c.ps[:, 6].rearrange("p (t d) -> p t d", t=HT), scalar=2.0,
                                   in1=bcast(c.w("L0x_wp"), 1, HT), op0=ALU.mult, op1=ALU.mult)\
                .then_inc(s.doubled, 1)
            v.wait_ge(s.doubled, 1)
            v.tensor_tensor(c.x[:], c.x[:], y, ALU.add).then_inc(s.summed, 1)
            v.wait_ge(s.summed, 1)
            v.tensor_tensor(c.x[:], c.x[:], bcast(c.w("L0x_bp"), 1, HT), ALU.add).then_inc(s.biased, 1)


ROUTE = "logits_ps logits_ready top_ready index_ready index_f gap gap_exp denominator first second "


def route_vector(c, v, s, top, bank):
    T = c.tiny
    v.wait_ge(s.logits_ps, HT)
    for t in range(HT):
        v.tensor_copy(T[:, t, 0], c.ps[:, bank, t * E:(t + 1) * E]).then_inc(s.logits_ready, 1)
        v.wait_ge(s.logits_ready, t + 1)
        v.max(T[:, t, 1], T[:, t, 0]).then_inc(s.top_ready, 1)
        v.wait_ge(s.top_ready, t + 1)
        v.max_index(c.index[:, t], T[:, t, 1], T[:, t, 0]).then_inc(s.index_ready, 1)
    v.wait_ge(s.index_ready, HT)
    v.tensor_copy(T[:, :, 2], c.index[:]).then_inc(s.index_f, 1)


def experts(c, n, top, gated):
    nc = c.nc
    twice = n != "L0f"
    c.turn_over()
    s = signals(c, NORM + TURN + ROUTE + "up_ps gate_ps hidden_ready activated down_ps added base "
                "total prob onehot rank_ps ranked kept counted picked weights_ready wT_ps wT_ready counts_ps")
    if twice:
        r = signals(c, NORM)
    src = c.hn if twice else c.h
    chunks, width = (I2C, IC) if gated else (HC, P)
    hidden = lambda e: c.room(2 * (e % 2), 2)[0:width].rearrange("p (c n) -> p c n", c=chunks)
    act_buf = lambda k: c.room(4)[0:width, (k % 2) * 512:(k % 2 + 1) * 512]
    T = c.tiny
    wT = c.room(5)[0:E, 0:HT * P]
    ps_small = 7
    with nc.Block() as block:
        @block.tensor
        def _(pe):
            turn_tensor(c, pe, (r if twice else s).ready, s, src)
            for t in range(HT):
                pe.wait_ge(s.turned, t + 1)
                pe.matmul(c.ps[:, ps_small, t * E:(t + 1) * E], c.hT[:, tok(t)],
                          c.w(n + ("_wr" if n == "L0f" else "_gate")), start=True, stop=True)\
                    .then_inc(s.logits_ps, 1)

            def up(e):
                for j in range(chunks):
                    k = e * chunks + j
                    cols = slice(k * width, (k + 1) * width)
                    if gated:
                        for w, bank, sig in (("w1", 0, s.up_ps), ("w3", 2, s.gate_ps)):
                            if k >= 2:
                                pe.wait_ge(s.hidden_ready, k - 1)
                            pe.matmul(c.ps[0:width, bank + k % 2], c.big[n + "_" + w][:, cols], c.hT[:],
                                      start=True, stop=True).then_inc(sig, 1)
                    else:
                        if k >= 4:
                            pe.wait_ge(s.hidden_ready, k - 3)
                        pe.matmul(c.ps[:, k % 4], c.big[n + "_w1"][:, cols], c.hT[:], start=True,
                                  stop=True).then_inc(s.up_ps, 1)

            def down(e):
                pe.wait_ge(s.hidden_ready, (e + 1) * chunks)
                if e >= 2:
                    pe.wait_ge(s.added, HT * (e - 1))
                for t in range(HT):
                    for j in range(chunks):
                        k = e * chunks + j
                        last = pe.matmul(c.ps[:, 4 + e % 2, tok(t)], hidden(e)[:, j, tok(t)],
                                         c.big[n + "_w2"][0:width, k * D:(k + 1) * D],
                                         start=(j == 0), stop=(j == chunks - 1))
                last.then_inc(s.down_ps, 1)

            for m in ("w1", "w3", "w2") if gated else ("w1", "w2"):
                pe.wait_ge(c.loaded[f"{n}_{m}"], 16)
            up(0)
            if n == "L1f":
                for t in range(HT):
                    pe.wait_ge(s.onehot, HT)
                    for q in range(t + 1):
                        m = "before" if q == t else "ones"
                        last = pe.matmul(c.ps[:, 6, 256 + t * E:256 + (t + 1) * E], c.w(m), T[:, q, 4],
                                         start=(q == 0), stop=(q == t))
                    last.then_inc(s.rank_ps, 1)
                for q in range(HT):
                    last = pe.matmul(c.ps[:, 6, 384:384 + E], c.w("ones"), T[:, q, 4], start=(q == 0),
                                     stop=(q == HT - 1))
                last.then_inc(s.counts_ps, 1)
            if n == "L0f":
                for t in range(HT):
                    pe.wait_ge(s.weights_ready, t + 1)
                    pe.transpose(c.ps[0:E, 6, tok(t)], T[:, t, 3], c.w("ident")).then_inc(s.wT_ps, 1)
                pe.wait_ge(s.wT_ready, 1)
                for t in range(HT):
                    pe.matmul(c.ps[:, 7, tok(t)], wT[:, tok(t)], c.w("L0f_b2"), start=True, stop=True)\
                        .then_inc(s.rank_ps, 1)
            for e in range(E):
                if e + 1 < E:
                    up(e + 1)
                down(e)

        @block.scalar
        def _(act):
            turn_scalar(c, act, s, c.hT)

            def activate(e):
                for j in range(chunks):
                    k = e * chunks + j
                    act.wait_ge(s.up_ps, k + 1)
                    if gated:
                        if k >= 2:
                            act.wait_ge(s.hidden_ready, k - 1)
                        act.activation(act_buf(k), c.ps[0:width, k % 2], ACT.Silu).then_inc(s.activated, 1)
                    else:
                        if e >= 2:
                            act.wait_ge(s.down_ps, e - 1)
                        out = hidden(e)[:, j]
                        if n == "L0f":
                            act.activation(out, c.ps[:, k % 4], ACT.Gelu, bias=c.w("L0f_b1")[:, k:k + 1])\
                                .then_inc(s.hidden_ready, 1)
                        else:
                            act.activation(out, c.ps[:, k % 4], ACT.Gelu).then_inc(s.hidden_ready, 1)

            act.wait_ge(s.gap, 1)
            exp_in = T[:, :, 5] if n == "L1f" else T[:, :, 5, 0:1]
            act.activation(exp_in, exp_in, ACT.Exp).then_inc(s.gap_exp, 1)
            if n == "L0f":
                act.wait_ge(s.wT_ps, HT)
                act.copy(wT, c.ps[0:E, 6]).then_inc(s.wT_ready, 1)
            for e in range(E):
                activate(e)

        @block.gpsimd
        def _(g):
            c.begin(g)
            norm_gpsimd(c, g, s, 1e-5)
            if twice:
                norm_gpsimd(c, g, r, 1e-6 if gated else 1e-5, "rms" if gated else "mean")

        @block.vector
        def _(v):
            norm_vector(c, v, s, c.x, c.h)
            if twice:
                v.wait_ge(s.ready, HT)
                if gated:
                    norm_vector(c, v, r, c.h, c.hn, "rms", c.w(n + "_rms"))
                else:
                    norm_vector(c, v, r, c.h, c.hn, "mean", c.w(n + "_gamma"), c.w(n + "_beta"))
                v.tensor_tensor(c.x[:], c.x[:], c.h[:], ALU.add).then_inc(s.base, 1)
            route_vector(c, v, s, top, ps_small)
            v.wait_ge(s.index_f, 1)
            where = lambda t, k: T[:, t, 2, k:k + 1]
            if n == "L1f":
                for t in range(HT):
                    last = v.tensor_scalar(T[:, t, 5], T[:, t, 0], T[:, t, 1, 0:1], None, ALU.subtract)
                last.then_inc(s.gap, 1)
                for t in range(HT):
                    v.tensor_scalar(T[:, t, 4], c.w("expert_index"), where(t, 0), None, ALU.is_equal)\
                        .then_inc(s.onehot, 1)
                v.wait_ge(s.gap_exp, 1)
                v.tensor_reduce(T[:, :, 6, 0:1], T[:, :, 5], AX.X, ALU.add).then_inc(s.total, 1)
                v.wait_ge(s.total, 1)
                v.reciprocal(T[:, :, 6, 1:2], T[:, :, 6, 0:1]).then_inc(s.prob, 1)
                v.wait_ge(s.rank_ps, HT)
                v.wait_ge(s.counts_ps, 1)
                for t in range(HT):
                    v.tensor_tensor(T[:, t, 7], c.ps[:, 6, 256 + t * E:256 + (t + 1) * E], c.counts[:],
                                    ALU.add).then_inc(s.ranked, 1)
                    v.wait_ge(s.ranked, t + 1)
                    v.scalar_tensor_tensor(out=T[:, t, 8], in0=T[:, t, 7], scalar=float(CAPACITY),
                                           in1=T[:, t, 4], op0=ALU.is_lt, op1=ALU.mult).then_inc(s.kept, 1)
                    v.wait_ge(s.kept, t + 1)
                    if t == 0:
                        v.wait_ge(s.prob, 1)
                    v.tensor_scalar(T[:, t, 3], T[:, t, 8], T[:, t, 6, 1:2], None, ALU.mult)\
                        .then_inc(s.weights_ready, 1)
                v.wait_ge(s.ranked, HT)
                v.tensor_tensor(c.counts[:], c.counts[:], c.ps[:, 6, 384:384 + E], ALU.add)\
                    .then_inc(s.counted, 1)
            else:
                v.tensor_tensor(T[:, :, 5, 0:1], T[:, :, 1, 1:2], T[:, :, 1, 0:1], ALU.subtract)\
                    .then_inc(s.gap, 1)
                v.wait_ge(s.gap_exp, 1)
                v.tensor_scalar(T[:, :, 5, 1:2], T[:, :, 5, 0:1], 1.0, None, ALU.add)\
                    .then_inc(s.denominator, 1)
                v.wait_ge(s.denominator, 1)
                v.reciprocal(T[:, :, 5, 2:3], T[:, :, 5, 1:2]).then_inc(s.first, 1)
                v.wait_ge(s.first, 1)
                v.tensor_tensor(T[:, :, 5, 3:4], T[:, :, 5, 0:1], T[:, :, 5, 2:3], ALU.mult)\
                    .then_inc(s.second, 1)
                v.wait_ge(s.second, 1)
                for t in range(HT):
                    v.tensor_scalar(T[:, t, 4], c.w("expert_index"), where(t, 0), T[:, t, 5, 2:3],
                                    ALU.is_equal, ALU.mult)
                    v.tensor_scalar(T[:, t, 6], c.w("expert_index"), where(t, 1), T[:, t, 5, 3:4],
                                    ALU.is_equal, ALU.mult).then_inc(s.picked, 1)
                    v.wait_ge(s.picked, t + 1)
                    v.tensor_tensor(T[:, t, 3], T[:, t, 4], T[:, t, 6], ALU.add).then_inc(s.weights_ready, 1)
            v.wait_ge(s.weights_ready, HT)

            def hide(e):
                for j in range(chunks):
                    k = e * chunks + j
                    v.wait_ge(s.gate_ps, k + 1)
                    v.wait_ge(s.activated, k + 1)
                    if e >= 2:
                        v.wait_ge(s.down_ps, e - 1)
                    v.tensor_tensor(hidden(e)[:, j], act_buf(k), c.ps[0:width, 2 + k % 2], ALU.mult)\
                        .then_inc(s.hidden_ready, 1)

            if n == "L0f":
                v.wait_ge(s.rank_ps, HT)
                for t in range(HT):
                    v.tensor_tensor(c.x[:, t], c.x[:, t], c.ps[:, 7, tok(t)], ALU.add).then_inc(s.base, 1)
            if gated:
                hide(0)
            for e in range(E):
                if gated and e + 1 < E:
                    hide(e + 1)
                v.wait_ge(s.down_ps, e + 1)
                for t in range(HT):
                    if e == 0:
                        v.wait_ge(s.base, t + 1 if n == "L0f" else 1)
                    else:
                        v.wait_ge(s.added, HT * (e - 1) + t + 1)
                    v.scalar_tensor_tensor(out=c.x[:, t], in0=c.ps[:, 4 + e % 2, tok(t)],
                                           scalar=T[:, t, 3, e:e + 1], in1=c.x[:, t], op0=ALU.mult,
                                           op1=ALU.add).then_inc(s.added, 1)


def rotary_attention(c):
    nc = c.nc
    n = "L1a"
    c.turn_over()
    s = signals(c, NORM + TURN + "plain_ps turned_cols_ps by_cos by_sin rotated v_ps v_ready scores_ps "
                "scored max_ready shifted exp_ready sum_ready inv_ready probs_ready probsT_ps "
                "probsT_ready o_ps o_ready mid_ps mid_ready y_ps y_ready added")
    r = signals(c, NORM)
    w = c.big["L1_qkv"]
    CH = INNER // P
    roomq, roomk = c.room(0), c.room(1)
    sines = lambda k: c.room((2, 8)[k])
    values = lambda t: c.room((3, 7)[t % 2])
    probs, probsT, outT = c.room(4), c.room(5), c.room(6)
    cos = lambda a: a.rearrange("p (m k) -> p m k", k=S)
    banks = lambda k: c.ps[:, k:k + 2].rearrange("p b n -> p (b n)")
    with nc.Block() as block:
        @block.sync
        def _(sp):
            for m in ("L0f_w1", "L0f_w2"):
                sp.wait_ge(c.loaded[m], 16)
            for m in ("L1f_w1", "L1f_w2"):
                sp.dma_start(c.big[m][:], c.dram[m]).then_inc(c.loaded[m], 16)

        @block.tensor
        def _(pe):
            for half in range(NT // 4):
                turn_tensor(c, pe, s.ready, s, c.h, half, s.turned)
            pe.wait_ge(s.turned, NT)
            pe.wait_ge(c.loaded["L1_qkv"], 16)

            def project(t, k):
                if t > 0 or k > 0:
                    pe.wait_ge(s.by_sin, 2 * t + k)
                if t > 0:
                    pe.wait_ge(s.scored, t)
                for m in range(2):
                    for j in range(CH):
                        at = (2 * m + k) * INNER + j * P
                        last = pe.matmul(c.ps[:, 2 * m + j // 4, (j % 4) * P:(j % 4 + 1) * P],
                                         w[:, at:at + P], c.hT[:, tok(t)], start=True, stop=True)
                last.then_inc(s.plain_ps, 1)

            def project_values(t):
                if t == 1:
                    pe.wait_ge(s.v_ready, 1)
                elif t >= 2:
                    pe.wait_ge(s.probsT_ready, 2 * (t - 1))
                for b in range(2):
                    for u in range(2):
                        last = pe.matmul(c.ps[part(u), 4 + b], c.hT[:, seq(t, b)],
                                         w[:, 4 * INNER + u * 512:4 * INNER + (u + 1) * 512],
                                         start=True, stop=True)
                last.then_inc(s.v_ps, 1)

            def scores(t):
                pe.wait_ge(s.rotated, 2 * t + 2)
                for j in range(CH):
                    for a in range(2):
                        for b in range(2):
                            ch = slice(j * P + b * S, j * P + b * S + S)
                            last = pe.matmul(c.ps[part(b), a, j * S:(j + 1) * S], roomq[part(a), ch],
                                             roomk[part(a), ch], start=True, stop=True)
                last.then_inc(s.scores_ps, 1)

            def turn_probs(t):
                pe.wait_ge(s.v_ready, min(t + 2, NT))
                pe.wait_ge(s.probs_ready, t + 1)
                for k in range(2):
                    for j in range(4):
                        last = pe.transpose(c.ps[:, 4 + k, j * P:(j + 1) * P],
                                            probs[:, (4 * k + j) * P:(4 * k + j + 1) * P], c.w("ident"))
                    last.then_inc(s.probsT_ps, 1)

            def weigh_values(t):
                pe.wait_ge(s.probsT_ready, 2 * t + 2)
                if t > 0:
                    pe.wait_ge(s.y_ready, t)
                for q in range(CH):
                    u, m = q % 2, q // 2
                    for a in range(2):
                        for b in range(2):
                            last = pe.matmul(c.ps[part(a), 6 + u, m * P + b * S:m * P + b * S + S],
                                             values(t)[part(u), b * 512 + m * P + a * 64:b * 512 + m * P + a * 64 + 64],
                                             probsT[part(u), a * 512 + m * P + b * S:a * 512 + m * P + b * S + S],
                                             start=True, stop=True)
                last.then_inc(s.o_ps, 1)

            def project_out(t):
                pe.wait_ge(s.o_ready, 2 * t + 2)
                for q in range(CH):
                    last = pe.matmul(c.ps[:, 6, 0:P], c.w("L1_wo1")[:, q * P:(q + 1) * P],
                                     outT[:, (q % 2) * 512 + (q // 2) * P:(q % 2) * 512 + (q // 2 + 1) * P],
                                     start=(q == 0), stop=(q == CH - 1))
                last.then_inc(s.mid_ps, 1)
                pe.wait_ge(s.mid_ready, t + 1)
                pe.matmul(c.ps[:, 7, 0:P], c.oT[:, tok(t)], c.w("L1_wo2"), start=True, stop=True)\
                    .then_inc(s.y_ps, 1)

            for t in range(NT + 1):
                if t < NT:
                    project_values(t)
                    project(t, 0)
                if t > 0:
                    turn_probs(t - 1)
                if t < NT:
                    project(t, 1)
                if t > 0:
                    weigh_values(t - 1)
                if t < NT:
                    scores(t)
                if t > 0:
                    project_out(t - 1)

        @block.scalar
        def _(act):
            for half in range(NT // 4):
                turn_scalar(c, act, s, c.hT, half)
            for k in range(NT + 1):
                t = k - 1
                if t >= 0:
                    act.wait_ge(s.shifted, t + 1)
                    act.activation(probs, probs, ACT.Exp, scale=WH ** -0.5).then_inc(s.exp_ready, 1)
                if k < NT:
                    act.wait_ge(s.v_ps, k + 1)
                    if k >= 2:
                        act.wait_ge(s.o_ps, k - 1)
                    act.copy(values(k), banks(4)).then_inc(s.v_ready, 1)
                if t < 0:
                    continue
                for j in range(2):
                    act.wait_ge(s.probsT_ps, 2 * t + j + 1)
                    if t > 0:
                        act.wait_ge(s.o_ps, t)
                    act.copy(probsT[:, j * 512:(j + 1) * 512], c.ps[:, 4 + j]).then_inc(s.probsT_ready, 1)
                act.wait_ge(s.o_ps, t + 1)
                if t > 0:
                    act.wait_ge(s.mid_ps, t)
                for u in range(2):
                    act.copy(outT[:, u * 512:(u + 1) * 512], c.ps[:, 6 + u]).then_inc(s.o_ready, 1)
                act.wait_ge(s.mid_ps, t + 1)
                act.activation(c.oT[:, tok(t)], c.ps[:, 6, 0:P], ACT.Relu).then_inc(s.mid_ready, 1)
                act.wait_ge(s.y_ps, t + 1)
                act.copy(c.att[:, t], c.ps[:, 7, 0:P]).then_inc(s.y_ready, 1)

        @block.gpsimd
        def _(g):
            c.begin(g)
            norm_gpsimd(c, g, s, 1e-5)
            for k in range(NT + 1):
                if k > 0:
                    g.wait_ge(s.inv_ready, k)
                    g.tensor_tensor(cos(probs), cos(probs), bcast(c.row_inv[:, k - 1], 2, S), ALU.mult)\
                        .then_inc(s.probs_ready, 1)
                if k < NT:
                    for j, room in enumerate((roomq, roomk)):
                        g.wait_ge(s.by_sin, 2 * k + j + 1)
                        g.tensor_tensor(room, room, sines(j), ALU.add).then_inc(s.rotated, 1)
            norm_gpsimd(c, g, r, 1e-5)

        @block.vector
        def _(v):
            norm_vector(c, v, s, c.x, c.h)

            def rotate(t, k):
                room = (roomq, roomk)[k]
                v.wait_ge(s.plain_ps, 2 * t + k + 1)
                if t > 0:
                    v.wait_ge(s.scores_ps, t)
                    v.wait_ge(s.rotated, 2 * (t - 1) + k + 1)
                v.tensor_tensor(cos(room), cos(banks(0)), bcast(c.w("rope_cos"), 1, 2 * CH), ALU.mult)\
                    .then_inc(s.by_cos, 1)
                v.tensor_tensor(cos(sines(k)), cos(banks(2)), bcast(c.w("rope_sin"), 1, 2 * CH), ALU.mult)\
                    .then_inc(s.by_sin, 1)

            def soften(t):
                v.wait_ge(s.scores_ps, t + 1)
                if t > 0:
                    v.wait_ge(s.probsT_ps, 2 * t)
                v.tensor_tensor(cos(probs), cos(banks(0)), bcast(c.w("causal"), 1, HEADS), ALU.add)\
                    .then_inc(s.scored, 1)
                v.wait_ge(s.scored, t + 1)
                v.tensor_reduce(c.row_max[:, t], cos(probs), AX.X, ALU.max).then_inc(s.max_ready, 1)
                v.wait_ge(s.max_ready, t + 1)
                v.tensor_tensor(cos(probs), cos(probs), bcast(c.row_max[:, t], 2, S), ALU.subtract)\
                    .then_inc(s.shifted, 1)
                v.wait_ge(s.exp_ready, t + 1)
                v.tensor_reduce(c.row_max[:, t], cos(probs), AX.X, ALU.add).then_inc(s.sum_ready, 1)
                v.wait_ge(s.sum_ready, t + 1)
                v.reciprocal(c.row_inv[:, t], c.row_max[:, t]).then_inc(s.inv_ready, 1)

            for t in range(NT + 1):
                if t > 0:
                    soften(t - 1)
                if t < NT:
                    rotate(t, 0)
                    rotate(t, 1)
            v.wait_ge(s.y_ready, NT)
            norm_vector(c, v, r, c.att, c.hn, "mean", c.w("L1_gamma"))
            v.wait_ge(r.ready, NT)
            v.tensor_tensor(c.x[:], c.x[:], c.hn[:], ALU.add).then_inc(s.added, 1)


def matrix_lstm(c):
    nc = c.nc
    c.turn_over()
    s = signals(c, NORM + TURN + "gates_ps gates_ready magnitude exp_ready log_ready floor log_f "
                "decay_ps input spread level_ps masked max_ready shifted weights_ready top floor_exp "
                "qk_ps qk_weighted sum_ready absolute least eps_added inv_ready CT_ps CT_ready o_ps normed "
                "values head_stats head_moments head_eps head_rstd centred scaled_heads gained added")
    H4, W = 4, 32
    T = lambda i: c.tiny[:, :, i, 0:H4]
    gates = c.tiny[:, :, 0]
    weights = c.room(0).rearrange("p (t h k) -> p t h k", t=HT, k=S)
    C = c.room(1).rearrange("p (t h k) -> p t h k", t=HT, k=S)
    CT = c.room(2)
    spread = c.room(3).rearrange("p (t h k) -> p t h k", t=HT, k=S)
    stats = c.room(4)[:, 0:HT * H4 * 6].rearrange("p (t h k) -> p t h k", t=HT, k=6)
    moments = c.room(4)[:, 512:512 + HT * H4 * 2].rearrange("p (t h k) -> p t h k", t=HT, k=2)
    eps = c.room(4)[:, 768:768 + HT * H4].rearrange("p (t h) -> p t h", t=HT)
    rstd = c.room(4)[:, 896:896 + HT * H4].rearrange("p (t h) -> p t h", t=HT)
    hs = c.att[:].rearrange("p t (h d) -> p t h d", d=W)
    values = c.room(5).rearrange("p (t b d) -> p t b d", t=HT, b=2)
    with nc.Block() as block:
        @block.sync
        def _(sp):
            for b in range(2):
                for u in range(2):
                    sp.dma_start(values[part(u), :, b], c.context[c.group, part(b), c.own_tiles]).then_inc(s.values, 16)

        @block.tensor
        def _(pe):
            turn_tensor(c, pe, s.ready, s, c.h)
            for t in range(HT):
                pe.wait_ge(s.turned, t + 1)
                for m, src in enumerate((c.hT, c.ctxT, c.ctxT)):
                    last = pe.matmul(c.ps[:, 7, t * 8:t * 8 + 8], src[:, tok(t)], c.w(f"L2x_g{m}"),
                                     start=(m == 0), stop=(m == 2))
                last.then_inc(s.gates_ps, 1)
            pe.wait_ge(s.turned, HT)
            for t in range(HT):
                for h in range(H4):
                    rows = slice(W * h, W * h + W)
                    for b in range(2):
                        last = pe.matmul(c.ps[part(b), h, t * S:(t + 1) * S], c.hT[rows, seq(t, b)],
                                         c.ctxT[rows, seq(t, b)], start=True, stop=True)
            last.then_inc(s.qk_ps, 1)
            pe.wait_ge(s.log_f, 1)
            for t in range(HT):
                last = pe.matmul(c.ps[:, 7, 64 + t * 4:64 + t * 4 + 4], c.w("prefix_seq"), T(3)[:, t],
                                 start=True, stop=True)
            last.then_inc(s.decay_ps, 1)
            pe.wait_ge(s.spread, 1)
            for t in range(HT):
                last = pe.matmul(c.ps[:, 4 + t // 2, (t % 2) * 256:(t % 2 + 1) * 256], c.w("same_seq"),
                                 spread[:, t].rearrange("p h k -> p (h k)"), start=True, stop=True)
            last.then_inc(s.level_ps, 1)
            pe.wait_ge(s.qk_weighted, 1)
            pe.wait_ge(s.masked, 1)
            for t in range(HT):
                for j in range(2):
                    last = pe.transpose(c.ps[:, 4 + t // 2, (2 * (t % 2) + j) * P:(2 * (t % 2) + j + 1) * P],
                                        C[:, t, 2 * j:2 * j + 2].rearrange("p h k -> p (h k)"),
                                        c.w("ident"))
                if t % 2:
                    last.then_inc(s.CT_ps, 1)
            pe.wait_ge(s.CT_ready, 2)
            pe.wait_ge(s.values, 4 * 16)
            for t in range(HT):
                for b in range(2):
                    for h in range(H4):
                        at = (2 * t + h // 2) * P + b * S
                        last = pe.matmul(c.ps[part(b), h % 2, t * P + h * W:t * P + h * W + W],
                                         CT[part(h % 2), at:at + S],
                                         values[part(h % 2), t, b, h * W:h * W + W],
                                         start=True, stop=True)
            last.then_inc(s.o_ps, 1)

        @block.scalar
        def _(act):
            turn_scalar(c, act, s, c.hT)
            act.wait_ge(s.magnitude, 1)
            act.activation(T(1), T(1), ACT.Exp).then_inc(s.exp_ready, 1)
            act.wait_ge(s.exp_ready, 1)
            act.activation(T(1), T(1), ACT.Ln, bias=1.0).then_inc(s.log_ready, 1)
            act.wait_ge(s.shifted, 1)
            act.activation(weights, weights, ACT.Exp).then_inc(s.weights_ready, 1)
            act.wait_ge(s.top, 1)
            act.activation(T(7), T(6), ACT.Exp, scale=-1.0).then_inc(s.floor_exp, 1)
            for k in range(2):
                act.wait_ge(s.CT_ps, k + 1)
                act.copy(CT[:, k * 512:(k + 1) * 512], c.ps[:, 4 + k]).then_inc(s.CT_ready, 1)

        @block.gpsimd
        def _(g):
            c.begin(g)
            norm_gpsimd(c, g, s, 1e-5)
            g.wait_ge(s.head_moments, HT * H4)
            g.tensor_scalar(eps, moments[:, :, :, 1], 1e-6, None, ALU.add).then_inc(s.head_eps, 1)
            g.wait_ge(s.head_eps, 1)
            g.tensor_tensor(rstd, eps, c.minus_half[:, 0:HT * H4].rearrange("p (t h) -> p t h", t=HT),
                            ALU.pow).then_inc(s.head_rstd, 1)

        @block.vector
        def _(v):
            norm_vector(c, v, s, c.x, c.h)
            v.wait_ge(s.gates_ps, HT)
            v.tensor_tensor(gates, c.ps[:, 7, 0:32].rearrange("p (t n) -> p t n", t=HT),
                            bcast(c.w("L2x_gb"), 1, HT), ALU.add).then_inc(s.gates_ready, 1)
            v.wait_ge(s.gates_ready, 1)
            forget, enter = gates[:, :, 4:8], gates[:, :, 0:4]
            v.scalar_tensor_tensor(out=T(1), in0=forget, scalar=-1.0, in1=forget, op0=ALU.mult, op1=ALU.min)\
                .then_inc(s.magnitude, 1)
            v.tensor_scalar(T(2), forget, 0.0, None, ALU.min).then_inc(s.floor, 1)
            v.wait_ge(s.floor, 1)
            v.wait_ge(s.log_ready, 1)
            v.tensor_tensor(T(3), T(2), T(1), ALU.subtract).then_inc(s.log_f, 1)
            v.wait_ge(s.decay_ps, 1)
            decay_ps = c.ps[:, 7, 64:80].rearrange("p (t h) -> p t h", t=HT)
            v.tensor_tensor(T(4), enter, decay_ps, ALU.subtract).then_inc(s.input, 1)
            v.wait_ge(s.input, 1)
            for t in range(HT):
                last = v.tensor_tensor(spread[:, t], bcast(T(4)[:, t], 2, S), bcast(c.w("pos_onehot"), 1, H4),
                                       ALU.mult)
            last.then_inc(s.spread, 1)
            v.wait_ge(s.level_ps, 1)
            for t in range(HT):
                last = v.tensor_tensor(weights[:, t], c.ps[:, 4 + t // 2, (t % 2) * 256:(t % 2 + 1) * 256]
                                       .rearrange("p (h k) -> p h k", k=S), bcast(c.w("causal"), 1, H4), ALU.add)
            last.then_inc(s.masked, 1)
            v.wait_ge(s.masked, 1)
            v.tensor_reduce(T(5), weights, AX.X, ALU.max).then_inc(s.max_ready, 1)
            v.wait_ge(s.max_ready, 1)
            for t in range(HT):
                last = v.tensor_tensor(weights[:, t], weights[:, t], bcast(T(5)[:, t], 2, S), ALU.subtract)
            last.then_inc(s.shifted, 1)
            v.tensor_tensor(T(6), T(5), decay_ps, ALU.add).then_inc(s.top, 1)
            v.wait_ge(s.weights_ready, 1)
            v.wait_ge(s.qk_ps, 1)
            for t in range(HT):
                last = v.scalar_tensor_tensor(out=C[:, t], in0=c.ps[:, 0:4, t * S:(t + 1) * S],
                                              scalar=W ** -0.5, in1=weights[:, t], op0=ALU.mult, op1=ALU.mult)
            last.then_inc(s.qk_weighted, 1)
            v.wait_ge(s.qk_weighted, 1)
            v.tensor_reduce(T(8), C, AX.X, ALU.add).then_inc(s.sum_ready, 1)
            v.wait_ge(s.sum_ready, 1)
            v.scalar_tensor_tensor(out=T(9), in0=T(8), scalar=-1.0, in1=T(8), op0=ALU.mult, op1=ALU.max)\
                .then_inc(s.absolute, 1)
            v.wait_ge(s.absolute, 1)
            v.wait_ge(s.floor_exp, 1)
            v.tensor_tensor(T(12), T(9), T(7), ALU.max).then_inc(s.least, 1)
            v.wait_ge(s.least, 1)
            v.tensor_scalar(T(10), T(12), 1e-6, None, ALU.add).then_inc(s.eps_added, 1)
            v.wait_ge(s.eps_added, 1)
            v.reciprocal(T(11), T(10)).then_inc(s.inv_ready, 1)
            v.wait_ge(s.inv_ready, 1)
            v.wait_ge(s.o_ps, 1)
            for t in range(HT):
                for u in range(2):
                    last = v.tensor_tensor(hs[:, t, u::2], c.ps[:, u, tok(t)]
                                           .rearrange("p (h d) -> p h d", d=W)[:, u::2],
                                           bcast(T(11)[:, t, u::2], 2, W), ALU.mult)
            last.then_inc(s.normed, 1)
            v.wait_ge(s.normed, 1)
            for t in range(HT):
                for h in range(H4):
                    v.bn_stats(stats[:, t, h], hs[:, t, h]).then_inc(s.head_stats, 1)
            for t in range(HT):
                for h in range(H4):
                    v.wait_ge(s.head_stats, t * H4 + h + 1)
                    v.bn_aggr(moments[:, t, h], stats[:, t, h]).then_inc(s.head_moments, 1)
            v.wait_ge(s.head_moments, HT * H4)
            for t in range(HT):
                last = v.tensor_tensor(hs[:, t], hs[:, t], bcast(moments[:, t, :, 0], 2, W), ALU.subtract)
            last.then_inc(s.centred, 1)
            v.wait_ge(s.centred, 1)
            v.wait_ge(s.head_rstd, 1)
            for t in range(HT):
                last = v.tensor_tensor(hs[:, t], hs[:, t], bcast(rstd[:, t], 2, W), ALU.mult)
            last.then_inc(s.scaled_heads, 1)
            v.wait_ge(s.scaled_heads, 1)
            v.tensor_tensor(c.att[:], c.att[:], bcast(c.w("L2x_on"), 1, HT), ALU.mult).then_inc(s.gained, 1)
            v.wait_ge(s.gained, 1)
            v.tensor_tensor(c.x[:], c.x[:], c.att[:], ALU.add).then_inc(s.added, 1)


def gated_mlp(c):
    nc = c.nc
    c.turn_over()
    s = signals(c, NORM + TURN + "logits_ps logits_ready top_ready less_max exps total inv prob "
                "two eps_added eps_inv factor up_ps hidden_ready down_ps y_ready added")
    T = c.tiny
    hidden = c.room(0, 2).rearrange("p (c n) -> p c n", c=HC)
    with nc.Block() as block:
        @block.tensor
        def _(pe):
            turn_tensor(c, pe, s.ready, s, c.hn)
            for t in range(HT):
                pe.wait_ge(s.turned, t + 1)
                pe.matmul(c.ps[:, 7, t * E:(t + 1) * E], c.hT[:, tok(t)], c.w("L3f_gate"), start=True,
                          stop=True).then_inc(s.logits_ps, 1)
            for j in range(HC):
                pe.matmul(c.ps[:, j], c.w("L3f_up")[:, j * P:(j + 1) * P], c.hT[:], start=True,
                          stop=True).then_inc(s.up_ps, 1)
            pe.wait_ge(s.hidden_ready, HC)
            for t in range(HT):
                for j in range(HC):
                    last = pe.matmul(c.ps[:, 4, tok(t)], hidden[:, j, tok(t)],
                                     c.w("L3f_down")[:, j * D:(j + 1) * D], start=(j == 0), stop=(j == HC - 1))
                last.then_inc(s.down_ps, 1)

        @block.scalar
        def _(act):
            turn_scalar(c, act, s, c.hT)
            act.wait_ge(s.less_max, 1)
            act.activation(T[:, :, 2], T[:, :, 2], ACT.Exp).then_inc(s.exps, 1)
            for j in range(HC):
                act.wait_ge(s.up_ps, j + 1)
                act.activation(hidden[:, j], c.ps[:, j], ACT.Silu).then_inc(s.hidden_ready, 1)

        @block.gpsimd
        def _(g):
            c.begin(g)
            norm_gpsimd(c, g, s, 1e-6, "rms")

        @block.vector
        def _(v):
            norm_vector(c, v, s, c.h, c.hn, "rms", c.w("L3f_n2"))
            v.wait_ge(s.logits_ps, HT)
            for t in range(HT):
                v.tensor_copy(T[:, t, 0], c.ps[:, 7, t * E:(t + 1) * E]).then_inc(s.logits_ready, 1)
                v.wait_ge(s.logits_ready, t + 1)
                v.max(T[:, t, 1], T[:, t, 0]).then_inc(s.top_ready, 1)
                v.wait_ge(s.top_ready, t + 1)
                last = v.tensor_scalar(T[:, t, 2], T[:, t, 1], T[:, t, 1, 0:1], None, ALU.subtract)
            last.then_inc(s.less_max, 1)
            v.wait_ge(s.exps, 1)
            v.tensor_reduce(T[:, :, 3, 0:1], T[:, :, 2], AX.X, ALU.add).then_inc(s.total, 1)
            v.tensor_reduce(T[:, :, 3, 1:2], T[:, :, 2, 0:2], AX.X, ALU.add).then_inc(s.two, 1)
            v.wait_ge(s.total, 1)
            v.reciprocal(T[:, :, 3, 2:3], T[:, :, 3, 0:1]).then_inc(s.inv, 1)
            v.wait_ge(s.inv, 1)
            v.wait_ge(s.two, 1)
            v.tensor_tensor(T[:, :, 3, 3:4], T[:, :, 3, 1:2], T[:, :, 3, 2:3], ALU.mult).then_inc(s.prob, 1)
            v.wait_ge(s.prob, 1)
            v.tensor_scalar(T[:, :, 3, 4:5], T[:, :, 3, 3:4], 1e-9, None, ALU.add).then_inc(s.eps_added, 1)
            v.wait_ge(s.eps_added, 1)
            v.reciprocal(T[:, :, 3, 5:6], T[:, :, 3, 4:5]).then_inc(s.eps_inv, 1)
            v.wait_ge(s.eps_inv, 1)
            v.tensor_tensor(T[:, :, 3, 6:7], T[:, :, 3, 3:4], T[:, :, 3, 5:6], ALU.mult).then_inc(s.factor, 1)
            v.wait_ge(s.factor, 1)
            v.wait_ge(s.down_ps, HT)
            for t in range(HT):
                v.scalar_tensor_tensor(out=c.h[:, t], in0=c.ps[:, 4, tok(t)], scalar=T[:, t, 3, 6:7],
                                       in1=c.h[:, t], op0=ALU.mult, op1=ALU.add).then_inc(s.y_ready, 1)
            v.wait_ge(s.y_ready, HT)
            v.tensor_tensor(c.x[:], c.x[:], c.h[:], ALU.add).then_inc(s.added, 1)


def prepare(c, dram_small, dram_big):
    nc = c.nc
    c.turns.half = 1
    s = signals(c, "small constants tables_ps maps_ps maps")
    with nc.Block() as block:
        @block.sync
        def _(sp):
            sp.dma_start(c.small[:], dram_small).then_inc(s.small, 16)
            sp.dma_start(c.big["L1_qkv"][:], dram_big["L1_qkv"]).then_inc(c.loaded["L1_qkv"], 16)

        @block.gpsimd
        def _(g):
            g.memset(c.minus_half[:], -0.5).then_inc(s.constants, 1)
            g.memset(c.counts[:], 0.0).then_inc(s.constants, 1)
            g.memset(c.q_apart[:].rearrange("p t m b q -> p (t m b q)"), 0.0).then_inc(s.constants, 1)
            g.memset(c.vx[:].rearrange("p t b j n -> p (t b j n)"), 0.0).then_inc(s.constants, 1)
            g.wait_ge(s.constants, 4)
            for u in range(2):
                g.memset(c.vx[part(u)].rearrange("p t b j n -> p (t b j) n")[:, :, u * 9 + HD], 1.0)\
                    .then_inc(s.constants, 1)

        @block.tensor
        def _(pe):
            pe.wait_ge(s.small, 16)
            for k in range(S):
                for b in range(2):
                    last = pe.matmul(c.ps[part(b), k // 16, (k % 16) * 32:(k % 16) * 32 + 17],
                                     c.w("distance_onehot")[:, 63 - k:127 - k], c.w("distance_table"),
                                     start=True, stop=True)
            last.then_inc(s.tables_ps, 1)
            for i, (a, b) in enumerate((("dq", "uq"), ("dkv", "uk"), ("kr", "qr"), ("dkv", "uv"))):
                last = pe.matmul(c.ps[:, 4, i * P:(i + 1) * P], c.w("L2a_" + a), c.w("L2a_" + b),
                                 start=True, stop=True)
            last.then_inc(s.maps_ps, 1)

        @block.vector
        def _(v):
            v.wait_ge(s.tables_ps, 1)
            table = c.ps[:, 0:4].rearrange("p b (k n) -> p b k n", n=32)
            by_head = c.bias0[:].rearrange("p (h k) -> p h k", k=S)
            for q in range(4):
                v.tensor_copy(by_head[:, :, q * 16:(q + 1) * 16].rearrange("p h k -> p k h"),
                              table[:, q, :, 0:HEADS])
                v.tensor_copy(c.decay3[:, q * 16:(q + 1) * 16], table[:, q, :, HEADS])
            v.wait_ge(s.maps_ps, 1)
            for i in range(3):
                v.tensor_tensor(c.q_of_h[:, i * D:(i + 1) * D], c.ps[:, 4, i * P:(i + 1) * P],
                                c.w("head_block"), ALU.mult)
            v.tensor_tensor(c.v_of_h[:], c.ps[:, 4, 3 * P:4 * P], c.w("head_block_pairs"), ALU.mult)\
                .then_inc(s.maps, 1)


def load_group(c, x_dram, ctx_dram, big_dram, i):
    nc = c.nc
    c.turn_over()
    s = signals(c, "x ctx ctxT_ps ctxT")
    with nc.Block() as block:
        @block.sync
        def _(sp):
            sp.dma_start(c.x[:], x_dram[i]).then_inc(s.x, 16)
            sp.dma_start(c.ctx_tok[:], ctx_dram[i]).then_inc(s.ctx, 16)
            sp.dma_start(c.big["L0f_w1"][:], big_dram["L0f_w1"]).then_inc(c.loaded["L0f_w1"], 16)
            sp.dma_start(c.big["L0f_w2"][:], big_dram["L0f_w2"]).then_inc(c.loaded["L0f_w2"], 16)
            sp.wait_ge(s.x, 16)
            sp.wait_ge(s.ctx, 16)

        @block.tensor
        def _(pe):
            pe.wait_ge(s.ctx, 16)
            for t in range(NT):
                pe.transpose(c.ps[:, t // 4, tok(t % 4)], c.ctx_tok[:, t], c.w("ident")).then_inc(s.ctxT_ps, 1)

        @block.scalar
        def _(act):
            act.wait_ge(s.ctxT_ps, NT)
            for k in range(NT // 4):
                act.copy(c.ctxT[:, k * 512:(k + 1) * 512], c.ps[:, k]).then_inc(s.ctxT, 1)

        @block.gpsimd
        def _(g):
            c.begin(g)


def store_group(c, out_dram, i):
    nc = c.nc
    c.turn_over()
    s = signals(c, "out")
    with nc.Block() as block:
        @block.sync
        def _(sp):
            sp.dma_start(out_dram[i], c.x[:]).then_inc(s.out, 16)
            sp.wait_ge(s.out, 16)

        @block.gpsimd
        def _(g):
            c.begin(g)


def end_group(c):
    c.turn_over()
    with c.nc.Block() as block:
        @block.gpsimd
        def _(g):
            c.begin(g)
            for s in c.per_group:
                g.sem_clear(s)


def by_halves(c, sub_layer, *options):
    for k in range(NT // HT):
        sub_layer(SomeTiles(c, k * HT, (k + 1) * HT), *options)


STAGES = {
    "L0a": lambda c: attention(c, "L0a", mode="bias", q_scale=HD ** -0.5, bias=True, out_bias=True),
    "L0x": lambda c: by_halves(c, channel_attention),
    "L0f": lambda c: by_halves(c, experts, "L0f", 2, False),
    "L1a": rotary_attention,
    "L1x": lambda c: attention(c, "L1x", "ctx", exp_scale=HD ** -0.5),
    "L1f": lambda c: by_halves(c, experts, "L1f", 1, False),
    "L2a": lambda c: attention(c, "L2a", mode="latent", exp_scale=HD ** -0.5, loads=("L2f_w1", "L2f_w3", "L2f_w2")),
    "L2x": lambda c: by_halves(c, matrix_lstm),
    "L2f": lambda c: by_halves(c, experts, "L2f", 2, True),
    "L3a": lambda c: attention(c, "L3a", mode="decay", exp_scale=HD ** -0.5, out_bias=True),
    "L3x": lambda c: by_halves(c, attention, "L3x", "ctx", "sparse", HD ** -0.5, 1.0, True, True),
    "L3f": lambda c: (attention(c, "L3f", mode="causal", exp_scale=HD ** -0.5, rms=True),
                      by_halves(c, gated_mlp)),
}


def decoder(nc, x, context, small, big, out, where, stages=tuple(STAGES), groups=NG):
    with ExitStack() as ctx:
        c = Core(nc, ctx, where, {n: a.shape for n, a in big.items()})
        c.dram = big
        c.loaded = {n: ctx.enter_context(nc.semaphore("loaded_" + n)) for n in big}
        c.per_group = [s for n, s in c.loaded.items() if n != "L1_qkv"]
        prepare(c, small, big)
        with nc.Fori(0, groups) as i:
            c.group, c.context = i, context
            load_group(c, x, context, big, i)
            for n in stages:
                STAGES[n](c)
            store_group(c, out, i)
            end_group(c)
            if c.turns.half == 0:
                end_group(c)


def kernel(**inputs):
    import concourse.bacc as bacc
    from concourse.bass_utils import run_bass_kernel_spmd

    i = {n: np.asarray(a) for n, a in inputs.items()}
    small, big = lay_out(i)
    packed, where = pack(small)
    grouped = lambda a: np.ascontiguousarray(a.reshape(NG, NT, P, D).transpose(0, 2, 1, 3))
    arrays = {"x_in": grouped(i["x"]), "ctx_in": grouped(i["ctx_1024"]), "small_in": packed}
    arrays.update({n + "_in": np.ascontiguousarray(a) for n, a in big.items()})
    nc = bacc.Bacc("TRN2", target_bir_lowering=False, num_devices=1)
    dram = {n: nc.dram_tensor(n, a.shape, F32, kind="ExternalInput").ap() for n, a in arrays.items()}
    out = nc.dram_tensor("out", (NG, P, NT, D), F32, kind="ExternalOutput").ap()
    decoder(nc, dram["x_in"], dram["ctx_in"], dram["small_in"], {n: dram[n + "_in"] for n in big}, out, where)
    got = run_bass_kernel_spmd(nc, [arrays], core_ids=[0]).results[0]["out"]
    return np.ascontiguousarray(np.asarray(got).transpose(0, 2, 1, 3)).reshape(B, S, D)
```

```python
from collections import namedtuple
from contextlib import ExitStack

import numpy as np

import concourse.bass as bass
from concourse import mybir

F32 = mybir.dt.float32
ALU = mybir.AluOpType
ACT = mybir.ActivationFunctionType
AX = mybir.AxisListType

P = 128
D = 128
B, S = 32, 64
NT = 8
HT = 4
GROUP = NT * P
NG = B * S // GROUP
HEADS, HD = 16, 8
E = 8
HID = 512
HC = HID // P
I2W, I2C = 448, 4
IC = I2W // I2C
INNER, WH = 1024, 64
XR = 33
CAPACITY = 2 * 1024 // E
SIGNALS = 64
TOP = 8
SORT_STEPS = 21
BIG = 1.0e30


def shape_constants():
    p = np.arange(P)
    q = p % S
    k = np.arange(S)
    out = {}
    out["ident"] = np.eye(P)
    out["head_of_row"] = (p[:, None] % 64 // HD == np.arange(HEADS // 2)[None]) * 1.0
    out["causal"] = np.where(k[None, :] <= q[:, None], 0.0, -BIG)
    out["head_block"] = (p[:, None] // HD == p[None, :] // HD) * 1.0
    pair, col = p // 64, p % 64
    out["head_block_pairs"] = (p[:, None] // HD == (2 * (col // HD) + pair)[None, :]) * 1.0
    m = np.arange(127)
    dist = np.clip(63 - m, -16, 16) + 16
    out["distance_onehot"] = np.pad((np.arange(XR)[:, None] == dist[None]) * 1.0, ((0, 0), (0, 1)))
    out["ones"] = np.ones((P, P))
    out["same_seq"] = (p[:, None] // S == p[None] // S) * 1.0
    out["prefix_seq"] = ((p[:, None] // S == p[None] // S) & (p[:, None] <= p[None])) * 1.0
    out["before"] = (p[:, None] < p[None]) * 1.0
    out["pos_onehot"] = (q[:, None] == k[None]) * 1.0
    out["block32"] = (p[:, None] // 32 == np.arange(4)[None]) * 1.0
    d = np.arange(P) % WH % 32
    inv = (1.0 / np.float32(10000.0) ** (2 * d.astype(np.float32) / np.float32(WH))).astype(np.float32)
    freq = (np.arange(S, dtype=np.float32)[None, :] * inv[:, None]).astype(np.float32)
    out["rope_cos"] = np.cos(freq)
    out["rope_sin"] = np.sin(freq) * np.where(np.arange(P) % WH < 32, -1.0, 1.0)[:, None]
    out["expert_index"] = np.tile(np.arange(E, dtype=np.float32)[None], (P, 1))
    out["inverse_rank"] = np.broadcast_to(1.0 / np.arange(1, S + 1), (P, S))
    return {n: np.asarray(a, np.float32) for n, a in out.items()}


def pair_columns(w):
    return w.reshape(w.shape[0], HEADS // 2, 2, HD).transpose(0, 2, 1, 3).reshape(w.shape[0], D)


def column(v):
    return v.reshape(-1, 1)


def halves(v):
    return np.tile(v.reshape(2, 64).T, (2, 1))


def row(v):
    return np.broadcast_to(v.reshape(1, -1), (P, v.size))


def blocks(w, per):
    return w.reshape(-1, per, w.shape[-1]).transpose(1, 0, 2).reshape(per, -1)


def lay_out(i):
    small, big = dict(shape_constants()), {}
    rel = np.clip(np.arange(XR) - 16, -15, 15) + 15
    small["distance_table"] = np.concatenate(
        [i["L0_attn_rel_bias"][rel], i["L3_attn_rel_emb"][np.abs(np.arange(XR) - 16)][:, None]], 1)

    def attention(name, wq, wk, wv, wo):
        small[name + "_wq"], small[name + "_wk"] = wq, wk
        small[name + "_wv"], small[name + "_wo"] = pair_columns(wv), wo

    a = "L0_attn_"
    attention("L0a", i[a + "Wq"].T, i[a + "Wk"].T, i[a + "Wv"].T, i[a + "Wo"].T)
    small["L0a_bq"], small["L0a_bk"] = halves(i[a + "bq"]), halves(i[a + "bk"])
    small["L0a_bv"] = column(i[a + "bv"])
    small["L0a_bo"] = row(i[a + "bo"])
    a = "L0_xattn_"
    for s in "gl":
        small["L0x_wq" + s], small["L0x_bq" + s] = row(i[a + "wq" + s]), row(i[a + "bq" + s])
        small["L0x_wk" + s], small["L0x_bk" + s] = row(i[a + "wk" + s]), row(i[a + "bk" + s])
        small["L0x_wv" + s], small["L0x_bv" + s] = column(i[a + "wv" + s]), column(i[a + "bv" + s])
    small["L0x_wp"], small["L0x_bp"] = row(i[a + "wp"]), row(i[a + "bp"])
    small["L0f_wr"] = i["L0_ffn_Wr"]
    small["L0f_b1"] = i["L0_ffn_b1"].reshape(E * HC, P).T
    small["L0f_b2"] = i["L0_ffn_b2"]
    small["L1_wo1"] = blocks(i["L1_attn_W_o1"], P)
    small["L1_wo2"] = i["L1_attn_W_o2"]
    small["L1_gamma"] = row(i["L1_attn_gamma"])
    a = "L1_xattn_W_"
    attention("L1x", i[a + "q"].T, i[a + "k"].T, i[a + "v"].T, i[a + "o"].T)
    small["L1f_gate"] = i["L1_ffn_gate_weight"].T
    small["L1f_gamma"], small["L1f_beta"] = row(i["L1_ffn_ln_gamma"]), row(i["L1_ffn_ln_beta"])
    a = "L2_attn_W_"
    tile16 = lambda w: np.tile(w, (1, HEADS))
    small["L2a_dq"], small["L2a_uq"] = tile16(i[a + "DQ"]), tile16(i[a + "UQ"].T)
    small["L2a_dkv"] = tile16(i[a + "DKV"])
    small["L2a_uk"], small["L2a_uv"] = tile16(i[a + "UKV"][:HD].T), tile16(i[a + "UKV"][HD:].T)
    small["L2a_kr"], small["L2a_qr"] = tile16(i[a + "KR"]), tile16(i[a + "QR"])
    wo = np.zeros((D, D), np.float32)
    for h in range(HEADS):
        wo[h * HD:(h + 1) * HD, h * HD:(h + 1) * HD] = i[a + "O"].T
    small["L2a_wo"] = wo
    small["L2a_qn"] = column(np.tile(i["L2_attn_q_norm_w"], HEADS))
    small["L2a_kn"] = row(np.tile(i["L2_attn_k_norm_w"], HEADS))
    a = "L2_xattn_"
    for n in range(3):
        small[f"L2x_g{n}"] = np.concatenate(
            [i[a + "igate_kernel"][n * D:(n + 1) * D], i[a + "fgate_kernel"][n * D:(n + 1) * D]], 1)
    small["L2x_gb"] = row(np.concatenate([i[a + "igate_bias"], i[a + "fgate_bias"]]))
    small["L2x_on"] = row(i[a + "outnorm_scale"])
    small["L2f_rms"], small["L2f_gate"] = row(i["L2_ffn_rms_weight"]), i["L2_ffn_gate_w"].T
    a = "L3_attn_"
    attention("L3a", i[a + "Wq"], i[a + "Wk"], i[a + "Wv"], i[a + "Wo"])
    small["L3a_bo"] = row(i[a + "bo"])
    a = "L3_xattn_"
    attention("L3x", i[a + "Wq"], i[a + "Wk"], i[a + "Wv"], i[a + "Wo"])
    small["L3x_bq"], small["L3x_bk"] = halves(i[a + "bq"]), halves(i[a + "bk"])
    small["L3x_bv"] = column(i[a + "bv"])
    small["L3x_bo"] = row(i[a + "bo"])
    a = "L3_ffn_"
    w = i[a + "qkv_w"].T
    attention("L3f", w[:, :D], w[:, D:2 * D], w[:, 2 * D:], i[a + "o_w"].T)
    small["L3f_n1"], small["L3f_n2"] = row(i[a + "n1_w"]), row(i[a + "n2_w"])
    small["L3f_gate"], small["L3f_up"] = i[a + "gate_w"].T, i[a + "up_w"].T
    small["L3f_down"] = blocks(i[a + "down_w"].T, P)

    big["L0f_w1"] = np.ascontiguousarray(i["L0_ffn_W1"].transpose(1, 0, 2)).reshape(P, -1)
    big["L0f_w2"] = blocks(i["L0_ffn_W2"].reshape(-1, D), P)
    w = i["L1_attn_W_qkv"]
    turned = w[:, :2 * INNER].reshape(D, 2 * HEADS, 2, 32)[:, :, ::-1].reshape(D, 2 * INNER)
    v = w[:, 2 * INNER:].reshape(D, HEADS // 4, 2, 2, WH).transpose(0, 2, 1, 3, 4).reshape(D, INNER)
    big["L1_qkv"] = np.concatenate([w[:, :2 * INNER], turned, v], 1)
    big["L1f_w1"] = np.ascontiguousarray(i["L1_ffn_wi"].transpose(1, 0, 2)).reshape(P, -1)
    big["L1f_w2"] = blocks(i["L1_ffn_wo"].reshape(-1, D), P)
    big["L2f_w1"] = np.ascontiguousarray(i["L2_ffn_w1"].transpose(2, 0, 1)).reshape(P, -1)
    big["L2f_w3"] = np.ascontiguousarray(i["L2_ffn_w3"].transpose(2, 0, 1)).reshape(P, -1)
    big["L2f_w2"] = blocks(np.ascontiguousarray(i["L2_ffn_w2"].transpose(0, 2, 1)).reshape(-1, D), IC)
    return small, big


FIRST = ("distance_onehot", "distance_table", "L2a_dq", "L2a_uq", "L2a_dkv", "L2a_uk", "L2a_kr", "L2a_qr",
         "L2a_uv", "head_block", "head_block_pairs", "L2x_g1", "L2x_g2")


def pack(arrays):
    at, where, parts = 0, {}, []
    for name in FIRST + tuple(n for n in arrays if n not in FIRST):
        a = arrays[name]
        where[name] = (at, a.shape[1], a.shape[0])
        parts.append(np.pad(a, ((0, P - a.shape[0]), (0, 0))))
        at += a.shape[1]
    return np.ascontiguousarray(np.concatenate(parts, 1)), where


def signals(core, names):
    words = names.split()
    turns = core.turns
    first = turns.taken
    turns.taken += len(words)
    return namedtuple("Signals", words)(*core.halves[turns.half][first:turns.taken])


class Turns:
    half, taken = 1, 0


class Core:

    def __init__(self, nc, ctx, where, big):
        self.nc, self.ctx, self.where = nc, ctx, where
        self.halves = [[ctx.enter_context(nc.semaphore(f"signal_{h}_{i}")) for i in range(SIGNALS)]
                       for h in range(2)]
        self.turns = Turns()
        self.small = self.buf("small", [P, max(a + n for a, n, _ in where.values())])
        self.big = {"L1_qkv": self.buf("L1_qkv", big["L1_qkv"])}
        layers = [[n for n in big if n[:3] == layer] for layer in ("L0f", "L1f", "L2f")]
        place = self.buf("experts_weights", [P, max(sum(big[n][1] for n in layer) for layer in layers)])
        for layer in layers:
            at = 0
            for n in layer:
                rows, cols = big[n]
                self.big[n] = place[0:rows, at:at + cols]
                at += cols
        self.experts_place = place
        self.nt, self.own_tiles = NT, slice(0, NT)
        self.x = self.buf("x", [P, NT, D])
        self.h = self.buf("h", [P, NT, D])
        self.hn = self.buf("hn", [P, NT, D])
        self.hT = self.buf("hT", [P, GROUP])
        self.ctx_tok = self.buf("ctx_tok", [P, NT, D])
        self.ctxT = self.buf("ctxT", [P, GROUP])
        self.q_apart = self.buf("q_apart", [P, NT, 2, 2, S])
        self.scaled_bias = self.buf("scaled_bias", [P, 2])
        self.oT = self.buf("oT", [P, GROUP])
        self.att = self.buf("att", [P, NT, D])
        self.norm_places = [(self.buf(f"stats_{k}", [P, NT, 6]), self.buf(f"moments_{k}", [P, NT, 2]),
                             self.buf(f"var_eps_{k}", [P, NT]), self.buf(f"rstd_{k}", [P, NT]))
                            for k in range(2)]
        self.stats, self.moments, self.var_eps, self.rstd = self.norm_places[0]
        self.row_max = self.buf("row_max", [P, NT, HEADS])
        self.row_inv = self.buf("row_inv", [P, NT, HEADS])
        self.bias0 = self.buf("bias0", [P, HEADS * S])
        self.decay3 = self.buf("decay3", [P, S])
        self.vx = self.buf("vx", [P, NT, 2, HEADS // 2, 2 * (HD + 1)])
        self.minus_half = self.buf("minus_half", [P, 2 * HEADS])
        self.q_of_h = self.buf("q_of_h", [P, 3 * D])
        self.gate_of_ctx = self.buf("gate_of_ctx", [P, 8])
        self.v_of_h = self.buf("v_of_h", [P, D])
        self.counts = self.buf("counts", [P, E])
        self.tiny = self.buf("tiny", [P, NT, 16, E])
        self.row_open = self.buf("row_open", [P, 1])
        self.count_open = self.ctx.enter_context(nc.sbuf_tensor("count_open", [1, 1], mybir.dt.int32))
        self.index = self.ctx.enter_context(nc.sbuf_tensor("index", [P, NT, E], mybir.dt.uint32))
        self.arena = self.buf("arena", [P, 9 * HEADS * S])
        self.ps = ctx.enter_context(nc.psum_tensor("ps", [P, 8, 512], F32))

    def turn_over(self):
        self.turns.half, self.turns.taken = 1 - self.turns.half, 0

    def begin(self, g):
        last = self.halves[1 - self.turns.half]
        g.sem_clear(range(last[0].num, last[-1].num + 1))

    def buf(self, name, shape):
        return self.ctx.enter_context(self.nc.sbuf_tensor(name, shape, F32))

    def w(self, name):
        at, n, rows = self.where[name]
        return self.small[0:rows, at:at + n]

    def room(self, k, n=1):
        return self.arena[:, k * 1024:(k + n) * 1024]


class SomeTiles(Core):

    def __init__(self, c, first, end):
        own, columns = slice(first, end), slice(first * P, end * P)
        self.nt, self.own_tiles = end - first, own
        self.nc, self.where, self.small, self.big, self.ps = c.nc, c.where, c.small, c.big, c.ps
        self.halves, self.turns, self.loaded = c.halves, c.turns, c.loaded
        self.group, self.context, self.arena = c.group, c.context, c.arena
        self.bias0, self.decay3, self.minus_half, self.counts = c.bias0, c.decay3, c.minus_half, c.counts
        self.scaled_bias, self.row_open, self.count_open = c.scaled_bias, c.row_open, c.count_open
        self.x, self.h, self.hn, self.att = c.x[:, own], c.h[:, own], c.hn[:, own], c.att[:, own]
        self.ctx_tok, self.vx, self.q_apart = c.ctx_tok[:, own], c.vx[:, own], c.q_apart[:, own]
        self.hT, self.ctxT, self.oT = c.hT[:, columns], c.ctxT[:, columns], c.oT[:, columns]
        self.norm_places = [[a[:, own] for a in places] for places in c.norm_places]
        self.stats, self.moments, self.var_eps, self.rstd = self.norm_places[0]
        self.row_max, self.row_inv = c.row_max[:, own], c.row_inv[:, own]
        self.tiny, self.index = c.tiny[:, own], c.index[:, own]


def bcast(ap, dim, n):
    ap = ap.unsqueeze(dim)
    shape = list(ap.shape)
    shape[dim] = n
    return ap.to_broadcast(shape)


def tok(t):
    return slice(t * P, (t + 1) * P)


def seq(t, b):
    return slice(t * P + b * S, t * P + (b + 1) * S)


def part(b):
    return slice(b * 64, (b + 1) * 64)


NORM = "stats moments square var_eps rstd scaled weighted ready "


def norm_vector(c, v, s, src, dst, kind="mean", weight=None, shift=None):
    for t in range(c.nt):
        v.bn_stats(c.stats[:, t], src[:, t]).then_inc(s.stats, 1)
    for t in range(c.nt):
        v.wait_ge(s.stats, t + 1)
        v.bn_aggr(c.moments[:, t], c.stats[:, t]).then_inc(s.moments, 1)
    v.wait_ge(s.moments, c.nt)
    v.wait_ge(s.rstd, 1)
    for t in range(c.nt):
        if kind == "rms":
            v.scalar_tensor_tensor(out=dst[:, t], in0=src[:, t], scalar=c.rstd[:, t:t + 1], in1=weight,
                                   op0=ALU.mult, op1=ALU.mult).then_inc(s.ready, 1)
            continue
        v.tensor_scalar(dst[:, t], src[:, t], c.moments[:, t, 0:1], c.rstd[:, t:t + 1],
                        ALU.subtract, ALU.mult).then_inc(s.scaled, 1)
        if t % 4 == 3:
            tiles, done = slice(t - 3, t + 1), t // 4 + 1
            v.wait_ge(s.scaled, t + 1)
            v.tensor_tensor(dst[:, tiles], dst[:, tiles], bcast(weight, 1, 4), ALU.mult).then_inc(s.weighted, 1)
            v.wait_ge(s.weighted, done)
            v.tensor_tensor(dst[:, tiles], dst[:, tiles], bcast(shift, 1, 4), ALU.add).then_inc(s.ready, 4)


def norm_gpsimd(c, g, s, eps, kind="mean"):
    mean, var = c.moments[:, :, 0], c.moments[:, :, 1]
    g.wait_ge(s.moments, c.nt)
    if kind == "rms":
        g.tensor_tensor(c.rstd[:], mean, mean, ALU.mult).then_inc(s.square, 1)
        g.wait_ge(s.square, 1)
        g.tensor_tensor(c.rstd[:], c.rstd[:], var, ALU.add).then_inc(s.square, 1)
        g.wait_ge(s.square, 2)
        var = c.rstd[:]
    g.tensor_scalar(c.var_eps[:], var, eps, None, ALU.add).then_inc(s.var_eps, 1)
    g.wait_ge(s.var_eps, 1)
    g.tensor_tensor(c.rstd[:], c.var_eps[:], c.minus_half[:, 0:c.nt], ALU.pow).then_inc(s.rstd, 1)


UNIT_NORM = "stats moments var_eps rstd normed"


def unit_norm(c, k):
    places = c.norm_places[k]
    names = ["stats_of", "moments_of", "var_eps_of", "rstd_of"] + UNIT_NORM.split()
    return namedtuple("UnitNorm", names)(*places, *signals(c, UNIT_NORM))


def measure(v, m, src, u, n=1):
    for t in range(u * n, u * n + n):
        v.bn_stats(m.stats_of[:, t], src[:, t]).then_inc(m.stats, 1)
    for t in range(u * n, u * n + n):
        v.wait_ge(m.stats, t + 1)
        v.bn_aggr(m.moments_of[:, t], m.stats_of[:, t]).then_inc(m.moments, 1)


def invert(c, g, m, u, n=1):
    own = slice(u * n, u * n + n)
    g.wait_ge(m.moments, u * n + n)
    g.tensor_scalar(m.var_eps_of[:, own], m.moments_of[:, own, 1], 1e-5, None, ALU.add).then_inc(m.var_eps, 1)
    g.wait_ge(m.var_eps, u + 1)
    g.tensor_tensor(m.rstd_of[:, own], m.var_eps_of[:, own], c.minus_half[:, 0:n], ALU.pow).then_inc(m.rstd, 1)


def scale(v, m, src, dst, u, n=1):
    v.wait_ge(m.rstd, u + 1)
    for t in range(u * n, u * n + n):
        v.tensor_scalar(dst[:, t], src[:, t], m.moments_of[:, t, 0:1], m.rstd_of[:, t:t + 1],
                        ALU.subtract, ALU.mult).then_inc(m.normed, 1)


TURN = "turned_ps turned "


def turn_tensor(c, pe, ready, s, src, half=0, bank_free=None):
    for t in range(4 * half, 4 * half + 4):
        if ready is not None:
            pe.wait_ge(ready, t + 1)
        if half > 0:
            pe.wait_ge(bank_free, t - 3)
        pe.transpose(c.ps[:, t % 4, 0:P], src[:, t], c.w("ident")).then_inc(s.turned_ps, 1)


def turn_scalar(c, act, s, dst, half=0):
    for t in range(4 * half, 4 * half + 4):
        act.wait_ge(s.turned_ps, t + 1)
        act.copy(dst[:, tok(t)], c.ps[:, t % 4, 0:P]).then_inc(s.turned, 1)


def attention(c, n, keys_from="h", mode="plain", q_scale=1.0, exp_scale=1.0, bias=False,
              out_bias=False, rms=False, loads=()):
    nc, nt = c.nc, c.nt
    c.turn_over()
    s = signals(c, TURN + "k_ps v_ps q_ready kx_ready vx_ready scores_ps factored scored "
                "max_ready shifted probs_ready probsT_ps probsT_ready o_ps inv_ready att_ready oT_ps "
                "oT_ready y_ps y_added biased values_read qk_read bias_scaled")
    if rms:
        r = signals(c, NORM)
    else:
        following = unit_norm(c, 1)
    if mode == "latent":
        l = signals(c, "maps_ps copied squared sums means root step q_normed k_normed k_weighted "
                    "keys_ready")
    if mode == "sparse":
        sp = signals(c, "row_starts top less_max summed candidates tau compared row_open open_ps count_open step "
                     "shifted_tau less_tau")
    kvT = c.hT if keys_from == "h" else c.ctxT
    kc = c.room(2)[:, 0:nt * P].rearrange("p (t m k) -> p t m k", t=nt, m=2)
    kx = lambda t: c.room(t % 2)
    if mode == "sparse":
        places = [c.room(k) for k in (3, 4, 5, 8)]
        places += [c.experts_place[:, k * 1024:(k + 1) * 1024] for k in range(nt - 4)]
        buf = lambda t: places[t]
    else:
        buf = lambda t: c.room(3 + t % 3)
    probsT = lambda t: c.room(6 + t % 2)
    of_tiles = lambda half, k: c.tiny[:, 4 * half:4 * half + 4, 4 * k:4 * k + 4].rearrange("p t a b -> p t (a b)")
    sums, rms_of = (lambda t: of_tiles(t // 4, 0)[:, t % 4]), (lambda t: of_tiles(t // 4, 1)[:, t % 4])
    squares = lambda t: c.room(5)[:, (t % 4) * 256:(t % 4 + 1) * 256]
    scores_ps = lambda t: c.ps[:, 2 * (t % 2):2 * (t % 2) + 2].rearrange("p m n -> p (m n)")
    q_ps = lambda t: c.ps[:, 4 + t % 4, 0:P]
    k_ps = lambda t: c.ps[:, 4 + t % 4, P:2 * P]
    qk_ps = lambda half, k: c.ps[:, 4 + 2 * half + k].rearrange("p (m t q) -> p m t q", m=2, t=4)
    maps_ps = lambda t: c.ps[:, 4 + t % 4, 0:3 * D]
    maps = lambda t: c.room(3 + t % 4 // 2)[:, (t % 2) * 512:(t % 2) * 512 + 3 * D]
    o_ps = lambda t: c.ps[:, 6 + t % 2, 0:144]
    oT_ps = lambda t: c.ps[:, 6 + t % 2, 256:256 + P]
    y_ps = lambda t: c.ps[:, 6 + t % 2, 384:384 + P]
    heads = lambda a: a.rearrange("p (h d) -> p h d", d=HD)
    scores_read = s.shifted if mode == "plain" else s.factored if mode == "decay" else s.scored
    probs_ready = s.probs_ready

    lag = 1 if mode in ("sparse", "bias") else 2
    with nc.Block() as block:
        if loads:
            @block.sync
            def _(sp):
                for m in ("L1f_w1", "L1f_w2"):
                    sp.wait_ge(c.loaded[m], 16)
                for m in loads:
                    sp.dma_start(c.big[m][:], c.dram[m]).then_inc(c.loaded[m], 16)

        @block.tensor
        def _(pe):
            for half in range(nt // 4):
                tiles = range(4 * half, 4 * half + 4)
                turn_tensor(c, pe, r.ready if rms else None, s, c.hn if rms else c.h, half,
                            s.values_read)
                if mode != "latent":
                    pe.wait_ge(s.turned, 4 * half + 4)
                    own = slice(512 * half, 512 * half + 512)
                    for k, w, src in ((0, "_wq", c.hT), (1, "_wk", kvT)):
                        of_seq = src[:, own].rearrange("p (t b q) -> p t b q", t=4, b=2)
                        for b in range(2):
                            for m in range(2):
                                last = pe.matmul(qk_ps(half, k)[part(b), m], c.w(n + w)[:, part(m)],
                                                 of_seq[:, :, b], start=True, stop=True)
                    last.then_inc(s.k_ps, 1)
                for t in tiles:
                    pe.wait_ge(s.turned, t + 1)
                    if mode == "latent":
                        if t >= 4:
                            pe.wait_ge(s.qk_read, t - 3)
                        pe.matmul(maps_ps(t), c.hT[:, tok(t)], c.q_of_h[:], start=True, stop=True)\
                            .then_inc(l.maps_ps, 1)
                    wv = c.v_of_h[:] if mode == "latent" else c.w(n + "_wv")
                    for b in range(2):
                        for u in range(2):
                            last = pe.matmul(c.ps[part(u), t % 4, part(b)], kvT[:, seq(t, b)],
                                             wv[:, part(u)], start=True, stop=True)
                    last.then_inc(s.v_ps, 1)
                if mode == "latent":
                    for t in tiles:
                        pe.wait_ge(l.q_normed, t + 1)
                        pe.wait_ge(l.keys_ready, t + 1)
                        for at, src in ((0, c.att), (P, c.hn)):
                            for b in range(2):
                                for m in range(2):
                                    cols = slice(at + m * S, at + m * S + S)
                                    last = pe.matmul(c.ps[part(b), 4 + t % 4, cols], src[part(b), t, part(m)],
                                                     c.w("ident")[part(b), part(b)], start=True, stop=True)
                        last.then_inc(s.k_ps, 1)

            def scores(t):
                pe.wait_ge(s.q_ready, t + 1)
                pe.wait_ge(s.kx_ready, t + 1)
                if t < 2:
                    pe.wait_ge(s.values_read, nt - 2 + 2 * t)
                else:
                    pe.wait_ge(scores_read, t - 1)
                for m in range(2):
                    last = pe.matmul(c.ps[:, 2 * (t % 2) + m], c.q_apart[:, t, m].rearrange("p b q -> p (b q)"),
                                     kx(t)[:, m * 512:(m + 1) * 512], start=True, stop=True)
                last.then_inc(s.scores_ps, 1)

            def turn_probs(t):
                pe.wait_ge(probs_ready, t + 1)
                if t == 0:
                    pe.wait_ge(s.qk_read, nt - 2)
                for k in range(2):
                    if t >= 1:
                        pe.wait_ge(s.probsT_ready, 2 * (t - 1) + k + 1)
                    for j in range(4):
                        last = pe.transpose(c.ps[:, 4 + k, j * P:(j + 1) * P],
                                            buf(t)[:, (4 * k + j) * P:(4 * k + j + 1) * P], c.w("ident"))
                    last.then_inc(s.probsT_ps, 1)

            def weigh_values(t):
                if t == 0:
                    pe.wait_ge(s.qk_read, nt)
                if t >= 2:
                    pe.wait_ge(s.y_added, t - 1)
                pe.wait_ge(s.probsT_ready, 2 * t + 2)
                for j in range(HEADS // 2):
                    for b in range(2):
                        last = pe.matmul(o_ps(t)[part(b), j * 18:(j + 1) * 18],
                                         probsT(t)[:, seq(j, b)], c.vx[:, t, b, j], start=True, stop=True)
                last.then_inc(s.o_ps, 1)

            def turn_output(t):
                pe.wait_ge(s.att_ready, t + 1)
                pe.transpose(oT_ps(t), c.att[:, t], c.w("ident")).then_inc(s.oT_ps, 1)

            def project(t):
                pe.wait_ge(s.oT_ready, t + 1)
                pe.matmul(y_ps(t), c.oT[:, tok(t)], c.w(n + "_wo"), start=True, stop=True)\
                    .then_inc(s.y_ps, 1)

            if mode == "sparse":
                for t in range(nt):
                    scores(t)
                pe.wait_ge(s.qk_read, nt)
                pe.wait_ge(sp.row_open, 1)
                pe.matmul(c.ps[0:1, 7, 0:1], c.row_open[:], c.w("ones")[:, 0:1], start=True, stop=True)\
                    .then_inc(sp.open_ps, 1)
            for k in range(nt + lag + 2):
                if k < nt and mode != "sparse":
                    scores(k)
                if 0 <= k - lag < nt:
                    turn_probs(k - lag)
                if 0 <= k - lag - 2 < nt:
                    turn_output(k - lag - 2)
                if 0 <= k - lag - 1 < nt:
                    weigh_values(k - lag - 1)
                if 0 <= k - lag - 2 < nt:
                    project(k - lag - 2)

        @block.scalar
        def _(act):
            def take_values(t):
                act.wait_ge(s.v_ps, t + 1)
                for u in range(2):
                    act.copy(c.vx[part(u), t, :, :, u * 9:u * 9 + HD],
                             c.ps[part(u), t % 4, 0:P].rearrange("p (b j d) -> p b j d", b=2, d=HD))\
                        .then_inc(s.vx_ready if u == 0 else s.values_read, 1)

            def take_maps(t):
                act.wait_ge(l.maps_ps, t + 1)
                if t >= 4:
                    act.wait_ge(l.keys_ready, t - 3)
                act.copy(maps(t), maps_ps(t)).then_inc(l.copied, 1)
                act.wait_ge(l.copied, t + 1)
                act.activation(squares(t), maps(t)[:, 0:2 * D], ACT.Square).then_inc(l.squared, 1)

            def take_queries_and_keys(half):
                tiles = slice(4 * half, 4 * half + 4)
                act.wait_ge(s.k_ps, half + 1)
                queries, keys = qk_ps(half, 0), qk_ps(half, 1)
                if bias:
                    act.wait_ge(s.bias_scaled, 1)
                    for m in range(2):
                        for b in range(2):
                            last = act.activation(c.q_apart[part(b), tiles, m, b], queries[part(b), m], ACT.Identity,
                                                  bias=c.scaled_bias[part(b), m:m + 1], scale=q_scale)
                    last.then_inc(s.q_ready, 4)
                    for m in range(2):
                        last = act.activation(kc[:, tiles, m], keys[:, m], ACT.Identity,
                                              bias=c.w(n + "_bk")[:, m:m + 1])
                    last.then_inc(s.qk_read, 4)
                    return
                for b in range(2):
                    last = act.copy(c.q_apart[part(b), tiles, :, b], queries[part(b)].rearrange("p m t q -> p t m q"))
                last.then_inc(s.q_ready, 4)
                act.copy(kc[:, tiles], keys.rearrange("p m t k -> p t m k")).then_inc(s.qk_read, 4)

            def take_latent(t):
                halves_of = lambda a: a.rearrange("p (m k) -> p m k", m=2)
                act.wait_ge(s.k_ps, t + 1)
                for b in range(2):
                    last = act.activation(c.q_apart[part(b), t, :, b], halves_of(q_ps(t)[part(b)]), ACT.Identity,
                                          scale=c.w("L2a_qn")[part(b)])
                last.then_inc(s.q_ready, 1)
                act.copy(kc[:, t], halves_of(k_ps(t))).then_inc(s.qk_read, 1)

            for half in range(nt // 4):
                turn_scalar(c, act, s, c.hT, half)
                if mode != "latent":
                    take_queries_and_keys(half)
                for t in range(4 * half, 4 * half + 4):
                    take_values(t)
                    if mode == "latent":
                        take_maps(t)
                if mode == "latent":
                    act.wait_ge(l.means, half + 1)
                    act.activation(of_tiles(half, 1), of_tiles(half, 0), ACT.Sqrt).then_inc(l.root, 1)
                    for t in range(4 * half, 4 * half + 4):
                        take_latent(t)
            if mode == "sparse":
                for t in range(nt):
                    act.wait_ge(s.scores_ps, t + 1)
                    act.copy(buf(t), scores_ps(t)).then_inc(s.scored, 1)
            def weights(k):
                if mode == "sparse":
                    act.wait_ge(sp.less_tau, k + 1)
                else:
                    act.wait_ge(s.shifted, k + 1)
                act.activation(buf(k), buf(k), ACT.Relu if mode == "sparse" else ACT.Exp,
                               scale=exp_scale).then_inc(s.probs_ready, 1)

            for k in range(nt + lag + 2):
                if k < nt and mode == "sparse":
                    weights(k)
                t = k - lag
                if 0 <= t < nt:
                    for j in range(2):
                        act.wait_ge(s.probsT_ps, 2 * t + j + 1)
                        if t >= 2:
                            act.wait_ge(s.o_ps, t - 1)
                        act.copy(probsT(t)[:, j * 512:(j + 1) * 512], c.ps[:, 4 + j])\
                            .then_inc(s.probsT_ready, 1)
                t = k - lag - 2
                if 0 <= t < nt:
                    act.wait_ge(s.oT_ps, t + 1)
                    if bias:
                        act.activation(c.oT[:, tok(t)], oT_ps(t), ACT.Identity, bias=c.w(n + "_bv"))\
                            .then_inc(s.oT_ready, 1)
                    else:
                        act.copy(c.oT[:, tok(t)], oT_ps(t)).then_inc(s.oT_ready, 1)
                if k < nt and mode != "sparse":
                    weights(k)

        @block.gpsimd
        def _(g):
            c.begin(g)
            if bias:
                g.tensor_scalar(c.scaled_bias[:], c.w(n + "_bq"), q_scale, None, ALU.mult)\
                    .then_inc(s.bias_scaled, 1)
            if rms:
                norm_gpsimd(c, g, r, 1e-6, "rms")
            if mode == "sparse":
                row_starts = c.room(6)[:, 0:nt * HEADS * TOP]
                g.memset(row_starts, 1.0).then_inc(sp.row_starts, 1)
                g.wait_ge(sp.row_starts, 1)
                g.memset(row_starts.rearrange("p (r k) -> p r k", k=TOP)[:, :, 0], 0.0)\
                    .then_inc(sp.row_starts, 1)

            def spread_keys(t):
                g.wait_ge(s.qk_read, t + 1)
                if t >= 2:
                    g.wait_ge(s.scores_ps, t - 1)
                g.tensor_tensor(kx(t).rearrange("p (m h k) -> p m h k", m=2, k=S), bcast(kc[:, t], 2, HEADS // 2),
                                bcast(bcast(c.w("head_of_row"), 2, S), 1, 2), ALU.mult)\
                    .then_inc(s.kx_ready, 1)

            behind = nt if mode == "sparse" else lag + 3
            for k in range(nt + behind):
                if k < nt:
                    spread_keys(k)
                if not rms and 0 <= k - behind < nt:
                    invert(c, g, following, k - behind)

        @block.vector
        def _(v):
            if rms:
                norm_vector(c, v, r, c.h, c.hn, "rms", c.w(n + "_n1"))
            for half in range(nt // 4 if mode == "latent" else 0):
                tiles = range(4 * half, 4 * half + 4)
                for t in tiles:
                    v.wait_ge(l.squared, t + 1)
                    v.tensor_reduce(sums(t), heads(squares(t)), AX.X, ALU.add).then_inc(l.sums, 1)
                mean, inv, work = (of_tiles(half, k) for k in range(3))
                v.wait_ge(l.sums, 4 * half + 4)
                v.tensor_scalar(mean, mean, 1.0 / HD, 1.1920929e-07, ALU.mult, ALU.add).then_inc(l.means, 1)
                v.wait_ge(l.root, half + 1)
                v.reciprocal(inv, inv).then_inc(l.step, 1)
                v.wait_ge(l.step, 5 * half + 1)
                v.tensor_tensor(work, mean, inv, ALU.mult).then_inc(l.step, 1)
                v.wait_ge(l.step, 5 * half + 2)
                v.tensor_tensor(work, work, inv, ALU.mult).then_inc(l.step, 1)
                v.wait_ge(l.step, 5 * half + 3)
                v.tensor_scalar(work, work, -0.5, 1.5, ALU.mult, ALU.add).then_inc(l.step, 1)
                v.wait_ge(l.step, 5 * half + 4)
                v.tensor_tensor(inv, inv, work, ALU.mult).then_inc(l.step, 1)
                v.wait_ge(l.step, 5 * half + 5)
                for t in tiles:
                    keys = c.hn[:, t]
                    v.tensor_tensor(heads(c.att[:, t]), heads(maps(t)[:, 0:D]),
                                    bcast(rms_of(t)[:, 0:HEADS], 2, HD), ALU.mult).then_inc(l.q_normed, 1)
                    v.tensor_tensor(heads(keys), heads(maps(t)[:, D:2 * D]),
                                    bcast(rms_of(t)[:, HEADS:2 * HEADS], 2, HD), ALU.mult)\
                        .then_inc(l.k_normed, 1)
                    v.wait_ge(l.k_normed, t + 1)
                    v.tensor_tensor(keys, keys, c.w("L2a_kn"), ALU.mult).then_inc(l.k_weighted, 1)
                    v.wait_ge(l.k_weighted, t + 1)
                    v.tensor_tensor(keys, keys, maps(t)[:, 2 * D:3 * D], ALU.add).then_inc(l.keys_ready, 1)

            def shift(t):
                shaped = buf(t).rearrange("p (h k) -> p h k", k=S)
                if t >= 3:
                    v.wait_ge(s.probsT_ps, 2 * (t - 2))
                ps = scores_ps(t).rearrange("p (h k) -> p h k", k=S)
                v.wait_ge(s.scores_ps, t + 1)
                if mode == "bias":
                    v.tensor_tensor(buf(t), scores_ps(t), c.bias0[:], ALU.add).then_inc(s.scored, 1)
                elif mode == "decay":
                    v.tensor_tensor(shaped, ps, bcast(c.decay3[:], 1, HEADS), ALU.mult).then_inc(s.factored, 1)
                    v.wait_ge(s.factored, t + 1)
                    v.tensor_tensor(shaped, shaped, bcast(c.w("causal"), 1, HEADS), ALU.add)\
                        .then_inc(s.scored, 1)
                elif mode != "plain":
                    v.tensor_tensor(shaped, ps, bcast(c.w("causal"), 1, HEADS), ALU.add).then_inc(s.scored, 1)
                src = ps
                if mode != "plain":
                    src = shaped
                    v.wait_ge(s.scored, t + 1)
                v.tensor_reduce(c.row_max[:, t], src, AX.X, ALU.max).then_inc(s.max_ready, 1)
                v.wait_ge(s.max_ready, t + 1)
                v.tensor_tensor(shaped, src, bcast(c.row_max[:, t], 2, S), ALU.subtract).then_inc(s.shifted, 1)

            def normalise(t):
                o = o_ps(t).rearrange("p (h d) -> p h d", d=HD + 1)
                v.wait_ge(s.o_ps, t + 1)
                v.reciprocal(c.row_inv[:, t], o[:, :, HD]).then_inc(s.inv_ready, 1)
                v.wait_ge(s.inv_ready, t + 1)
                v.tensor_tensor(heads(c.att[:, t]), o[:, :, 0:HD], bcast(c.row_inv[:, t], 2, HD),
                                ALU.mult).then_inc(s.att_ready, 1)

            def add(t):
                x = c.h if rms else c.x
                v.wait_ge(s.y_ps, t + 1)
                v.tensor_tensor(x[:, t], x[:, t], y_ps(t), ALU.add).then_inc(s.y_added, 1)
                if out_bias:
                    v.wait_ge(s.y_added, t + 1)
                    v.tensor_tensor(x[:, t], x[:, t], c.w(n + "_bo"), ALU.add).then_inc(s.biased, 1)

            def less_threshold(t):
                shaped = buf(t).rearrange("p (h k) -> p h k", k=S)
                v.tensor_tensor(shaped, shaped, bcast(c.row_inv[:, t], 2, S), ALU.subtract)\
                    .then_inc(sp.less_tau, 1)

            if mode == "sparse":
                thresholds(c, v, s, sp, buf)
            for k in range(nt + lag + 3):
                if k < nt:
                    if mode == "sparse":
                        less_threshold(k)
                    else:
                        shift(k)
                if 0 <= k - lag - 1 < nt:
                    normalise(k - lag - 1)
                if 0 <= k - lag - 2 < nt:
                    add(k - lag - 2)
                    if not rms:
                        v.wait_ge(s.biased if out_bias else s.y_added, k - lag - 1)
                        measure(v, following, c.x, k - lag - 2)
                if not rms and 0 <= k - lag - 3 < nt:
                    scale(v, following, c.x, c.h, k - lag - 3)


def thresholds(c, v, s, sp, z):
    by_row = lambda a: a.rearrange("p (r k) -> p r k", k=TOP)
    count = c.nt * HEADS * TOP
    top, sums = by_row(c.room(7)[:, 0:count]), by_row(c.room(0)[:, 0:count])
    of_head = c.row_max[:].rearrange("p t h -> p (t h)")
    tau = c.row_inv[:].rearrange("p t h -> p (t h)")
    open_rows = c.tiny[:, 0].rearrange("p a b -> p (a b)")
    for t in range(c.nt):
        v.wait_ge(s.scored, t + 1)
        for h in range(HEADS):
            last = v.max(out=top[:, HEADS * t + h], in_=z(t)[:, h * S:(h + 1) * S])
        last.then_inc(sp.top, 1)
    v.wait_ge(sp.top, c.nt)
    v.tensor_copy(of_head, top[:, :, 0]).then_inc(s.max_ready, 1)
    v.wait_ge(s.max_ready, 1)
    v.tensor_tensor(top, top, bcast(of_head, 2, TOP), ALU.subtract).then_inc(sp.less_max, 1)
    v.wait_ge(sp.less_max, 1)
    flat = lambda a: a.rearrange("p r k -> p (r k)")
    v.wait_ge(sp.row_starts, 2)
    v.tensor_tensor_scan(flat(sums), c.room(6)[:, 0:c.nt * HEADS * TOP], flat(top), 0.0, ALU.mult, ALU.add)\
        .then_inc(sp.summed, 1)
    v.wait_ge(sp.summed, 1)
    v.scalar_tensor_tensor(out=sums, in0=sums, scalar=-1.0,
                           in1=bcast(c.w("inverse_rank")[:, 0:TOP], 1, c.nt * HEADS), op0=ALU.add,
                           op1=ALU.mult).then_inc(sp.candidates, 1)
    v.wait_ge(sp.candidates, 1)
    v.tensor_reduce(tau, sums, AX.X, ALU.max).then_inc(sp.tau, 1)
    v.wait_ge(sp.tau, 1)
    v.tensor_tensor(open_rows, top[:, :, TOP - 1], tau, ALU.is_gt).then_inc(sp.compared, 1)
    v.wait_ge(sp.compared, 1)
    v.tensor_reduce(c.row_open[:], open_rows, AX.X, ALU.max).then_inc(sp.row_open, 1)
    v.wait_ge(sp.open_ps, 1)
    v.tensor_copy(c.count_open[:], c.ps[0:1, 7, 0:1]).then_inc(sp.count_open, 1)
    v.wait_ge(sp.count_open, 1)
    open_count = v.value_load(c.count_open[0:1, 0:1], min_val=0, max_val=P)
    with v.If(open_count > 0):
        v.memset(c.room(1), 1.0).then_inc(sp.step, 1)
        v.wait_ge(sp.step, 1)
        v.memset(c.room(1).rearrange("p (h k) -> p h k", k=S)[:, :, 0], 0.0).then_inc(sp.step, 1)
        for t in range(c.nt):
            sort_rows(c, v, sp.step, t, z(t))
    v.tensor_tensor(tau, tau, of_head, ALU.add).then_inc(sp.shifted_tau, 1)
    v.wait_ge(sp.shifted_tau, 1)


def sort_rows(c, v, step, t, z):
    spare = [c.room(6), c.room(7)]
    shaped = lambda a: a.rearrange("p (h k) -> p h k", k=S)
    done = (SORT_STEPS + 4) * t + 3
    src, at = spare[1], 0
    v.tensor_tensor(shaped(src), shaped(z), bcast(c.row_max[:, t], 2, S), ALU.subtract).then_inc(step, 1)
    v.wait_ge(step, done)
    k = 2
    while k <= S:
        j = k // 2
        while j >= 1:
            dst = spare[at % 2]
            ways = 2 if k < S else 1
            cut = lambda a: a.rearrange("p (b way g s r) -> p b way g s r", way=ways, g=k // (2 * j), s=2, r=j)
            for way in range(ways):
                for side in range(2):
                    op = ALU.max if side == way else ALU.min
                    last = v.tensor_tensor(cut(dst)[:, :, way, :, side], cut(src)[:, :, way, :, 0],
                                           cut(src)[:, :, way, :, 1], op)
            at += 1
            last.then_inc(step, 1)
            v.wait_ge(step, done + at)
            src = dst
            j //= 2
        k *= 2
    sums = spare[at % 2]
    v.tensor_tensor_scan(sums, c.room(1), src, 0.0, ALU.mult, ALU.add).then_inc(step, 1)
    v.wait_ge(step, done + at + 1)
    v.scalar_tensor_tensor(out=shaped(src), in0=shaped(sums), scalar=-1.0,
                           in1=bcast(c.w("inverse_rank"), 1, HEADS), op0=ALU.add, op1=ALU.mult)\
        .then_inc(step, 1)
    v.wait_ge(step, done + at + 2)
    v.tensor_reduce(c.row_inv[:, t], shaped(src), AX.X, ALU.max).then_inc(step, 1)
    v.wait_ge(step, done + at + 3)


def channel_attention(c):
    nc = c.nc
    c.turn_over()
    s = signals(c, "q_scaled q_ready k0_scaled k1_scaled k0_ready k1_ready v_ready scores_ps max_ready shifted "
                "exp_ready sum_ready inv_ready weights_ready spread turned_ps turned y_ps doubled summed "
                "biased")
    following = unit_norm(c, 1)
    SETS = "gl"
    q = [c.room(0)[:, i * 512:(i + 1) * 512].rearrange("p (t d) -> p t d", t=HT) for i in range(2)]
    k = [c.room(1)[:, i * 512:(i + 1) * 512].rearrange("p (t d) -> p t d", t=HT) for i in range(2)]
    vT = [c.room(2)[:, i * 512:(i + 1) * 512] for i in range(2)]
    score = c.room(3)[:, 0:512].rearrange("p (b m e) -> p b m e", b=2, e=32)
    score_ps = c.ps[:, 0:2, 0:256].rearrange("p b (m e) -> p b m e", e=32)
    row = c.tiny[:, 0].rearrange("p a b -> p (a b)")
    stat = lambda i: row[:, i * 16:(i + 1) * 16].rearrange("p (b m) -> p b m", b=2)
    blocks_of = c.room(5, 2)
    diag = c.room(7, 2)
    k_scaled, k_ready = (s.k0_scaled, s.k1_scaled), (s.k0_ready, s.k1_ready)

    def key_set(engine, i):
        engine.tensor_tensor(k[i], c.ctx_tok[:], bcast(c.w("L0x_wk" + SETS[i]), 1, HT), ALU.mult)\
            .then_inc(k_scaled[i], 1)
        engine.wait_ge(k_scaled[i], 1)
        engine.tensor_tensor(k[i], k[i], bcast(c.w("L0x_bk" + SETS[i]), 1, HT), ALU.add).then_inc(k_ready[i], 1)

    with nc.Block() as block:
        @block.tensor
        def _(pe):
            pe.wait_ge(s.q_ready, 2)
            pe.wait_ge(s.k0_ready, 1)
            pe.wait_ge(s.k1_ready, 1)
            for t in range(HT):
                for b in range(2):
                    for i in range(2):
                        for h in range(4):
                            ch = slice(32 * h, 32 * h + 32)
                            last = pe.matmul(c.ps[ch, b, (2 * t + i) * 32:(2 * t + i + 1) * 32],
                                             q[i][part(b), t, ch], k[i][part(b), t, ch],
                                             start=True, stop=True,
                                             tile_position=(64 * b, 32 * h))
            last.then_inc(s.scores_ps, 1)
            for m in range(4):
                pe.wait_ge(s.spread, m + 1)
                for j in range(4):
                    last = pe.transpose(c.ps[:, 2 + m, j * P:(j + 1) * P],
                                        diag[:, (4 * m + j) * P:(4 * m + j + 1) * P], c.w("ident"))
                last.then_inc(s.turned_ps, 1)
            pe.wait_ge(s.v_ready, 2)
            pe.wait_ge(s.turned, 4)
            for t in range(HT):
                for b in range(2):
                    for i in range(2):
                        last = pe.matmul(c.ps[part(b), 6, tok(t)], vT[i][:, seq(t, b)],
                                         blocks_of[:, (8 * b + 2 * t + i) * P:(8 * b + 2 * t + i + 1) * P],
                                         start=(i == 0), stop=(i == 1))
            last.then_inc(s.y_ps, 1)

        @block.scalar
        def _(act):
            for i, n in enumerate(SETS):
                act.activation(vT[i], c.ctxT[:], ACT.Identity, bias=c.w("L0x_bv" + n),
                               scale=c.w("L0x_wv" + n)).then_inc(s.v_ready, 1)
            act.wait_ge(s.shifted, 1)
            act.activation(score, score, ACT.Exp, scale=D ** -0.5).then_inc(s.exp_ready, 1)
            for m in range(4):
                act.wait_ge(s.turned_ps, m + 1)
                act.copy(blocks_of[:, m * 512:(m + 1) * 512], c.ps[:, 2 + m]).then_inc(s.turned, 1)

        @block.gpsimd
        def _(g):
            c.begin(g)
            key_set(g, 0)
            invert(c, g, following, 0, HT)

        @block.vector
        def _(v):
            for i, n in enumerate(SETS):
                v.tensor_tensor(q[i], c.h[:], bcast(c.w("L0x_wq" + n), 1, HT), ALU.mult)\
                    .then_inc(s.q_scaled, 1)
                v.wait_ge(s.q_scaled, i + 1)
                v.tensor_tensor(q[i], q[i], bcast(c.w("L0x_bq" + n), 1, HT), ALU.add).then_inc(s.q_ready, 1)
            key_set(v, 1)
            v.wait_ge(s.scores_ps, 1)
            v.tensor_reduce(stat(0), score_ps, AX.X, ALU.max).then_inc(s.max_ready, 1)
            v.wait_ge(s.max_ready, 1)
            v.tensor_tensor(score, score_ps, bcast(stat(0), 3, 32), ALU.subtract).then_inc(s.shifted, 1)
            v.wait_ge(s.exp_ready, 1)
            v.tensor_reduce(stat(1), score, AX.X, ALU.add).then_inc(s.sum_ready, 1)
            v.wait_ge(s.sum_ready, 1)
            v.reciprocal(stat(2), stat(1)).then_inc(s.inv_ready, 1)
            v.wait_ge(s.inv_ready, 1)
            v.tensor_tensor(score, score, bcast(stat(2), 3, 32), ALU.mult).then_inc(s.weights_ready, 1)
            v.wait_ge(s.weights_ready, 1)
            flat = c.room(3)[:, 0:512].rearrange("p (m e) -> p m e", e=32)
            for m in range(4):
                v.tensor_tensor(diag[:, m * 512:(m + 1) * 512].rearrange("p (m h e) -> p m h e", h=4, e=32),
                                bcast(flat[:, 4 * m:4 * m + 4], 2, 4),
                                bcast(bcast(c.w("block32"), 2, 32), 1, 4), ALU.mult).then_inc(s.spread, 1)
            v.wait_ge(s.y_ps, 1)
            y = c.att[:]
            v.scalar_tensor_tensor(out=y, in0=c.ps[:, 6].rearrange("p (t d) -> p t d", t=HT), scalar=2.0,
                                   in1=bcast(c.w("L0x_wp"), 1, HT), op0=ALU.mult, op1=ALU.mult)\
                .then_inc(s.doubled, 1)
            v.wait_ge(s.doubled, 1)
            v.tensor_tensor(c.x[:], c.x[:], y, ALU.add).then_inc(s.summed, 1)
            v.wait_ge(s.summed, 1)
            v.tensor_tensor(c.x[:], c.x[:], bcast(c.w("L0x_bp"), 1, HT), ALU.add).then_inc(s.biased, 1)
            v.wait_ge(s.biased, 1)
            measure(v, following, c.x, 0, HT)
            scale(v, following, c.x, c.h, 0, HT)


ROUTE = "logits_ps logits_ready top_ready index_ready index_f gap gap_exp denominator first second "


def route_vector(c, v, s, top, bank):
    T = c.tiny
    v.wait_ge(s.logits_ps, NT)
    v.tensor_copy(T[:, :, 0], c.ps[:, bank, 0:NT * E].rearrange("p (t e) -> p t e", t=NT))\
        .then_inc(s.logits_ready, 1)
    v.wait_ge(s.logits_ready, 1)
    for t in range(NT):
        v.max(T[:, t, 1], T[:, t, 0]).then_inc(s.top_ready, 1)
    for t in range(NT):
        v.wait_ge(s.top_ready, t + 1)
        v.max_index(c.index[:, t], T[:, t, 1], T[:, t, 0]).then_inc(s.index_ready, 1)
    v.wait_ge(s.index_ready, NT)
    v.tensor_copy(T[:, :, 2], c.index[:]).then_inc(s.index_f, 1)


def experts(c, n, top, gated):
    nc = c.nc
    twice = n != "L0f"
    c.turn_over()
    s = signals(c, TURN + ROUTE + "up_ps gate_ps hidden_ready activated down_ps added base "
                "total prob onehot rank_ps ranked kept counted picked weights_ready wT_ps wT_ready before_ready none_before")
    if twice:
        r = signals(c, NORM)
    following = unit_norm(c, 1)
    src = c.hn if twice else c.h
    chunks, width = (I2C, IC) if gated else (HC, P)
    PASSES = 2 * E
    tiles_of = lambda i: range(HT * (i // E), HT * (i // E) + HT)
    hidden = lambda i: c.room(2 * (i % 2), 2)[0:width].rearrange("p (c n) -> p c n", c=chunks)
    act_buf = lambda k: c.room(4)[0:width, (k % 2) * 512:(k % 2 + 1) * 512]
    T = c.tiny
    wT = c.room(5)[0:E]
    tiles_before = c.room(6)[:, 0:(NT + 1) * E].rearrange("p (t e) -> p t e", e=E)
    ps_small = 7
    with nc.Block() as block:
        @block.tensor
        def _(pe):
            for half in range(2):
                turn_tensor(c, pe, r.ready if twice else None, s, src, half, s.turned)
            for t in range(NT):
                pe.wait_ge(s.turned, t + 1)
                pe.matmul(c.ps[:, ps_small, t * E:(t + 1) * E], c.hT[:, tok(t)],
                          c.w(n + ("_wr" if n == "L0f" else "_gate")), start=True, stop=True)\
                    .then_inc(s.logits_ps, 1)

            def up(i):
                tokens = c.hT[:, 512 * (i // E):512 * (i // E) + 512]
                for j in range(chunks):
                    k = i * chunks + j
                    at = (i % E) * chunks + j
                    cols = slice(at * width, (at + 1) * width)
                    if gated:
                        for w, bank, sig in (("w1", 0, s.up_ps), ("w3", 2, s.gate_ps)):
                            if k >= 2:
                                pe.wait_ge(s.hidden_ready, k - 1)
                            pe.matmul(c.ps[0:width, bank + k % 2], c.big[n + "_" + w][:, cols], tokens,
                                      start=True, stop=True).then_inc(sig, 1)
                    else:
                        if k >= 4:
                            pe.wait_ge(s.hidden_ready, k - 3)
                        pe.matmul(c.ps[:, k % 4], c.big[n + "_w1"][:, cols], tokens, start=True,
                                  stop=True).then_inc(s.up_ps, 1)

            def down(i):
                pe.wait_ge(s.hidden_ready, (i + 1) * chunks)
                if i >= 2:
                    pe.wait_ge(s.added, HT * (i - 1))
                for q in range(HT):
                    for j in range(chunks):
                        at = (i % E) * chunks + j
                        last = pe.matmul(c.ps[:, 4 + i % 2, tok(q)], hidden(i)[:, j, tok(q)],
                                         c.big[n + "_w2"][0:width, at * D:(at + 1) * D],
                                         start=(j == 0), stop=(j == chunks - 1))
                last.then_inc(s.down_ps, 1)

            for m in ("w1", "w3", "w2") if gated else ("w1", "w2"):
                pe.wait_ge(c.loaded[f"{n}_{m}"], 16)
            up(0)
            up(1)
            down(0)
            if n == "L1f":
                pe.wait_ge(s.before_ready, NT)
                ranks = c.ps[:, 6, 0:(NT + 1) * E]
                pe.matmul(ranks, c.w("ones"), tiles_before.rearrange("p t e -> p (t e)"), start=True, stop=False)
                pe.matmul(ranks[:, 0:NT * E].rearrange("p (t e) -> p t e", e=E), c.w("before"), T[:, :, 4],
                          start=False, stop=True).then_inc(s.rank_ps, 1)
            if n == "L0f":
                for t in range(NT):
                    pe.wait_ge(s.weights_ready, t + 1)
                    pe.transpose(c.ps[0:E, 6 - t // 4, tok(t % 4)], T[:, t, 3], c.w("ident")).then_inc(s.wT_ps, 1)
                for t in range(NT):
                    pe.wait_ge(s.wT_ready, t // 4 + 1)
                    pe.matmul(c.ps[:, 7 - t // 4, tok(t % 4)], wT[:, tok(t)], c.w("L0f_b2"), start=True, stop=True)\
                        .then_inc(s.rank_ps, 1)
            for i in range(1, PASSES):
                if i < PASSES - 1:
                    up(i + 1)
                down(i)

        @block.scalar
        def _(act):
            for half in range(2):
                turn_scalar(c, act, s, c.hT, half)

            def activate(i):
                for j in range(chunks):
                    k = i * chunks + j
                    act.wait_ge(s.up_ps, k + 1)
                    if gated:
                        if k >= 2:
                            act.wait_ge(s.hidden_ready, k - 1)
                        act.activation(act_buf(k), c.ps[0:width, k % 2], ACT.Silu).then_inc(s.activated, 1)
                    else:
                        if i >= 2:
                            act.wait_ge(s.down_ps, i - 1)
                        out = hidden(i)[:, j]
                        if n == "L0f":
                            at = (i % E) * chunks + j
                            act.activation(out, c.ps[:, k % 4], ACT.Gelu, bias=c.w("L0f_b1")[:, at:at + 1])\
                                .then_inc(s.hidden_ready, 1)
                        else:
                            act.activation(out, c.ps[:, k % 4], ACT.Gelu).then_inc(s.hidden_ready, 1)

            act.wait_ge(s.gap, 1)
            exp_in = T[:, :, 5] if n == "L1f" else T[:, :, 5, 0:1]
            act.activation(exp_in, exp_in, ACT.Exp).then_inc(s.gap_exp, 1)
            activate(0)
            activate(1)
            if n == "L0f":
                for half in range(2):
                    act.wait_ge(s.wT_ps, 4 * half + 4)
                    act.copy(wT[:, half * 512:(half + 1) * 512], c.ps[0:E, 6 - half]).then_inc(s.wT_ready, 1)
            for i in range(2, PASSES):
                activate(i)

        @block.gpsimd
        def _(g):
            c.begin(g)
            if twice:
                norm_gpsimd(c, g, r, 1e-6 if gated else 1e-5, "rms" if gated else "mean")
            if n == "L1f":
                g.memset(tiles_before[:, 0], 0.0).then_inc(s.none_before, 1)
            for half in range(2):
                invert(c, g, following, half, HT)

        @block.vector
        def _(v):
            if twice:
                if gated:
                    norm_vector(c, v, r, c.h, c.hn, "rms", c.w(n + "_rms"))
                else:
                    norm_vector(c, v, r, c.h, c.hn, "mean", c.w(n + "_gamma"), c.w(n + "_beta"))
                v.tensor_tensor(c.x[:], c.x[:], c.h[:], ALU.add).then_inc(s.base, 1)
            def hide(i):
                for j in range(chunks):
                    k = i * chunks + j
                    v.wait_ge(s.gate_ps, k + 1)
                    v.wait_ge(s.activated, k + 1)
                    if i >= 2:
                        v.wait_ge(s.down_ps, i - 1)
                    v.tensor_tensor(hidden(i)[:, j], act_buf(k), c.ps[0:width, 2 + k % 2], ALU.mult)\
                        .then_inc(s.hidden_ready, 1)

            route_vector(c, v, s, top, ps_small)
            v.wait_ge(s.index_f, 1)
            where = lambda t, k: T[:, t, 2, k:k + 1]
            if n == "L1f":
                for t in range(NT):
                    last = v.tensor_scalar(T[:, t, 5], T[:, t, 0], T[:, t, 1, 0:1], None, ALU.subtract)
                last.then_inc(s.gap, 1)
                for t in range(NT):
                    v.tensor_scalar(T[:, t, 4], c.w("expert_index"), where(t, 0), None, ALU.is_equal)\
                        .then_inc(s.onehot, 1)
                v.wait_ge(s.onehot, NT)
                v.wait_ge(s.none_before, 1)
                for t in range(NT):
                    v.tensor_tensor(tiles_before[:, t + 1], tiles_before[:, t], T[:, t, 4], ALU.add)\
                        .then_inc(s.before_ready, 1)
                    v.wait_ge(s.before_ready, t + 1)
                v.wait_ge(s.gap_exp, 1)
                v.tensor_reduce(T[:, :, 6, 0:1], T[:, :, 5], AX.X, ALU.add).then_inc(s.total, 1)
                v.wait_ge(s.total, 1)
                v.reciprocal(T[:, :, 6, 1:2], T[:, :, 6, 0:1]).then_inc(s.prob, 1)
                v.wait_ge(s.rank_ps, 1)
                v.wait_ge(s.prob, 1)
                ranks = c.ps[:, 6, 0:NT * E].rearrange("p (t e) -> p t e", e=E)
                v.tensor_tensor(T[:, :, 7], ranks, bcast(c.counts[:], 1, NT), ALU.add).then_inc(s.ranked, 1)
                v.wait_ge(s.ranked, 1)
                v.scalar_tensor_tensor(out=T[:, :, 8], in0=T[:, :, 7], scalar=float(CAPACITY), in1=T[:, :, 4],
                                       op0=ALU.is_lt, op1=ALU.mult).then_inc(s.kept, 1)
                v.wait_ge(s.kept, 1)
                v.tensor_tensor(T[:, :, 3], T[:, :, 8], T[:, :, 6, 1:2].to_broadcast([P, NT, E]), ALU.mult)\
                    .then_inc(s.weights_ready, NT)
                v.tensor_tensor(c.counts[:], c.counts[:], c.ps[:, 6, NT * E:(NT + 1) * E], ALU.add)\
                    .then_inc(s.counted, 1)
            else:
                v.tensor_tensor(T[:, :, 5, 0:1], T[:, :, 1, 1:2], T[:, :, 1, 0:1], ALU.subtract)\
                    .then_inc(s.gap, 1)
                if gated:
                    hide(0)
                v.wait_ge(s.gap_exp, 1)
                v.tensor_scalar(T[:, :, 5, 1:2], T[:, :, 5, 0:1], 1.0, None, ALU.add)\
                    .then_inc(s.denominator, 1)
                v.wait_ge(s.denominator, 1)
                v.reciprocal(T[:, :, 5, 2:3], T[:, :, 5, 1:2]).then_inc(s.first, 1)
                v.wait_ge(s.first, 1)
                v.tensor_tensor(T[:, :, 5, 3:4], T[:, :, 5, 0:1], T[:, :, 5, 2:3], ALU.mult)\
                    .then_inc(s.second, 1)
                v.wait_ge(s.second, 1)
                of_expert = bcast(c.w("expert_index"), 1, NT)
                spread = lambda a: a.to_broadcast([P, NT, E])
                v.tensor_tensor(T[:, :, 4], of_expert, spread(T[:, :, 2, 0:1]), ALU.is_equal).then_inc(s.picked, 1)
                v.tensor_tensor(T[:, :, 6], of_expert, spread(T[:, :, 2, 1:2]), ALU.is_equal).then_inc(s.picked, 1)
                v.wait_ge(s.picked, 1)
                v.tensor_tensor(T[:, :, 4], T[:, :, 4], spread(T[:, :, 5, 2:3]), ALU.mult).then_inc(s.picked, 1)
                v.wait_ge(s.picked, 2)
                v.tensor_tensor(T[:, :, 6], T[:, :, 6], spread(T[:, :, 5, 3:4]), ALU.mult).then_inc(s.picked, 1)
                v.wait_ge(s.picked, 4)
                v.tensor_tensor(T[:, :, 3], T[:, :, 4], T[:, :, 6], ALU.add).then_inc(s.weights_ready, NT)
            v.wait_ge(s.weights_ready, NT)

            if n == "L0f":
                v.wait_ge(s.rank_ps, NT)
                for t in range(NT):
                    v.tensor_tensor(c.x[:, t], c.x[:, t], c.ps[:, 7 - t // 4, tok(t % 4)], ALU.add)\
                        .then_inc(s.base, 1)
            for i in range(PASSES):
                if gated and i + 1 < PASSES:
                    hide(i + 1)
                v.wait_ge(s.down_ps, i + 1)
                for q, t in enumerate(tiles_of(i)):
                    if i % E == 0:
                        v.wait_ge(s.base, t + 1 if n == "L0f" else 1)
                    else:
                        v.wait_ge(s.added, HT * (i - 1) + q + 1)
                    v.scalar_tensor_tensor(out=c.x[:, t], in0=c.ps[:, 4 + i % 2, tok(q)],
                                           scalar=T[:, t, 3, (i % E):(i % E) + 1], in1=c.x[:, t], op0=ALU.mult,
                                           op1=ALU.add).then_inc(s.added, 1)
                if i % E == E - 1:
                    v.wait_ge(s.added, HT * (i + 1))
                    measure(v, following, c.x, i // E, HT)
                if i in (E, PASSES - 1):
                    scale(v, following, c.x, c.h, i // E - (i == E), HT)


def rotary_attention(c):
    nc = c.nc
    n = "L1a"
    c.turn_over()
    s = signals(c, TURN + "plain_ps by_cos by_sin q_rotated k_rotated v_ps v_ready scores_ps "
                "scored max_ready shifted exp_ready sum_ready inv_ready probs_ready probsT_ps "
                "probsT_ready o_ps o_ready mid_ps mid_ready y_ps y_ready weighted added")
    own, following = unit_norm(c, 0), unit_norm(c, 1)
    w = c.big["L1_qkv"]
    CH = INNER // P
    roomq, roomk = c.room(0), c.room(1)
    sines = lambda k: c.room((2, 8)[k])
    values = lambda t: c.room((3, 7)[t % 2])
    probs, probsT, outT = c.room(4), c.room(5), c.room(6)
    cos = lambda a: a.rearrange("p (m k) -> p m k", k=S)
    banks = lambda k: c.ps[:, k:k + 2].rearrange("p b n -> p (b n)")
    with nc.Block() as block:
        @block.sync
        def _(sp):
            for m in ("L0f_w1", "L0f_w2"):
                sp.wait_ge(c.loaded[m], 16)
            for m in ("L1f_w1", "L1f_w2"):
                sp.dma_start(c.big[m][:], c.dram[m]).then_inc(c.loaded[m], 16)

        @block.tensor
        def _(pe):
            for half in range(NT // 4):
                turn_tensor(c, pe, None, s, c.h, half, s.turned)
            pe.wait_ge(s.turned, NT)
            pe.wait_ge(c.loaded["L1_qkv"], 16)

            def project(t, k):
                if t > 0 or k > 0:
                    pe.wait_ge(s.by_sin, 2 * t + k)
                if t > 0:
                    pe.wait_ge(s.scored, t)
                for m in range(2):
                    for j in range(CH):
                        at = (2 * m + k) * INNER + j * P
                        last = pe.matmul(c.ps[:, 2 * m + j // 4, (j % 4) * P:(j % 4 + 1) * P],
                                         w[:, at:at + P], c.hT[:, tok(t)], start=True, stop=True)
                last.then_inc(s.plain_ps, 1)

            def project_values(t):
                if t == 1:
                    pe.wait_ge(s.v_ready, 1)
                elif t >= 2:
                    pe.wait_ge(s.probsT_ready, 2 * (t - 1))
                for b in range(2):
                    for u in range(2):
                        last = pe.matmul(c.ps[part(u), 4 + b], c.hT[:, seq(t, b)],
                                         w[:, 4 * INNER + u * 512:4 * INNER + (u + 1) * 512],
                                         start=True, stop=True)
                last.then_inc(s.v_ps, 1)

            def scores(t):
                pe.wait_ge(s.q_rotated, t + 1)
                pe.wait_ge(s.k_rotated, t + 1)
                for j in range(CH):
                    for a in range(2):
                        for b in range(2):
                            ch = slice(j * P + b * S, j * P + b * S + S)
                            last = pe.matmul(c.ps[part(b), a, j * S:(j + 1) * S], roomq[part(a), ch],
                                             roomk[part(a), ch], start=True, stop=True)
                last.then_inc(s.scores_ps, 1)

            def turn_probs(t):
                pe.wait_ge(s.v_ready, min(t + 2, NT))
                pe.wait_ge(s.probs_ready, t + 1)
                for k in range(2):
                    for j in range(4):
                        last = pe.transpose(c.ps[:, 4 + k, j * P:(j + 1) * P],
                                            probs[:, (4 * k + j) * P:(4 * k + j + 1) * P], c.w("ident"))
                    last.then_inc(s.probsT_ps, 1)

            def weigh_values(t):
                pe.wait_ge(s.probsT_ready, 2 * t + 2)
                if t > 0:
                    pe.wait_ge(s.y_ready, t)
                for q in range(CH):
                    u, m = q % 2, q // 2
                    for a in range(2):
                        for b in range(2):
                            last = pe.matmul(c.ps[part(a), 6 + u, m * P + b * S:m * P + b * S + S],
                                             values(t)[part(u), b * 512 + m * P + a * 64:b * 512 + m * P + a * 64 + 64],
                                             probsT[part(u), a * 512 + m * P + b * S:a * 512 + m * P + b * S + S],
                                             start=True, stop=True)
                last.then_inc(s.o_ps, 1)

            def project_out(t):
                pe.wait_ge(s.o_ready, 2 * t + 2)
                for q in range(CH):
                    last = pe.matmul(c.ps[:, 6, 0:P], c.w("L1_wo1")[:, q * P:(q + 1) * P],
                                     outT[:, (q % 2) * 512 + (q // 2) * P:(q % 2) * 512 + (q // 2 + 1) * P],
                                     start=(q == 0), stop=(q == CH - 1))
                last.then_inc(s.mid_ps, 1)

            def project_mid(t):
                pe.wait_ge(s.mid_ready, t + 1)
                pe.matmul(c.ps[:, 7, 0:P], c.oT[:, tok(t)], c.w("L1_wo2"), start=True, stop=True)\
                    .then_inc(s.y_ps, 1)

            for t in range(NT + 1):
                if t < NT:
                    project_values(t)
                    project(t, 0)
                if t > 0:
                    turn_probs(t - 1)
                    weigh_values(t - 1)
                if t < NT:
                    project(t, 1)
                if t > 0:
                    project_out(t - 1)
                if t < NT:
                    scores(t)
                if t > 0:
                    project_mid(t - 1)

        @block.scalar
        def _(act):
            for half in range(NT // 4):
                turn_scalar(c, act, s, c.hT, half)
            for k in range(NT + 1):
                t = k - 1
                if t >= 0:
                    act.wait_ge(s.shifted, t + 1)
                    act.activation(probs, probs, ACT.Exp, scale=WH ** -0.5).then_inc(s.exp_ready, 1)
                if k < NT:
                    act.wait_ge(s.v_ps, k + 1)
                    if k >= 2:
                        act.wait_ge(s.o_ps, k - 1)
                    act.copy(values(k), banks(4)).then_inc(s.v_ready, 1)
                if t < 0:
                    continue
                for j in range(2):
                    act.wait_ge(s.probsT_ps, 2 * t + j + 1)
                    if t > 0:
                        act.wait_ge(s.o_ps, t)
                    act.copy(probsT[:, j * 512:(j + 1) * 512], c.ps[:, 4 + j]).then_inc(s.probsT_ready, 1)
                act.wait_ge(s.o_ps, t + 1)
                if t > 0:
                    act.wait_ge(s.mid_ps, t)
                for u in range(2):
                    act.copy(outT[:, u * 512:(u + 1) * 512], c.ps[:, 6 + u]).then_inc(s.o_ready, 1)
                act.wait_ge(s.mid_ps, t + 1)
                act.activation(c.oT[:, tok(t)], c.ps[:, 6, 0:P], ACT.Relu).then_inc(s.mid_ready, 1)
                act.wait_ge(s.y_ps, t + 1)
                act.copy(c.att[:, t], c.ps[:, 7, 0:P]).then_inc(s.y_ready, 1)

        @block.gpsimd
        def _(g):
            c.begin(g)
            for k in range(NT + 4):
                if k < NT:
                    g.wait_ge(s.by_sin, 2 * k + 1)
                    g.tensor_tensor(roomq, roomq, sines(0), ALU.add).then_inc(s.q_rotated, 1)
                if 0 <= k - 2 < NT:
                    invert(c, g, own, k - 2)
                if 0 <= k - 3 < NT:
                    invert(c, g, following, k - 3)

        @block.vector
        def _(v):
            def rotate(t, k):
                room = (roomq, roomk)[k]
                v.wait_ge(s.plain_ps, 2 * t + k + 1)
                if t > 0:
                    v.wait_ge(s.scores_ps, t)
                    if k == 0:
                        v.wait_ge(s.q_rotated, t)
                v.tensor_tensor(cos(room), cos(banks(0)), bcast(c.w("rope_cos"), 1, 2 * CH), ALU.mult)\
                    .then_inc(s.by_cos, 1)
                v.tensor_tensor(cos(sines(k)), cos(banks(2)), bcast(c.w("rope_sin"), 1, 2 * CH), ALU.mult)\
                    .then_inc(s.by_sin, 1)
                if k == 1:
                    v.wait_ge(s.by_cos, 2 * t + 2)
                    v.wait_ge(s.by_sin, 2 * t + 2)
                    v.tensor_tensor(roomk, roomk, sines(1), ALU.add).then_inc(s.k_rotated, 1)

            def soften(t):
                v.wait_ge(s.scores_ps, t + 1)
                if t > 0:
                    v.wait_ge(s.probsT_ps, 2 * t)
                v.tensor_tensor(cos(probs), cos(banks(0)), bcast(c.w("causal"), 1, HEADS), ALU.add)\
                    .then_inc(s.scored, 1)
                v.wait_ge(s.scored, t + 1)
                v.tensor_reduce(c.row_max[:, t], cos(probs), AX.X, ALU.max).then_inc(s.max_ready, 1)
                v.wait_ge(s.max_ready, t + 1)
                v.tensor_tensor(cos(probs), cos(probs), bcast(c.row_max[:, t], 2, S), ALU.subtract)\
                    .then_inc(s.shifted, 1)
                v.wait_ge(s.exp_ready, t + 1)
                v.tensor_reduce(c.row_max[:, t], cos(probs), AX.X, ALU.add).then_inc(s.sum_ready, 1)
                v.wait_ge(s.sum_ready, t + 1)
                v.reciprocal(c.row_inv[:, t], c.row_max[:, t]).then_inc(s.inv_ready, 1)
                v.wait_ge(s.inv_ready, t + 1)
                v.tensor_tensor(cos(probs), cos(probs), bcast(c.row_inv[:, t], 2, S), ALU.mult)\
                    .then_inc(s.probs_ready, 1)

            for k in range(NT + 5):
                if 0 <= k - 1 < NT:
                    soften(k - 1)
                if k < NT:
                    rotate(k, 0)
                    rotate(k, 1)
                if 0 <= k - 2 < NT:
                    v.wait_ge(s.y_ready, k - 1)
                    measure(v, own, c.att, k - 2)
                t = k - 3
                if 0 <= t < NT:
                    scale(v, own, c.att, c.hn, t)
                    v.wait_ge(own.normed, t + 1)
                    v.tensor_tensor(c.hn[:, t], c.hn[:, t], c.w("L1_gamma"), ALU.mult).then_inc(s.weighted, 1)
                    v.wait_ge(s.weighted, t + 1)
                    v.tensor_tensor(c.x[:, t], c.x[:, t], c.hn[:, t], ALU.add).then_inc(s.added, 1)
                    v.wait_ge(s.added, t + 1)
                    measure(v, following, c.x, t)
                if 0 <= k - 4 < NT:
                    scale(v, following, c.x, c.h, k - 4)


def matrix_lstm(c):
    nc = c.nc
    c.turn_over()
    following = unit_norm(c, 1)
    s = signals(c, TURN + "gates_ps gates_ready magnitude exp_ready log_ready floor log_f "
                "decay_ps decay input spread level_ps masked max_ready shifted weights_ready top floor_exp "
                "qk_ps qk_weighted sum_ready absolute least eps_added inv_ready CT_ps CT_ready o_ps normed "
                "values head_stats head_moments head_eps head_rstd centred scaled_heads gained added")
    H4, W = 4, 32
    T = lambda i: c.tiny[:, :, i, 0:H4]
    gates = c.tiny[:, :, 0]
    weights = c.room(0, 2).rearrange("p (t h k) -> p t h k", t=NT, k=S)
    C = c.room(2, 2).rearrange("p (t h k) -> p t h k", t=NT, k=S)
    CT = c.room(4, 2)
    spread = c.room(2, 2).rearrange("p (t h k) -> p t h k", t=NT, k=S)
    stats = c.room(6)[:, 0:NT * H4 * 6].rearrange("p (t h k) -> p t h k", t=NT, k=6)
    moments = c.room(6)[:, 512:512 + NT * H4 * 2].rearrange("p (t h k) -> p t h k", t=NT, k=2)
    eps = c.room(6)[:, 768:768 + NT * H4].rearrange("p (t h) -> p t h", t=NT)
    rstd = c.room(6)[:, 896:896 + NT * H4].rearrange("p (t h) -> p t h", t=NT)
    hs = c.att[:].rearrange("p t (h d) -> p t h d", d=W)
    values = c.room(7, 2).rearrange("p (t b d) -> p t b d", t=NT, b=2)
    with nc.Block() as block:
        @block.sync
        def _(sp):
            for b in range(2):
                for u in range(2):
                    sp.dma_start(values[part(u), :, b], c.context[c.group, part(b), c.own_tiles]).then_inc(s.values, 16)

        @block.tensor
        def _(pe):
            for half in range(2):
                turn_tensor(c, pe, None, s, c.h, half, s.turned)
            for t in range(NT):
                pe.wait_ge(s.turned, t + 1)
                for m, (src, gate) in enumerate(((c.hT, c.w("L2x_g0")), (c.ctxT, c.gate_of_ctx[:]))):
                    last = pe.matmul(c.ps[:, 7, t * 8:t * 8 + 8], src[:, tok(t)], gate,
                                     start=(m == 0), stop=(m == 1))
                last.then_inc(s.gates_ps, 1)
            pe.wait_ge(s.turned, NT)
            for t in range(NT):
                if t == NT // 4:
                    pe.wait_ge(s.log_f, 1)
                    pe.matmul(c.ps[:, 7, 64:64 + NT * 4].rearrange("p (t h) -> p t h", t=NT), c.w("prefix_seq"),
                              T(3), start=True, stop=True).then_inc(s.decay_ps, 1)
                for h in range(H4):
                    rows = slice(W * h, W * h + W)
                    for b in range(2):
                        last = pe.matmul(c.ps[part(b), h, t * S:(t + 1) * S], c.hT[rows, seq(t, b)],
                                         c.ctxT[rows, seq(t, b)], start=True, stop=True)
            last.then_inc(s.qk_ps, 1)
            pe.wait_ge(s.spread, 1)
            for t in range(NT):
                last = pe.matmul(c.ps[:, 4 + t // 2, (t % 2) * 256:(t % 2 + 1) * 256], c.w("same_seq"),
                                 spread[:, t].rearrange("p h k -> p (h k)"), start=True, stop=True)
            last.then_inc(s.level_ps, 1)
            pe.wait_ge(s.qk_weighted, 1)
            pe.wait_ge(s.masked, 1)
            for t in range(NT):
                for j in range(2):
                    last = pe.transpose(c.ps[:, 4 + t // 2, (2 * (t % 2) + j) * P:(2 * (t % 2) + j + 1) * P],
                                        C[:, t, 2 * j:2 * j + 2].rearrange("p h k -> p (h k)"),
                                        c.w("ident"))
                if t % 2:
                    last.then_inc(s.CT_ps, 1)
            pe.wait_ge(s.CT_ready, 4)
            pe.wait_ge(s.values, 4 * 16)
            for t in range(NT):
                for b in range(2):
                    for h in range(H4):
                        at = (2 * t + h // 2) * P + b * S
                        last = pe.matmul(c.ps[part(b), 2 * (t // 4) + h % 2, t % 4 * P + h * W:t % 4 * P + h * W + W],
                                         CT[part(h % 2), at:at + S],
                                         values[part(h % 2), t, b, h * W:h * W + W],
                                         start=True, stop=True)
            last.then_inc(s.o_ps, 1)

        @block.scalar
        def _(act):
            for half in range(2):
                turn_scalar(c, act, s, c.hT, half)
            act.wait_ge(s.magnitude, 1)
            act.activation(T(1), T(1), ACT.Exp).then_inc(s.exp_ready, 1)
            act.wait_ge(s.exp_ready, 1)
            act.activation(T(1), T(1), ACT.Ln, bias=1.0).then_inc(s.log_ready, 1)
            act.wait_ge(s.shifted, 1)
            act.activation(weights, weights, ACT.Exp).then_inc(s.weights_ready, 1)
            act.wait_ge(s.top, 1)
            act.activation(T(7), T(6), ACT.Exp, scale=-1.0).then_inc(s.floor_exp, 1)
            for k in range(4):
                act.wait_ge(s.CT_ps, k + 1)
                act.copy(CT[:, k * 512:(k + 1) * 512], c.ps[:, 4 + k]).then_inc(s.CT_ready, 1)

        @block.gpsimd
        def _(g):
            c.begin(g)
            for half in range(2):
                own = slice(4 * half, 4 * half + 4)
                g.wait_ge(s.head_moments, 4 * (half + 1) * H4)
                g.tensor_scalar(eps[:, own], moments[:, own, :, 1], 1e-6, None, ALU.add).then_inc(s.head_eps, 1)
                g.wait_ge(s.head_eps, half + 1)
                g.tensor_tensor(rstd[:, own], eps[:, own],
                                c.minus_half[:, 0:4 * H4].rearrange("p (t h) -> p t h", t=4),
                                ALU.pow).then_inc(s.head_rstd, 1)
            for half in range(2):
                invert(c, g, following, half, 4)

        @block.vector
        def _(v):
            v.wait_ge(s.gates_ps, NT)
            v.tensor_tensor(gates, c.ps[:, 7, 0:NT * 8].rearrange("p (t n) -> p t n", t=NT),
                            bcast(c.w("L2x_gb"), 1, NT), ALU.add).then_inc(s.gates_ready, 1)
            v.wait_ge(s.gates_ready, 1)
            forget, enter = gates[:, :, 4:8], gates[:, :, 0:4]
            v.scalar_tensor_tensor(out=T(1), in0=forget, scalar=-1.0, in1=forget, op0=ALU.mult, op1=ALU.min)\
                .then_inc(s.magnitude, 1)
            v.tensor_scalar(T(2), forget, 0.0, None, ALU.min).then_inc(s.floor, 1)
            v.wait_ge(s.floor, 1)
            v.wait_ge(s.log_ready, 1)
            v.tensor_tensor(T(3), T(2), T(1), ALU.subtract).then_inc(s.log_f, 1)
            v.wait_ge(s.decay_ps, 1)
            v.tensor_copy(T(13), c.ps[:, 7, 64:64 + NT * 4].rearrange("p (t h) -> p t h", t=NT)).then_inc(s.decay, 1)
            v.wait_ge(s.decay, 1)
            v.tensor_tensor(T(4), enter, T(13), ALU.subtract).then_inc(s.input, 1)
            v.wait_ge(s.input, 1)
            for t in range(NT):
                last = v.tensor_tensor(spread[:, t], bcast(T(4)[:, t], 2, S), bcast(c.w("pos_onehot"), 1, H4),
                                       ALU.mult)
            last.then_inc(s.spread, 1)
            v.wait_ge(s.level_ps, 1)
            for t in range(NT):
                last = v.tensor_tensor(weights[:, t], c.ps[:, 4 + t // 2, (t % 2) * 256:(t % 2 + 1) * 256]
                                       .rearrange("p (h k) -> p h k", k=S), bcast(c.w("causal"), 1, H4), ALU.add)
            last.then_inc(s.masked, 1)
            v.wait_ge(s.masked, 1)
            v.tensor_reduce(T(5), weights, AX.X, ALU.max).then_inc(s.max_ready, 1)
            v.wait_ge(s.max_ready, 1)
            for t in range(NT):
                last = v.tensor_tensor(weights[:, t], weights[:, t], bcast(T(5)[:, t], 2, S), ALU.subtract)
            last.then_inc(s.shifted, 1)
            v.tensor_tensor(T(6), T(5), T(13), ALU.add).then_inc(s.top, 1)
            v.wait_ge(s.weights_ready, 1)
            v.wait_ge(s.qk_ps, 1)
            for t in range(NT):
                last = v.scalar_tensor_tensor(out=C[:, t], in0=c.ps[:, 0:4, t * S:(t + 1) * S],
                                              scalar=W ** -0.5, in1=weights[:, t], op0=ALU.mult, op1=ALU.mult)
            last.then_inc(s.qk_weighted, 1)
            v.wait_ge(s.qk_weighted, 1)
            v.tensor_reduce(T(8), C, AX.X, ALU.add).then_inc(s.sum_ready, 1)
            v.wait_ge(s.sum_ready, 1)
            v.scalar_tensor_tensor(out=T(9), in0=T(8), scalar=-1.0, in1=T(8), op0=ALU.mult, op1=ALU.max)\
                .then_inc(s.absolute, 1)
            v.wait_ge(s.absolute, 1)
            v.wait_ge(s.floor_exp, 1)
            v.tensor_tensor(T(12), T(9), T(7), ALU.max).then_inc(s.least, 1)
            v.wait_ge(s.least, 1)
            v.tensor_scalar(T(10), T(12), 1e-6, None, ALU.add).then_inc(s.eps_added, 1)
            v.wait_ge(s.eps_added, 1)
            v.reciprocal(T(11), T(10)).then_inc(s.inv_ready, 1)
            v.wait_ge(s.inv_ready, 1)
            v.wait_ge(s.o_ps, 1)
            for t in range(NT):
                for u in range(2):
                    last = v.tensor_tensor(hs[:, t, u::2], c.ps[:, 2 * (t // 4) + u, tok(t % 4)]
                                           .rearrange("p (h d) -> p h d", d=W)[:, u::2],
                                           bcast(T(11)[:, t, u::2], 2, W), ALU.mult)
            last.then_inc(s.normed, 1)
            v.wait_ge(s.normed, 1)
            for half in range(2):
                for t in range(4 * half, 4 * half + 4):
                    for h in range(H4):
                        v.bn_stats(stats[:, t, h], hs[:, t, h]).then_inc(s.head_stats, 1)
                for t in range(4 * half, 4 * half + 4):
                    for h in range(H4):
                        v.wait_ge(s.head_stats, t * H4 + h + 1)
                        v.bn_aggr(moments[:, t, h], stats[:, t, h]).then_inc(s.head_moments, 1)
            v.wait_ge(s.head_moments, NT * H4)
            for half in range(2):
                own = slice(4 * half, 4 * half + 4)
                v.tensor_tensor(hs[:, own], hs[:, own], bcast(moments[:, own, :, 0], 3, W), ALU.subtract)\
                    .then_inc(s.centred, 1)
            for half in range(2):
                own = slice(4 * half, 4 * half + 4)
                v.wait_ge(s.centred, half + 1)
                v.wait_ge(s.head_rstd, half + 1)
                v.tensor_tensor(hs[:, own], hs[:, own], bcast(rstd[:, own], 3, W), ALU.mult)\
                    .then_inc(s.scaled_heads, 1)
                v.wait_ge(s.scaled_heads, half + 1)
                v.tensor_tensor(c.att[:, own], c.att[:, own], bcast(c.w("L2x_on"), 1, 4), ALU.mult)\
                    .then_inc(s.gained, 1)
                v.wait_ge(s.gained, half + 1)
                v.tensor_tensor(c.x[:, own], c.x[:, own], c.att[:, own], ALU.add).then_inc(s.added, 1)
                v.wait_ge(s.added, half + 1)
                measure(v, following, c.x, half, 4)
            for half in range(2):
                scale(v, following, c.x, c.h, half, 4)


def gated_mlp(c):
    nc = c.nc
    c.turn_over()
    s = signals(c, NORM + TURN + "logits_ps logits_ready top_ready less_max exps total inv prob "
                "two eps_added eps_inv factor up_ps hidden_ready down_ps y_ready added")
    T = c.tiny
    hidden = lambda half: c.room(2 * half, 2).rearrange("p (c n) -> p c n", c=HC)
    with nc.Block() as block:
        @block.tensor
        def _(pe):
            for half in range(2):
                turn_tensor(c, pe, s.ready, s, c.hn, half, s.turned)
            for t in range(NT):
                pe.wait_ge(s.turned, t + 1)
                pe.matmul(c.ps[:, 7, t * E:(t + 1) * E], c.hT[:, tok(t)], c.w("L3f_gate"), start=True,
                          stop=True).then_inc(s.logits_ps, 1)
            for half in range(2):
                for j in range(HC):
                    if half == 1:
                        pe.wait_ge(s.hidden_ready, j + 1)
                    pe.matmul(c.ps[:, j], c.w("L3f_up")[:, j * P:(j + 1) * P],
                              c.hT[:, half * 512:(half + 1) * 512], start=True, stop=True).then_inc(s.up_ps, 1)
            for t in range(NT):
                half = t // 4
                pe.wait_ge(s.hidden_ready, HC * (half + 1))
                for j in range(HC):
                    last = pe.matmul(c.ps[:, 4 + half, tok(t % 4)], hidden(half)[:, j, tok(t % 4)],
                                     c.w("L3f_down")[:, j * D:(j + 1) * D], start=(j == 0), stop=(j == HC - 1))
                last.then_inc(s.down_ps, 1)

        @block.scalar
        def _(act):
            for half in range(2):
                turn_scalar(c, act, s, c.hT, half)
            act.wait_ge(s.less_max, 1)
            act.activation(T[:, :, 2], T[:, :, 2], ACT.Exp).then_inc(s.exps, 1)
            for half in range(2):
                for j in range(HC):
                    act.wait_ge(s.up_ps, HC * half + j + 1)
                    act.activation(hidden(half)[:, j], c.ps[:, j], ACT.Silu).then_inc(s.hidden_ready, 1)

        @block.gpsimd
        def _(g):
            c.begin(g)
            norm_gpsimd(c, g, s, 1e-6, "rms")

        @block.vector
        def _(v):
            norm_vector(c, v, s, c.h, c.hn, "rms", c.w("L3f_n2"))
            v.wait_ge(s.logits_ps, NT)
            v.tensor_copy(T[:, :, 0], c.ps[:, 7, 0:NT * E].rearrange("p (t e) -> p t e", t=NT))\
                .then_inc(s.logits_ready, 1)
            v.wait_ge(s.logits_ready, 1)
            for t in range(NT):
                v.max(T[:, t, 1], T[:, t, 0]).then_inc(s.top_ready, 1)
            v.wait_ge(s.top_ready, NT)
            v.tensor_tensor(T[:, :, 2], T[:, :, 1], T[:, :, 1, 0:1].to_broadcast([P, NT, E]), ALU.subtract)\
                .then_inc(s.less_max, 1)
            v.wait_ge(s.exps, 1)
            v.tensor_reduce(T[:, :, 3, 0:1], T[:, :, 2], AX.X, ALU.add).then_inc(s.total, 1)
            v.tensor_reduce(T[:, :, 3, 1:2], T[:, :, 2, 0:2], AX.X, ALU.add).then_inc(s.two, 1)
            v.wait_ge(s.total, 1)
            v.reciprocal(T[:, :, 3, 2:3], T[:, :, 3, 0:1]).then_inc(s.inv, 1)
            v.wait_ge(s.inv, 1)
            v.wait_ge(s.two, 1)
            v.tensor_tensor(T[:, :, 3, 3:4], T[:, :, 3, 1:2], T[:, :, 3, 2:3], ALU.mult).then_inc(s.prob, 1)
            v.wait_ge(s.prob, 1)
            v.tensor_scalar(T[:, :, 3, 4:5], T[:, :, 3, 3:4], 1e-9, None, ALU.add).then_inc(s.eps_added, 1)
            v.wait_ge(s.eps_added, 1)
            v.reciprocal(T[:, :, 3, 5:6], T[:, :, 3, 4:5]).then_inc(s.eps_inv, 1)
            v.wait_ge(s.eps_inv, 1)
            v.tensor_tensor(T[:, :, 3, 6:7], T[:, :, 3, 3:4], T[:, :, 3, 5:6], ALU.mult).then_inc(s.factor, 1)
            v.wait_ge(s.factor, 1)
            for t in range(NT):
                if t % 4 == 0:
                    v.wait_ge(s.down_ps, t + 4)
                v.scalar_tensor_tensor(out=c.h[:, t], in0=c.ps[:, 4 + t // 4, tok(t % 4)],
                                       scalar=T[:, t, 3, 6:7], in1=c.h[:, t], op0=ALU.mult, op1=ALU.add)\
                    .then_inc(s.y_ready, 1)
                if t % 4 == 3:
                    own = slice(t - 3, t + 1)
                    v.wait_ge(s.y_ready, t + 1)
                    v.tensor_tensor(c.x[:, own], c.x[:, own], c.h[:, own], ALU.add).then_inc(s.added, 1)


def prepare(c, dram_small, dram_big):
    nc = c.nc
    c.turns.half = 1
    s = signals(c, "first_small small constants tables_ps maps_ps maps")
    with nc.Block() as block:
        @block.sync
        def _(sp):
            last = c.where[FIRST[-1]]
            cut = last[0] + last[1]
            sp.dma_start(c.small[:, 0:cut], dram_small[:, 0:cut]).then_inc(s.first_small, 16)
            sp.dma_start(c.small[:, cut:], dram_small[:, cut:]).then_inc(s.small, 16)
            sp.dma_start(c.big["L1_qkv"][:], dram_big["L1_qkv"]).then_inc(c.loaded["L1_qkv"], 16)
            sp.wait_ge(s.small, 16)

        @block.gpsimd
        def _(g):
            g.memset(c.minus_half[:], -0.5).then_inc(s.constants, 1)
            g.memset(c.counts[:], 0.0).then_inc(s.constants, 1)
            g.memset(c.q_apart[:].rearrange("p t m b q -> p (t m b q)"), 0.0).then_inc(s.constants, 1)
            g.memset(c.vx[:].rearrange("p t b j n -> p (t b j n)"), 0.0).then_inc(s.constants, 1)
            g.wait_ge(s.constants, 4)
            for u in range(2):
                g.memset(c.vx[part(u)].rearrange("p t b j n -> p (t b j) n")[:, :, u * 9 + HD], 1.0)\
                    .then_inc(s.constants, 1)

        @block.tensor
        def _(pe):
            pe.wait_ge(s.first_small, 16)
            for k in range(S):
                for b in range(2):
                    last = pe.matmul(c.ps[part(b), k // 16, (k % 16) * 32:(k % 16) * 32 + 17],
                                     c.w("distance_onehot")[:, 63 - k:127 - k], c.w("distance_table"),
                                     start=True, stop=True)
            last.then_inc(s.tables_ps, 1)
            for i, (a, b) in enumerate((("dq", "uq"), ("dkv", "uk"), ("kr", "qr"), ("dkv", "uv"))):
                last = pe.matmul(c.ps[:, 4, i * P:(i + 1) * P], c.w("L2a_" + a), c.w("L2a_" + b),
                                 start=True, stop=True)
            last.then_inc(s.maps_ps, 1)

        @block.vector
        def _(v):
            v.wait_ge(s.tables_ps, 1)
            table = c.ps[:, 0:4].rearrange("p b (k n) -> p b k n", n=32)
            by_head = c.bias0[:].rearrange("p (h k) -> p h k", k=S)
            for q in range(4):
                v.tensor_copy(by_head[:, :, q * 16:(q + 1) * 16].rearrange("p h k -> p k h"),
                              table[:, q, :, 0:HEADS])
                v.tensor_copy(c.decay3[:, q * 16:(q + 1) * 16], table[:, q, :, HEADS])
            v.wait_ge(s.maps_ps, 1)
            for i in range(3):
                v.tensor_tensor(c.q_of_h[:, i * D:(i + 1) * D], c.ps[:, 4, i * P:(i + 1) * P],
                                c.w("head_block"), ALU.mult)
            v.tensor_tensor(c.gate_of_ctx[:], c.w("L2x_g1"), c.w("L2x_g2"), ALU.add)
            v.tensor_tensor(c.v_of_h[:], c.ps[:, 4, 3 * P:4 * P], c.w("head_block_pairs"), ALU.mult)\
                .then_inc(s.maps, 1)


def load_group(c, x_dram, ctx_dram, big_dram, i):
    nc = c.nc
    c.turn_over()
    s = signals(c, "x ctx ctxT_ps ctxT")
    following = unit_norm(c, 1)
    with nc.Block() as block:
        @block.sync
        def _(sp):
            sp.dma_start(c.x[:], x_dram[i]).then_inc(s.x, 16)
            sp.dma_start(c.ctx_tok[:], ctx_dram[i]).then_inc(s.ctx, 16)
            sp.dma_start(c.big["L0f_w1"][:], big_dram["L0f_w1"]).then_inc(c.loaded["L0f_w1"], 16)
            sp.dma_start(c.big["L0f_w2"][:], big_dram["L0f_w2"]).then_inc(c.loaded["L0f_w2"], 16)
            sp.wait_ge(s.x, 16)
            sp.wait_ge(s.ctx, 16)

        @block.tensor
        def _(pe):
            pe.wait_ge(s.ctx, 16)
            for t in range(NT):
                pe.transpose(c.ps[:, t // 4, tok(t % 4)], c.ctx_tok[:, t], c.w("ident")).then_inc(s.ctxT_ps, 1)

        @block.scalar
        def _(act):
            act.wait_ge(s.ctxT_ps, NT)
            for k in range(NT // 4):
                act.copy(c.ctxT[:, k * 512:(k + 1) * 512], c.ps[:, k]).then_inc(s.ctxT, 1)

        @block.gpsimd
        def _(g):
            c.begin(g)
            invert(c, g, following, 0, NT)

        @block.vector
        def _(v):
            v.wait_ge(s.x, 16)
            measure(v, following, c.x, 0, NT)
            scale(v, following, c.x, c.h, 0, NT)


def store_group(c, out_dram, i):
    nc = c.nc
    c.turn_over()
    s = signals(c, "out")
    with nc.Block() as block:
        @block.sync
        def _(sp):
            sp.dma_start(out_dram[i], c.x[:]).then_inc(s.out, 16)
            sp.wait_ge(s.out, 16)

        @block.gpsimd
        def _(g):
            c.begin(g)
            for loaded in c.per_group:
                g.sem_clear(loaded)


def clear_last(c):
    c.turn_over()
    with c.nc.Block() as block:
        @block.gpsimd
        def _(g):
            c.begin(g)


def by_halves(c, sub_layer, *options):
    for k in range(NT // HT):
        sub_layer(SomeTiles(c, k * HT, (k + 1) * HT), *options)


STAGES = {
    "L0a": lambda c: attention(c, "L0a", mode="bias", q_scale=HD ** -0.5, bias=True, out_bias=True),
    "L0x": lambda c: by_halves(c, channel_attention),
    "L0f": lambda c: experts(c, "L0f", 2, False),
    "L1a": rotary_attention,
    "L1x": lambda c: attention(c, "L1x", "ctx", exp_scale=HD ** -0.5),
    "L1f": lambda c: experts(c, "L1f", 1, False),
    "L2a": lambda c: attention(c, "L2a", mode="latent", exp_scale=HD ** -0.5, loads=("L2f_w1", "L2f_w3", "L2f_w2")),
    "L2x": matrix_lstm,
    "L2f": lambda c: experts(c, "L2f", 2, True),
    "L3a": lambda c: attention(c, "L3a", mode="decay", exp_scale=HD ** -0.5, out_bias=True),
    "L3x": lambda c: attention(c, "L3x", "ctx", mode="sparse", q_scale=HD ** -0.5, bias=True, out_bias=True),
    "L3f": lambda c: (attention(c, "L3f", mode="causal", exp_scale=HD ** -0.5, rms=True),
                      gated_mlp(c)),
}


def decoder(nc, x, context, small, big, out, where, stages=tuple(STAGES), groups=NG):
    with ExitStack() as ctx:
        c = Core(nc, ctx, where, {n: a.shape for n, a in big.items()})
        c.dram = big
        c.loaded = {n: ctx.enter_context(nc.semaphore("loaded_" + n)) for n in big}
        c.per_group = [s for n, s in c.loaded.items() if n != "L1_qkv"]
        prepare(c, small, big)
        with nc.Fori(0, groups) as i:
            c.group, c.context = i, context
            load_group(c, x, context, big, i)
            for n in stages:
                STAGES[n](c)
            store_group(c, out, i)
            if c.turns.half == 0:
                clear_last(c)
        clear_last(c)


def kernel(**inputs):
    import concourse.bacc as bacc
    from concourse.bass_utils import run_bass_kernel_spmd

    i = {n: np.asarray(a) for n, a in inputs.items()}
    small, big = lay_out(i)
    packed, where = pack(small)
    grouped = lambda a: np.ascontiguousarray(a.reshape(NG, NT, P, D).transpose(0, 2, 1, 3))
    arrays = {"x_in": grouped(i["x"]), "ctx_in": grouped(i["ctx_1024"]), "small_in": packed}
    arrays.update({n + "_in": np.ascontiguousarray(a) for n, a in big.items()})
    nc = bacc.Bacc("TRN2", target_bir_lowering=False, num_devices=1)
    dram = {n: nc.dram_tensor(n, a.shape, F32, kind="ExternalInput").ap() for n, a in arrays.items()}
    out = nc.dram_tensor("out", (NG, P, NT, D), F32, kind="ExternalOutput").ap()
    decoder(nc, dram["x_in"], dram["ctx_in"], dram["small_in"], {n: dram[n + "_in"] for n in big}, out, where)
    got = run_bass_kernel_spmd(nc, [arrays], core_ids=[0]).results[0]["out"]
    return np.ascontiguousarray(np.asarray(got).transpose(0, 2, 1, 3)).reshape(B, S, D)
```
